# Optimizing a Trainium2 kernel written in Bass

```python
import numpy as np
import jax
import jax.numpy as jnp

def _softmax(x, axis=-1):
    return jax.nn.softmax(x, axis=axis)

def _gelu(x):
    return jax.nn.gelu(x, approximate=True)

def _silu(x):
    return jax.nn.silu(x)

def _sigmoid(x):
    return jax.nn.sigmoid(x)

def _layernorm(x, axis=-1, eps=1e-05):
    m = jnp.mean(x, axis=axis, keepdims=True)
    v = jnp.var(x, axis=axis, keepdims=True)
    return (x - m) / jnp.sqrt(v + eps)

def _scatter_add(tgt, idx, src, axis=0):
    return tgt.at[idx].add(src)

def _segment_sum(src, seg, n):
    return jax.ops.segment_sum(src, seg, n)
kernel_name = 'mk_adaln_d1_jaxref_r8_19fe72'

def setup_inputs(seed: int=0):
    np.random.seed(seed)
    _w = jnp.asarray

    def _L0_attn_setup():
        import jax, jax.numpy as jnp
        import numpy as np
        import math
        HIDDEN = 256
        NUM_HEADS = 16
        NUM_KV_HEADS = 4
        HEAD_DIM = 128
        GROUPS = NUM_HEADS // NUM_KV_HEADS
        BATCH = 1
        SEQ = 512
        THETA = 10000.0

        def _rope(x):
            seq = x.shape[2]
            freqs = 1.0 / THETA ** (jnp.arange(0, HEAD_DIM, 2, dtype=jnp.float32) / HEAD_DIM)
            angles = jnp.arange(seq, dtype=jnp.float32)[:, None] * freqs[None, :]
            cos = jnp.cos(angles)[None, None]
            sin = jnp.sin(angles)[None, None]
            x1 = x[..., 0::2]
            x2 = x[..., 1::2]
            rot = jnp.stack([x1 * cos - x2 * sin, x1 * sin + x2 * cos], axis=-1)
            return rot.reshape(x.shape)
        key = jax.random.key(seed)
        kx, kq, kk, kv, ko = jax.random.split(key, 5)
        scale = 0.02
        x = jax.random.normal(kx, (BATCH, SEQ, HIDDEN), dtype=jnp.float32)
        Wq = jax.random.normal(kq, (NUM_HEADS * HEAD_DIM, HIDDEN), dtype=jnp.float32) * scale
        Wk = jax.random.normal(kk, (NUM_KV_HEADS * HEAD_DIM, HIDDEN), dtype=jnp.float32) * scale
        Wv = jax.random.normal(kv, (NUM_KV_HEADS * HEAD_DIM, HIDDEN), dtype=jnp.float32) * scale
        Wo = jax.random.normal(ko, (HIDDEN, NUM_HEADS * HEAD_DIM), dtype=jnp.float32) * scale
        return {'x': x, 'Wq': Wq, 'Wk': Wk, 'Wv': Wv, 'Wo': Wo}
    _L0_attn_in = _L0_attn_setup()

    def _L0_ffn_setup():
        import jax, jax.numpy as jnp
        import numpy as np
        DIM = 256
        INTER = 176
        N_ROUTED = 15
        TOPK = 2
        SHARED_INTER = 176

        def _swiglu(x, wa, wb, wo):
            return jax.nn.silu(x @ wa.T) * (x @ wb.T) @ wo.T
        key = jax.random.key(seed)
        ks = jax.random.split(key, 8)
        s = 0.02
        return {'x': jax.random.normal(ks[0], (2, 256, DIM), dtype=jnp.float32), 'gate_w': jax.random.normal(ks[1], (N_ROUTED, DIM), dtype=jnp.float32) * s, 'w1': jax.random.normal(ks[2], (N_ROUTED, INTER, DIM), dtype=jnp.float32) * s, 'w3': jax.random.normal(ks[3], (N_ROUTED, INTER, DIM), dtype=jnp.float32) * s, 'w2': jax.random.normal(ks[4], (N_ROUTED, DIM, INTER), dtype=jnp.float32) * s, 'sw1': jax.random.normal(ks[5], (SHARED_INTER, DIM), dtype=jnp.float32) * s, 'sw3': jax.random.normal(ks[6], (SHARED_INTER, DIM), dtype=jnp.float32) * s, 'sw2': jax.random.normal(ks[7], (DIM, SHARED_INTER), dtype=jnp.float32) * s}
    _L0_ffn_in = _L0_ffn_setup()
    _L0_c = _w((lambda *s: np.random.randn(*s).astype(np.float32) * 0.05)(8, 256))
    _L0_wmod = _w((lambda *s: np.random.randn(*s).astype(np.float32) * 0.05)(256, 6 * 256) * 256 ** (-0.5))
    _d = {'L0_attn_x': _L0_attn_in['x'], 'L0_attn_Wq': _L0_attn_in['Wq'], 'L0_attn_Wk': _L0_attn_in['Wk'], 'L0_attn_Wv': _L0_attn_in['Wv'], 'L0_attn_Wo': _L0_attn_in['Wo'], 'L0_ffn_gate_w': _L0_ffn_in['gate_w'], 'L0_ffn_w1': _L0_ffn_in['w1'], 'L0_ffn_w2': _L0_ffn_in['w2'], 'L0_ffn_w3': _L0_ffn_in['w3'], 'L0_ffn_sw1': _L0_ffn_in['sw1'], 'L0_ffn_sw2': _L0_ffn_in['sw2'], 'L0_ffn_sw3': _L0_ffn_in['sw3'], 'L0_c': _L0_c, 'L0_wmod': _L0_wmod}
    _x0 = _d['L0_attn_x']
    _d['L0_attn_x'] = jax.random.normal(jax.random.fold_in(jax.random.key(seed), 1), (8, 512, 256), dtype=_x0.dtype)
    del _x0
    return _d

def reference(L0_attn_x, L0_attn_Wq, L0_attn_Wk, L0_attn_Wv, L0_attn_Wo, L0_ffn_gate_w, L0_ffn_w1, L0_ffn_w2, L0_ffn_w3, L0_ffn_sw1, L0_ffn_sw2, L0_ffn_sw3, L0_c, L0_wmod):

    def _L0_attn_ref(x, Wq, Wk, Wv, Wo):
        import jax, jax.numpy as jnp
        import numpy as np
        import math
        HIDDEN = 256
        NUM_HEADS = 16
        NUM_KV_HEADS = 4
        HEAD_DIM = 128
        GROUPS = NUM_HEADS // NUM_KV_HEADS
        BATCH = 1
        SEQ = 512
        THETA = 10000.0

        def _rope(x):
            seq = x.shape[2]
            freqs = 1.0 / THETA ** (jnp.arange(0, HEAD_DIM, 2, dtype=jnp.float32) / HEAD_DIM)
            angles = jnp.arange(seq, dtype=jnp.float32)[:, None] * freqs[None, :]
            cos = jnp.cos(angles)[None, None]
            sin = jnp.sin(angles)[None, None]
            x1 = x[..., 0::2]
            x2 = x[..., 1::2]
            rot = jnp.stack([x1 * cos - x2 * sin, x1 * sin + x2 * cos], axis=-1)
            return rot.reshape(x.shape)
        B, S, _ = x.shape
        q = (x @ Wq.T).reshape(B, S, NUM_HEADS, HEAD_DIM).transpose(0, 2, 1, 3)
        k = (x @ Wk.T).reshape(B, S, NUM_KV_HEADS, HEAD_DIM).transpose(0, 2, 1, 3)
        v = (x @ Wv.T).reshape(B, S, NUM_KV_HEADS, HEAD_DIM).transpose(0, 2, 1, 3)
        q = _rope(q)
        k = _rope(k)
        k = jnp.repeat(k, GROUPS, axis=1)
        v = jnp.repeat(v, GROUPS, axis=1)
        scale = 1.0 / math.sqrt(HEAD_DIM)
        scores = jnp.einsum('bhqd,bhkd->bhqk', q, k) * scale
        causal = jnp.triu(jnp.ones((S, S), dtype=bool), k=1)
        scores = jnp.where(causal[None, None], jnp.float32(-jnp.inf), scores)
        attn = jax.nn.softmax(scores, axis=-1)
        out = jnp.einsum('bhqk,bhkd->bhqd', attn, v)
        out = out.transpose(0, 2, 1, 3).reshape(B, S, NUM_HEADS * HEAD_DIM)
        return out @ Wo.T

    def _L0_ffn_ref(x, gate_w, w1, w2, w3, sw1, sw2, sw3):
        import jax, jax.numpy as jnp
        import numpy as np
        DIM = 256
        INTER = 176
        N_ROUTED = 15
        TOPK = 2
        SHARED_INTER = 176

        def _swiglu(x, wa, wb, wo):
            return jax.nn.silu(x @ wa.T) * (x @ wb.T) @ wo.T
        shape = x.shape
        xf = x.reshape(-1, shape[-1])
        T = xf.shape[0]
        probs = jax.nn.softmax(xf @ gate_w.T, axis=-1)
        weights, indices = jax.lax.top_k(probs, TOPK)
        combine = jnp.zeros((T, N_ROUTED), xf.dtype).at[jnp.arange(T)[:, None], indices].add(weights)
        y = jnp.zeros_like(xf)
        for i in range(N_ROUTED):
            y = y + _swiglu(xf, w1[i], w3[i], w2[i]) * combine[:, i:i + 1]
        z = _swiglu(xf, sw1, sw3, sw2)
        return (y + z).reshape(shape)
    x = L0_attn_x
    mod = (_silu(L0_c) @ L0_wmod).reshape(L0_c.shape[0], 6, 1, -1)
    sa, ca, ga, sb, cb, gb = (mod[:, 0], mod[:, 1], mod[:, 2], mod[:, 3], mod[:, 4], mod[:, 5])
    ga = (2 * (ga >= 0) - 1) * jnp.maximum(jnp.abs(ga), 0.25)
    gb = (2 * (gb >= 0) - 1) * jnp.maximum(jnp.abs(gb), 0.25)
    h = _layernorm(x, axis=-1) * (1 + ca) + sa
    x = x + ga * _L0_attn_ref(h, L0_attn_Wq, L0_attn_Wk, L0_attn_Wv, L0_attn_Wo)
    h = _layernorm(x, axis=-1) * (1 + cb) + sb
    x = x + gb * _L0_ffn_ref(h, L0_ffn_gate_w, L0_ffn_w1, L0_ffn_w2, L0_ffn_w3, L0_ffn_sw1, L0_ffn_sw2, L0_ffn_sw3)
    return x

_drawn_inputs = setup_inputs


def setup_inputs(seed=0):
    import zlib

    import numpy as np

    out = dict(_drawn_inputs(seed))
    spreads = {}
    factors = {'L0_attn_Wq': 8.0,
     'L0_attn_Wk': 8.0,
     'L0_attn_Wv': 6.756,
     'L0_attn_Wo': 6.702,
     'L0_ffn_gate_w': 8.0,
     'L0_ffn_w1': 8.0,
     'L0_ffn_w2': 8.0,
     'L0_ffn_w3': 8.0,
     'L0_ffn_sw1': 8.0,
     'L0_ffn_sw2': 8.0,
     'L0_ffn_sw3': 8.0,
     'L0_c': 6.236,
     'L0_wmod': 6.2}
    for name, (base, spread) in spreads.items():
        noise = np.random.default_rng([zlib.crc32(name.encode()), seed]).standard_normal(out[name].shape)
        drawn = base * np.exp(spread * noise) if base else spread * noise
        out[name] = jnp.asarray(drawn.astype(out[name].dtype))
    for name, factor in factors.items():
        out[name] = (out[name] * factor).astype(out[name].dtype)
    return out
```

```python
import math
from contextlib import ExitStack

import concourse.bass as bass
from concourse import mybir


def adaln_moe_kernel(nc, x, c_t, wmod, wqkv_t, wo_t, gate_t, w13_t, w2_t, rope, tabc, out):
    fp32, f16, bf16, u32 = mybir.dt.float32, mybir.dt.float16, mybir.dt.bfloat16, mybir.dt.uint32
    ALU, ACT, AX = mybir.AluOpType, mybir.ActivationFunctionType, mybir.AxisListType

    B, S, D = x.shape
    TT = S // 128
    KK = D // 128
    HD = 128
    NKV = 4
    NH = 16
    GRP = NH // NKV
    NQK = NH + NKV
    E = gate_t.shape[1]
    NE = E + 1
    INTER = 176
    HI = INTER // 2
    T = B * S
    REG = T + 128
    SH0 = E * REG
    NSH = T // 128
    NRT = NT_ROUTED
    NT = NSH + NRT
    UNR = 4
    WSCALE = 16.0
    PSCALE = 1024.0
    SCALE = 1.0 / math.sqrt(HD)
    EPS = 1e-5
    NEG = -1e30
    P_AT = [0, 128, 384, 768]
    PT_AT = [0, 512, 1024, 896]
    PW = 1280

    ctx = ExitStack()
    with ctx:
        def sb(name, shape, dt, stack=ctx):
            return stack.enter_context(nc.sbuf_tensor(name, shape, dt))

        def sem(name):
            return ctx.enter_context(nc.semaphore(name))

        xs = sb("xs", [128, B * TT, D], fp32)
        dst = sb("dst", [128, 2, B * TT], fp32)
        wts = sb("wts", [128, 2, B * TT], fp32)
        run = sb("run", [128, E], fp32)
        tc = sb("tc", [128, tabc.shape[0]], fp32)
        ident = sb("ident", [128, 128], fp32)
        carry = sb("carry", [128, 3], fp32)

        p1 = ExitStack()
        wqkv_hi = sb("wqkv_hi", [128, KK, 3072], f16, p1)
        wqkv_lo = sb("wqkv_lo", [128, KK, 3072], f16, p1)
        wo_hi = sb("wo_hi", [128, NH, D], f16, p1)
        wo_lo = sb("wo_lo", [128, NH, D], f16, p1)
        gate_f = sb("gate_f", [128, KK, E], fp32, p1)
        gate_hi = sb("gate_hi", [128, KK, E], f16, p1)
        gate_lo = sb("gate_lo", [128, KK, E], f16, p1)
        qk_hi = sb("qk_hi", [128, NQK, S], f16, p1)
        qk_lo = sb("qk_lo", [128, NQK, S], f16, p1)
        v_hi = sb("v_hi", [128, TT, NKV * HD], f16, p1)
        v_lo = sb("v_lo", [128, TT, NKV * HD], f16, p1)
        hT_hi = sb("hT_hi", [128, KK, S], f16, p1)
        hT_lo = sb("hT_lo", [128, KK, S], f16, p1)
        xn = sb("xn", [128, TT, D], fp32, p1)
        hm_a = sb("hm_a", [128, TT, D], fp32, p1)
        hm_b = sb("hm_b", [128, TT, D], fp32, p1)
        tmpD = sb("tmpD", [128, TT, D], fp32, p1)
        pr = sb("pr", [128, 2, PW], fp32, p1)
        pt_hi = sb("pt_hi", [128, PW], f16, p1)
        pt_lo = sb("pt_lo", [128, PW], f16, p1)
        ropes = sb("ropes", [128, 2, S], fp32, p1)
        qsw = sb("qsw", [128, 2, S], fp32, p1)
        rt1 = sb("rt1", [128, 2, S], fp32, p1)
        rt2 = sb("rt2", [128, 2, S], fp32, p1)
        hc = rt2[:, :, :].rearrange("p a b -> p (a b)").rearrange("p (t d) -> p t d", d=D)
        rows_a = sb("rows_a", [128, 2, D], fp32, p1)
        rows_b = sb("rows_b", [128, 3, D], fp32, p1)
        ones = sb("ones", [128, 128], f16, p1)
        upper = sb("upper", [128, 128], f16, p1)
        maskb = sb("maskb", [128, 128], bf16, p1)
        identb = sb("identb", [128, 128], bf16, p1)
        bst = sb("bst", [128, TT, 6], fp32, p1)
        mv = sb("mv", [128, TT, 2], fp32, p1)
        rstd = sb("rstd", [128, TT], fp32, p1)
        vare = sb("vare", [128, TT], fp32, p1)
        cst = sb("cst", [128, 2, TT], fp32, p1)
        negm = sb("negm", [128, 2, TT], fp32, p1)
        rsum = sb("rsum", [128, 2, TT], fp32, p1)
        rinv = sb("rinv", [128, 2, TT], fp32, p1)
        lg = sb("lg", [128, TT, 16], fp32, p1)
        ex = sb("ex", [128, TT, 16], fp32, p1)
        prob = sb("prob", [128, TT, 24], fp32, p1)
        rep = sb("rep", [128, 2, TT, 24], fp32, p1)
        mx8 = sb("mx8", [128, 2, TT, 8], fp32, p1)
        hot = sb("hot", [128, 3, TT, E], fp32, p1)
        hot16 = sb("hot16", [128, TT, E], f16, p1)
        posa = sb("posa", [128, 3, TT, E], fp32, p1)
        posf = sb("posf", [128, 2, TT], fp32, p1)
        idxs = sb("idxs", [128, 2, TT], u32, p1)
        lsum = sb("lsum", [128, 3, TT], fp32, p1)
        cT = sb("cT", [128, KK, B], fp32, p1)
        cE = sb("cE", [128, KK, B], fp32, p1)
        siluT = sb("siluT", [128, KK, B], fp32, p1)
        wst0 = sb("wst0", [128, 3072], fp32, p1)
        p1.close()

        p2 = ExitStack()
        w13_hi = sb("w13_hi", [128, KK, NE * 2 * INTER], f16, p2)
        w13_lo = sb("w13_lo", [128, KK, NE * 2 * INTER], f16, p2)
        w2_hi = sb("w2_hi", [HI, 2, NE * D], f16, p2)
        w2_lo = sb("w2_lo", [HI, 2, NE * D], f16, p2)
        stage = sb("stage", [128, 2, NE * INTER], fp32, p2)
        zrow = sb("zrow", [128, D], fp32, p2)
        tcmp = sb("tcmp", [128, NRT * E], fp32, p2)
        tcnt = sb("tcnt", [128, 6, E], fp32, p2)
        tseq = sb("tseq", [1, 5, NRT], fp32, p2)
        tab_e = sb("tab_e", [1, NT], u32, p2)
        tab_r = sb("tab_r", [1, NT], u32, p2)
        runu = sb("runu", [1, E], u32, p2)
        xt = sb("xt", [128, UNR, D], fp32, p2)
        xT_hi = sb("xT_hi", [128, 2, KK, 128], f16, p2)
        xT_lo = sb("xT_lo", [128, 2, KK, 128], f16, p2)
        sg = sb("sg", [128, 2, INTER], fp32, p2)
        hh = sb("hh", [128, 2, INTER], fp32, p2)
        aT_hi = sb("aT_hi", [HI, 2, 2, 128], f16, p2)
        aT_lo = sb("aT_lo", [HI, 2, 2, 128], f16, p2)
        ys = sb("ys", [128, UNR, D], fp32, p2)
        tsum = sb("tsum", [128, 2 * B * TT], fp32, p2)
        yrow = sb("yrow", [128, 2, B * TT], u32, p2)
        p2.close()

        p3 = ExitStack()
        yg = sb("yg", [128, 2, 2, TT, D], fp32, p3)
        ysh = sb("ysh", [128, 2, TT, D], fp32, p3)
        ixg = sb("ixg", [128, 2, 2, TT], u32, p3)
        gbr = sb("gbr", [128, 2, D], fp32, p3)
        yo = sb("yo", [128, 2, TT, D], fp32, p3)
        p3.close()

        wst = [wst0[:, :], xs[:, TT:TT + 12, :].rearrange("p a b -> p (a b)")]
        wo_st = qk_hi[:, 0:16, :].rearrange("p a b -> p (a b)").bitcast(fp32)
        wmod_st = qk_lo[:, 0:12, :].rearrange("p a b -> p (a b)").bitcast(fp32)
        mrow = pr[0:B, :, :].rearrange("p a b -> p (a b)")[:, 0:6 * D]
        mneg = v_hi[0:B, :, :].rearrange("p a b -> p (a b)").bitcast(fp32)[:, 0:D]
        mabs = v_lo[0:B, :, :].rearrange("p a b -> p (a b)").bitcast(fp32)[:, 0:D]
        mneg2 = v_hi[0:B, :, :].rearrange("p a b -> p (a b)").bitcast(fp32)[:, D:2 * D]
        mabs2 = v_lo[0:B, :, :].rearrange("p a b -> p (a b)").bitcast(fp32)[:, D:2 * D]

        ps = ctx.enter_context(nc.psum_tensor("ps", [128, 8, 512], fp32))
        mscr = nc.dram_tensor("mod_rows", (B, 6 * D), fp32, kind="Internal").ap()
        hd = nc.dram_tensor("expert_in", (NE * REG, D), fp32, kind="Internal").ap()
        yd = nc.dram_tensor("expert_out", (NT * 128, D), fp32, kind="Internal").ap()

        s_cmod = sem("s_cmod")
        s_x0, s_xr = sem("s_x0"), sem("s_xr")
        s_wq, s_wo, s_small = sem("s_wq"), sem("s_wo"), sem("s_small")
        s_const = sem("s_const")
        s_whi, s_wlo = sem("s_whi"), sem("s_wlo")
        s_cexp, s_silu, s_modmm, s_mod = sem("s_cexp"), sem("s_silu"), sem("s_modmm"), sem("s_mod")
        s_mscr, s_ra, s_rb = sem("s_mscr"), sem("s_ra"), sem("s_rb")
        s_bn, s_mv, s_var, s_rstd, s_xn = sem("s_bn"), sem("s_mv"), sem("s_var"), sem("s_rstd"), sem("s_xn")
        s_hc, s_hm = sem("s_hc"), sem("s_hm")
        s_tr, s_trhi, s_trlo = sem("s_tr"), sem("s_trhi"), sem("s_trlo")
        s_vmm, s_vhi, s_vlo = sem("s_vmm"), sem("s_vhi"), sem("s_vlo")
        s_qmm, s_qsw = sem("s_qmm"), sem("s_qsw")
        s_rt1 = sem("s_rt1")
        s_rt2, s_rot = sem("s_rt2"), sem("s_rot")
        s_qhi, s_qlo = sem("s_qhi"), sem("s_qlo")
        s_sc, s_max, s_rinv, s_norm = sem("s_sc"), sem("s_max"), sem("s_rinv"), sem("s_norm")
        s_exp = sem("s_exp")
        s_pt, s_pthi, s_ptlo = sem("s_pt"), sem("s_pthi"), sem("s_ptlo")
        s_pv, s_ohi = sem("s_pv"), sem("s_ohi")
        s_olo = sem("s_olo")
        s_op, s_opev, s_x2 = sem("s_op"), sem("s_opev"), sem("s_x2")
        s_lgmm, s_route, s_lgex = sem("s_lgmm"), sem("s_route"), sem("s_lgex")
        s_posmm, s_idx, s_run = sem("s_posmm"), sem("s_idx"), sem("s_run")
        s_p1 = sem("s_p1")
        s_scat, s_shst = sem("s_scat"), sem("s_shst")
        s_sent = sem("s_sent")
        s_w2st = [sem("s_w2st0"), sem("s_w2st1")]
        s_w2hi, s_w2lo, s_zero, s_pad = sem("s_w2hi"), sem("s_w2lo"), sem("s_zero"), sem("s_pad")
        s_tab = sem("s_tab")
        s_ld = [sem(f"s_ld{r}") for r in range(UNR)]
        s_t1, s_t1hi, s_t1lo = sem("s_t1"), sem("s_t1hi"), sem("s_t1lo")
        s_up, s_sg, s_hh = sem("s_up"), sem("s_sg"), sem("s_hh")
        s_t2, s_t2hi, s_t2lo = sem("s_t2"), sem("s_t2hi"), sem("s_t2lo")
        s_dn = sem("s_dn")
        s_ev = sem("s_ev")
        s_st = [sem(f"s_st{r}") for r in range(UNR)]
        s_ix = sem("s_ix")
        s_gat = sem("s_gat")
        s_ga = [sem("s_ga0"), sem("s_ga1")]
        s_sh = [sem("s_sh0"), sem("s_sh1")]
        s_c1, s_c2, s_c3, s_yo = sem("s_c1"), sem("s_c2"), sem("s_c3"), sem("s_yo")
        s_out = [sem("s_out0"), sem("s_out1")]

        SLOTS = 2
        QBANKS = 4
        NPIECE = 2 * KK + 2
        ROUTE = 8
        PIECE = NE * INTER
        P2 = [(w13_hi[:, k, h * PIECE:(h + 1) * PIECE], w13_lo[:, k, h * PIECE:(h + 1) * PIECE], 128, PIECE)
              for k in range(KK) for h in range(2)]
        P2 += [(w2_hi[:, m, h * 2048:(h + 1) * 2048], w2_lo[:, m, h * 2048:(h + 1) * 2048], HI, 2048)
               for m in range(2) for h in range(2)]
        NP2 = len(P2)
        STRIPS = [3, 0, 2, 1]
        S_BANK = {3: (0, 0), 0: (1, 0), 2: (1, 128), 1: (2, 0)}
        E_DONE = {3: 1, 0: 3, 1: 4}
        S_READY = {3: 1, 0: 2, 2: 2, 1: 3}
        M_READY = {3: 1, 0: 3, 2: 3, 1: 4}
        PT_BANK = [(3, 0), (4, 0), (5, 0), (4, 384)]
        PT_EVAC = [(3, 0, 512), (4, 512, 512), (5, 1024, 256)]
        C_E0, C_K, C_TRI, C_J, C_SE, C_SR = 0, 16, 48, 48 + E * E, 48 + E * E + NRT, 48 + E * E + NRT + NSH
        xd = x.rearrange("b (t p) d -> p (b t) d", p=128)
        od = out.rearrange("b (t p) d -> p (b t) d", p=128)
        hsh = hd[SH0:SH0 + T, :].rearrange("(t p) d -> p t d", p=128)
        ysd = yd[0:T, :].rearrange("(t p) d -> p t d", p=128)
        block = ctx.enter_context(nc.Block())

        def stages(u, r):
            for what, d in (("t1", 2), ("up", 1), ("t2", 0), ("dn", -1)):
                n = u * UNR + (1 + r + d)
                if not isinstance(u, int) or 0 <= n < NT:
                    yield what, n, (1 + r + d) % UNR, u + (1 + r + d) // UNR

        def run_tiles(eng, tile_step):
            for r in range(1, UNR):
                tile_step(-1, r)
            with eng.Fori(0, NT // UNR - 1) as u:
                for r in range(UNR):
                    tile_step(u, r)
            for r in range(UNR):
                tile_step(NT // UNR - 1, r)

        def pst1(m):
            return ps[:, m % 2, 0:KK * 128].rearrange("p (k t) -> p k t", k=KK)

        def pst2(m):
            return ps[0:HI, 4 + m % 2, 0:2 * 128].rearrange("p (k t) -> p k t", k=2)

        def carrier():
            nc.vector.tensor_copy(carry[:, 0:1], ident[:, 0:1])

        def pool_carrier(k=1):
            return nc.gpsimd.tensor_tensor(carry[:, k:k + 1], ident[:, 0:1], ident[:, 1:2], ALU.add)

        @block.sync
        def _(sp):
            sp.sem_inc(s_shst, 16)
            for r in range(UNR):
                sp.sem_inc(s_st[r], 16)
            for r in range(2):
                sp.sem_inc(s_out[r], 16)
            sp.dma_start(cT[:, :, :], c_t.rearrange("(k p) b -> p k b", p=128)).then_inc(s_cmod, 16)
            sp.dma_start(wmod_st.rearrange("p (k n) -> p k n", k=KK),
                         wmod.rearrange("(k p) n -> p k n", p=128)).then_inc(s_cmod, 16)
            sp.dma_start(xs[:, 0:TT, :], xd[:, 0:TT, :]).then_inc(s_x0, 16)
            for k in range(KK):
                sp.dma_start(wst[k], wqkv_t[k * 128:(k + 1) * 128, :]).then_inc(s_wq, 16)
            sp.dma_start(ropes[:, :, :], rope.rearrange("c p s -> p c s")).then_inc(s_small, 16)
            sp.dma_start(gate_f[:, :, :], gate_t.rearrange("(k p) e -> p k e", p=128)).then_inc(s_small, 16)
            sp.dma_start(tc[:, :], tabc.rearrange("(a n) -> a n", a=1).to_broadcast([128, tabc.shape[0]])).then_inc(s_small, 16)
            sp.dma_start(wo_st.rearrange("p (h d) -> p h d", h=NH),
                         wo_t.rearrange("(h p) d -> p h d", p=128)).then_inc(s_wo, 16)
            sp.wait_ge(s_mod, MODSTEPS)
            sp.dma_start(mscr[:, :], mrow).then_inc(s_mscr, 16)
            sp.wait_ge(s_mscr, 16)

            def mod_rows(dst, b, a, n, done):
                sp.dma_start(dst, mscr[bass.ds(b, 1), a * D:(a + n) * D].to_broadcast([128, n * D])).then_inc(done, 16)

            ra, rb = (t[:, :, :].rearrange("p a b -> p (a b)") for t in (rows_a, rows_b))
            mod_rows(ra, 0, 0, 2, s_ra)
            mod_rows(rb, 0, 2, 3, s_rb)
            sp.wait_ge(s_wlo, NPIECE)
            sp.dma_start(xs[:, TT:, :], xd[:, TT:, :]).then_inc(s_xr, 16)
            sp.wait_ge(s_hm, 1)
            mod_rows(ra, 1, 0, 2, s_ra)
            with sp.Fori(0, B - 2) as b:
                sp.wait_ge(s_hm, b * 2 + 2)
                mod_rows(ra, b + 2, 0, 2, s_ra)
                sp.wait_ge(s_hm, b * 2 + 3)
                mod_rows(rb, b + 1, 2, 3, s_rb)
                sp.dma_start(hsh[:, bass.ds(b * TT, TT), :], hm_b[:, :, :]).then_inc(s_shst, 16)
            sp.wait_ge(s_hm, 2 * B - 1)
            mod_rows(rb, B - 1, 2, 3, s_rb)
            sp.dma_start(hsh[:, (B - 2) * TT:(B - 1) * TT, :], hm_b[:, :, :]).then_inc(s_shst, 16)
            sp.wait_ge(s_hm, 2 * B)
            sp.dma_start(hsh[:, (B - 1) * TT:, :], hm_b[:, :, :]).then_inc(s_shst, 16)

            sp.wait_ge(s_idx, B)
            sp.wait_ge(s_shst, 16 * (B + 1))
            sp.wait_ge(s_sent, B + 1)
            for n, (hi, lo, p, w) in enumerate(P2):
                if n >= 2:
                    sp.wait_ge(s_w2lo, n - 1)
                src = w13_t[n // 2, :, (n % 2) * w:(n % 2 + 1) * w] if n < 2 * KK else \
                    w2_t[(n - 2 * KK) // 2, :, (n % 2) * w:(n % 2 + 1) * w]
                sp.dma_start(stage[0:p, n % 2, 0:w], src).then_inc(s_w2st[n % 2], 16)
            sp.wait_ge(s_zero, 1)
            sp.wait_ge(s_tab, TABSTEPS)
            with sp.Fori(0, E) as e:
                at = sp.value_load(runu[0:1, bass.ds(e, 1)], min_val=0, max_val=SH0 - 128)
                sp.dma_start(hd[bass.ds(at, 128), :], zrow[:, :]).then_inc(s_pad, 16)

            def load(j, r):
                at = sp.value_load(tab_r[0:1, bass.ds(j, 1)], min_val=0, max_val=SH0 + T - 128)
                sp.dma_start(xt[:, r, :], hd[bass.ds(at, 128), :]).then_inc(s_ld[r], 16)

            def store(j, u, r):
                sp.wait_ge(s_ev, j + (1 + SLOTS))
                sp.dma_start(yd[bass.ds(j * 128, 128), :], ys[:, r, :]).then_inc(s_st[r], 16)

            sp.wait_ge(s_pad, 16 * E)
            for r in range(UNR):
                load(r, r)
            with sp.Fori(0, NT // UNR - 1) as u:
                for r in range(UNR):
                    sp.wait_ge(s_t1, u * UNR + (r + 1))
                    load(u * UNR + (r + UNR), r)
                    store(u * UNR + r, u, r)
            for r in range(UNR):
                store(NT - UNR + r, None, r)
            for r in range(UNR):
                sp.wait_ge(s_st[r], 16 * (NT // UNR + 1))

            def fetch(b, r):
                sp.dma_start(ysh[:, r, :, :], ysd[:, bass.ds(b * TT, TT), :]).then_inc(s_sh[r], 16)
                sp.dma_start(gbr[:, r, :], mscr[bass.ds(b, 1), 5 * D:6 * D].to_broadcast([128, D])).then_inc(s_sh[r], 16)

            fetch(0, 0)
            fetch(1, 1)
            with sp.Fori(0, B // 2 - 1) as u:
                for r in range(2):
                    sp.wait_ge(s_yo, u * 2 + (r + 1))
                    sp.dma_start(od[:, bass.ds(u * 2 * TT + r * TT, TT), :], yo[:, r, :, :]).then_inc(s_out[r], 16)
                    fetch(u * 2 + (r + 2), r)
            for r in range(2):
                sp.wait_ge(s_yo, B - 1 + r)
                sp.dma_start(od[:, (B - 2 + r) * TT:(B - 1 + r) * TT, :], yo[:, r, :, :]).then_inc(s_out[r], 16)
            for r in range(2):
                sp.wait_ge(s_out[r], 16 * (B // 2 + 1))

        @block.gpsimd
        def _(pool):
            pool.sem_inc(s_rt2, SLOTS)
            pool.sem_inc(s_sent, 1)
            pool.sem_inc(s_gat, 1)
            nc.gpsimd.memset(ident[:, :], 0.0).then_inc(s_const, 1)
            nc.gpsimd.memset(identb[:, :], 0.0).then_inc(s_const, 1)
            nc.gpsimd.memset(maskb[:, :], 0.0).then_inc(s_const, 1)
            nc.gpsimd.memset(cst[:, 0, :], EPS).then_inc(s_const, 1)
            nc.gpsimd.memset(cst[:, 1, :], -0.5).then_inc(s_const, 1)
            nc.gpsimd.memset(prob[:, :, :], -1.0).then_inc(s_const, 1)
            nc.gpsimd.memset(mx8[:, :, :, :], -1.0).then_inc(s_const, 1)
            nc.gpsimd.memset(ones[:, :], 1.0).then_inc(s_const, 1)
            pool.wait_ge(s_const, 8)
            for m in (ident, identb):
                nc.gpsimd.affine_select(out=m[:, :], in_=m[:, :], compare_op=ALU.not_equal, fill=1.0, base=0,
                                        pattern=[[-1, 128]], channel_multiplier=1).then_inc(s_const, 1)
            nc.gpsimd.affine_select(out=maskb[:, :], in_=maskb[:, :], compare_op=ALU.is_ge, fill=NEG, base=0,
                                    pattern=[[-1, 128]], channel_multiplier=1).then_inc(s_const, 1)
            nc.gpsimd.affine_select(out=upper[:, :], in_=ones[:, :], compare_op=ALU.is_gt, fill=0.0, base=0,
                                    pattern=[[1, 128]], channel_multiplier=-1).then_inc(s_const, 1)

            def ln_rest(n, hm, rows, s_at, c_at, s_rows, b):
                pool.wait_ge(s_mv, n + 1)
                nc.gpsimd.tensor_tensor(vare[:, :], mv[:, :, 1], cst[:, 0, :], ALU.add).then_inc(s_var, 1)
                pool.wait_ge(s_var, n + 1)
                nc.gpsimd.tensor_tensor(rstd[:, :], vare[:, :], cst[:, 1, :], ALU.pow).then_inc(s_rstd, 1)
                pool.wait_ge(s_xn, n + 1)
                pool.wait_ge(s_rows, b * 16 + 16)
                nc.gpsimd.tensor_tensor(hc[:, :, :], xn[:, :, :], rows[:, c_at:c_at + 1, :].to_broadcast([128, TT, D]),
                                        ALU.mult).then_inc(s_hc, 1)
                pool.wait_ge(s_hc, n + 1)
                if hm is hm_b:
                    pool.wait_ge(s_shst, b * 16 + 16)
                nc.gpsimd.tensor_tensor(hm[:, :, :], hc[:, :, :], rows[:, s_at:s_at + 1, :].to_broadcast([128, TT, D]),
                                        ALU.add).then_inc(s_hm, 1)

            def rope_tiles(b):
                with pool.Fori(0, NQK // 2) as u:
                    for r in range(2):
                        n = u * 2 + (b * NQK + r)
                        if r == 0:
                            pool.wait_ge(s_hm, b * 2 + 1)
                        pool.wait_ge(s_qsw, n + 1)
                        pool.wait_ge(s_rot, n + 1)
                        nc.gpsimd.tensor_tensor(rt2[:, r, :], qsw[:, r, :], ropes[:, 1, :],
                                                ALU.mult).then_inc(s_rt2, 1)

            def attention(b):
                with pool.Fori(0, NH // 2) as u:
                    for r in range(2):
                        for q, i in enumerate(STRIPS):
                            w = 128 * (i + 1)
                            p = pr[:, r, P_AT[i]:P_AT[i] + w]
                            if q == 0:
                                pool.wait_ge(s_rinv, u * 2 + (b * NH + r + 1))
                            last = nc.gpsimd.tensor_tensor(p, p, rinv[:, r, i:i + 1].to_broadcast([128, w]), ALU.mult)
                        last.then_inc(s_norm, 1)

            def scatter(b, n):
                pool.wait_ge(s_idx, b + 1)
                pool.wait_ge(s_hm, n + 1)
                pool_carrier()
                for k in range(2):
                    for i in range(TT):
                        nc.gpsimd.indirect_dma_start(
                            out=hd[:, :], out_offset=bass.IndirectOffsetOnAxis(ap=idxs[:, k, i:i + 1], axis=0),
                            in_=hm_b[:, i, :], in_offset=None).then_inc(s_scat, 16)
                pool.wait_ge(s_scat, b * (16 * 2 * TT) + 16 * 2 * TT)
                pool_carrier(2).then_inc(s_sent, 1)

            pool.wait_ge(s_const, 12)
            pool.wait_ge(s_small, 48)
            ln_rest(0, hm_a, rows_a, 0, 1, s_ra, 0)
            rope_tiles(0)
            with pool.Fori(0, B - 1) as b:
                ln_rest(b * 2 + 1, hm_a, rows_a, 0, 1, s_ra, b + 1)
                attention(b)
                ln_rest(b * 2 + 2, hm_b, rows_b, 1, 2, s_rb, b)
                rope_tiles(b + 1)
                scatter(b, b * 2 + 2)
            attention(B - 1)
            ln_rest(2 * B - 1, hm_b, rows_b, 1, 2, s_rb, B - 1)
            scatter(B - 1, 2 * B - 1)

            pool.wait_ge(s_shst, 16 * (B + 1))
            nc.gpsimd.memset(zrow[:, :], 0.0).then_inc(s_zero, 1)

            for r in range(UNR):
                pool.wait_ge(s_st[r], 16 * (NT // UNR + 1))
            with pool.Fori(0, B // 2) as u:
                for r in range(2):
                    pool.wait_ge(s_ix, u * 2 + (r + 1))
                    pool.wait_ge(s_gat, u * 2 + (r + 1))
                    pool_carrier().then_inc(s_gat, 1)
                    for k in range(2):
                        for i in range(TT):
                            nc.gpsimd.indirect_dma_start(
                                out=yg[:, r, k, i, :], out_offset=None, in_=yd[:, :],
                                in_offset=bass.IndirectOffsetOnAxis(ap=ixg[:, r, k, i:i + 1], axis=0)).then_inc(s_ga[r], 16)

        @block.scalar
        def _(act):
            act.sem_inc(s_exp, TT)
            act.wait_ge(s_cmod, 32)
            nc.scalar.activation(cE[:, :, :], cT[:, :, :], ACT.Exp, scale=-1.0).then_inc(s_cexp, 1)
            act.wait_ge(s_wq, 32)
            for k in range(KK):
                for a, b, f in ((0, 2048, WSCALE * SCALE), (2048, 3072, WSCALE)):
                    nc.scalar.activation(wqkv_hi[:, k, a:b], wst[k][:, a:b], ACT.Copy,
                                         scale=f).then_inc(s_whi, 1)
            act.wait_ge(s_wo, 16)
            nc.scalar.activation(wo_hi[:, :, :].rearrange("p a b -> p (a b)"), wo_st, ACT.Copy,
                                 scale=WSCALE).then_inc(s_whi, 1)
            act.wait_ge(s_small, 48)
            nc.scalar.activation(gate_hi[:, :, :], gate_f[:, :, :], ACT.Copy, scale=WSCALE).then_inc(s_whi, 1)

            def transposed_hi(n, bank):
                for k in range(KK):
                    act.wait_ge(s_tr, n * KK + (k + 1))
                    nc.scalar.copy(hT_hi[:, k, :], ps[:, bank + k, :]).then_inc(s_trhi, 1)

            def swap(b, n, bank, slot):
                act.wait_ge(s_qmm, n + (b * NQK + 1))
                act.wait_ge(s_rt2, n + (b * NQK + 1))
                nc.scalar.copy(qsw[0:64, slot, :], ps[64:128, bank, :])
                nc.scalar.copy(qsw[64:128, slot, :], ps[0:64, bank, :]).then_inc(s_qsw, 1)

            def rot_hi(b, n, slot):
                act.wait_ge(s_rot, n + (b * NQK + 1 + SLOTS))
                nc.scalar.copy(qk_hi[:, n, :], rt1[:, slot, :]).then_inc(s_qhi, 1)

            def qkv(b):
                for m in range(TT):
                    act.wait_ge(s_vmm, b * TT + (m + 1))
                    nc.scalar.activation(v_hi[:, m, :], ps[:, m, :], ACT.Copy,
                                         scale=1.0 / WSCALE).then_inc(s_vhi, 1)
                swap(b, 0, 0, 0)
                swap(b, 1, 1, 1)
                with act.Fori(0, NQK // 4 - 1) as u:
                    for r in range(4):
                        rot_hi(b, u * 4 + r, r % 2)
                        swap(b, u * 4 + (r + 2), (r + 2) % 4, r % 2)
                for n in range(NQK - 4, NQK):
                    rot_hi(b, n, n % 2)
                    if n + 2 < NQK:
                        swap(b, n + 2, (n + 2) % 4, n % 2)

            def exps(H, slot):
                for q, i in enumerate(STRIPS):
                    bank, col = S_BANK[i]
                    w = 128 * (i + 1)
                    act.wait_ge(s_max, H * TT + M_READY[i])
                    nc.scalar.activation(pr[:, slot, P_AT[i]:P_AT[i] + w], ps[:, bank, col:col + w], ACT.Exp,
                                         bias=negm[:, slot, i:i + 1],
                                         accum_out=rsum[:, slot, i:i + 1]).then_inc(s_exp, 1)

            def head(b, h, slot, more):
                H = h + b * NH
                for n, (bank, at, w) in enumerate(PT_EVAC):
                    act.wait_ge(s_pt, H * 3 + (n + 1))
                    nc.scalar.activation(pt_hi[:, at:at + w], ps[:, bank, 0:w], ACT.Copy, scale=PSCALE).then_inc(s_pthi, 1)
                if more:
                    exps(H + 2, slot)
                act.wait_ge(s_pv, H + 1)
                nc.scalar.activation(qk_hi[:, h, :], ps[:, 6 + slot, :], ACT.Copy,
                                     scale=1.0 / PSCALE).then_inc(s_ohi, 1)

            def attention(b):
                exps(b * NH, 0)
                exps(b * NH + 1, 1)
                with act.Fori(0, NKV - 1) as g:
                    for r in range(GRP):
                        head(b, g * GRP + r, r % 2, True)
                for h in range(NH - GRP, NH):
                    head(b, h, h % 2, h < NH - 2)

            def routing(b):
                act.wait_ge(s_route, b * ROUTE + 2)
                for i in range(TT):
                    nc.scalar.activation(ex[:, i, 0:E], lg[:, i, 0:E], ACT.Exp, bias=lsum[:, 0, i:i + 1],
                                         accum_out=lsum[:, 1, i:i + 1]).then_inc(s_lgex, 1)

            transposed_hi(0, 2)
            qkv(0)
            with act.Fori(0, B - 1) as b:
                attention(b)
                transposed_hi(b * 2 + 1, 2)
                qkv(b + 1)
                transposed_hi(b * 2 + 2, 4)
                routing(b)
            attention(B - 1)
            transposed_hi(2 * B - 1, 4)
            routing(B - 1)

            for n, (hi, lo, p, w) in enumerate(P2):
                act.wait_ge(s_w2st[n % 2], 16 * (n // 2 + 1))
                nc.scalar.activation(hi, stage[0:p, n % 2, 0:w], ACT.Copy, scale=WSCALE).then_inc(s_w2hi, 1)

            def tile_step(u, r):
                for what, n, m, q in stages(u, r):
                    if what == "t1":
                        act.wait_ge(s_t1, n + 1)
                        nc.scalar.copy(xT_hi[:, m % 2, :, :], pst1(m)).then_inc(s_t1hi, 1)
                    if what == "up":
                        act.wait_ge(s_up, n + 1)
                        nc.scalar.activation(sg[:, m % 2, :], ps[:, 2 + m % 2, 0:INTER], ACT.Silu,
                                             scale=1.0 / WSCALE).then_inc(s_sg, 1)
                    if what == "t2":
                        act.wait_ge(s_t2, n + 1)
                        nc.scalar.copy(aT_hi[:, m % 2, :, :], pst2(m)).then_inc(s_t2hi, 1)

            run_tiles(act, tile_step)

        @block.vector
        def _(dve):
            dve.sem_inc(s_rot, SLOTS)
            dve.sem_inc(s_olo, SLOTS)
            dve.sem_inc(s_ev, SLOTS)
            dve.sem_inc(s_rt1, QBANKS)
            dve.wait_ge(s_const, 12)

            dve.wait_ge(s_cexp, 1)
            nc.vector.tensor_scalar(siluT[:, :, :], cE[:, :, :], 1.0, None, ALU.add).then_inc(s_silu, 1)
            dve.wait_ge(s_silu, 1)
            nc.vector.reciprocal(cE[:, :, :], siluT[:, :, :]).then_inc(s_silu, 1)
            dve.wait_ge(s_silu, 2)
            nc.vector.tensor_tensor(siluT[:, :, :], cE[:, :, :], cT[:, :, :], ALU.mult).then_inc(s_silu, 1)

            def layernorm(n, t):
                carrier()
                for i in range(TT):
                    last = nc.vector.bn_stats(bst[:, i, :], xs[:, t + i, :])
                last.then_inc(s_bn, 1)
                dve.wait_ge(s_bn, n + 1)
                carrier()
                for i in range(TT):
                    last = nc.vector.bn_aggr(mv[:, i, :], bst[:, i, :])
                last.then_inc(s_mv, 1)
                dve.wait_ge(s_mv, n + 1)
                dve.wait_ge(s_rstd, n + 1)
                for i in range(TT):
                    last = nc.vector.tensor_scalar(xn[:, i, :], xs[:, t + i, :], mv[:, i, 0:1], rstd[:, i:i + 1],
                                                   ALU.subtract, ALU.mult)
                last.then_inc(s_xn, 1)

            dve.wait_ge(s_x0, 16)
            layernorm(0, 0)

            dve.wait_ge(s_modmm, 1)
            nc.vector.tensor_copy(mrow, ps[0:B, 5:8, :].rearrange("p a b -> p (a b)")).then_inc(s_mod, 1)
            dve.wait_ge(s_mod, 1)
            for a in (1, 4):
                m = mrow[:, a * D:(a + 1) * D]
                nc.vector.tensor_scalar(m, m, 1.0, None, ALU.add).then_inc(s_mod, 1)
            for j, (a, neg, ab) in enumerate(((2, mneg, mabs), (5, mneg2, mabs2))):
                m = mrow[:, a * D:(a + 1) * D]
                nc.vector.tensor_scalar(neg, m, -1.0, None, ALU.mult).then_inc(s_mod, 1)
                dve.wait_ge(s_mod, 4 + 6 * j)
                nc.vector.tensor_tensor(ab, m, neg, ALU.max).then_inc(s_mod, 1)
                dve.wait_ge(s_mod, 5 + 6 * j)
                nc.vector.tensor_scalar(neg, m, 0.0, 2.0, ALU.is_ge, ALU.mult).then_inc(s_mod, 1)
                nc.vector.tensor_scalar(ab, ab, 0.25, None, ALU.max).then_inc(s_mod, 1)
                dve.wait_ge(s_mod, 7 + 6 * j)
                nc.vector.tensor_scalar(neg, neg, 1.0, None, ALU.subtract).then_inc(s_mod, 1)
                dve.wait_ge(s_mod, 8 + 6 * j)
                nc.vector.tensor_tensor(m, neg, ab, ALU.mult).then_inc(s_mod, 1)

            n = 0
            for k in range(KK):
                for a, b, f in ((0, 2048, WSCALE * SCALE), (2048, 3072, WSCALE)):
                    n += 1
                    dve.wait_ge(s_whi, n)
                    nc.vector.scalar_tensor_tensor(wqkv_lo[:, k, a:b], wst[k][:, a:b], f,
                                                   wqkv_hi[:, k, a:b], ALU.mult, ALU.subtract).then_inc(s_wlo, 1)
            dve.wait_ge(s_whi, n + 1)
            nc.vector.scalar_tensor_tensor(wo_lo[:, :, :].rearrange("p a b -> p (a b)"), wo_st, WSCALE,
                                           wo_hi[:, :, :].rearrange("p a b -> p (a b)"),
                                           ALU.mult, ALU.subtract).then_inc(s_wlo, 1)
            dve.wait_ge(s_whi, n + 2)
            nc.vector.scalar_tensor_tensor(gate_lo[:, :, :], gate_f[:, :, :], WSCALE, gate_hi[:, :, :],
                                           ALU.mult, ALU.subtract).then_inc(s_wlo, 1)
            dve.wait_ge(s_wlo, NPIECE)
            dve.wait_ge(s_small, 48)
            nc.vector.tensor_copy(run[:, :], tc[:, C_E0:C_E0 + E]).then_inc(s_run, 1)
            dve.wait_ge(s_xr, 16)

            def transposed_lo(n, bank):
                for k in range(KK):
                    dve.wait_ge(s_trhi, n * KK + (k + 1))
                    nc.vector.tensor_tensor(hT_lo[:, k, :], ps[:, bank + k, :], hT_hi[:, k, :],
                                            ALU.subtract).then_inc(s_trlo, 1)

            def rot_cos(b, n, bank, slot):
                dve.wait_ge(s_qsw, n + (b * NQK + 1))
                nc.vector.tensor_tensor(rt1[:, slot, :], ps[:, bank, :], ropes[:, 0, :],
                                        ALU.mult).then_inc(s_rt1, 1)

            def rot_sum(b, n, slot):
                dve.wait_ge(s_rt1, n + (b * NQK + 1 + QBANKS))
                dve.wait_ge(s_rt2, n + (b * NQK + 1 + SLOTS))
                nc.vector.tensor_tensor(rt1[:, slot, :], rt1[:, slot, :], rt2[:, slot, :],
                                        ALU.add).then_inc(s_rot, 1)

            def rot_lo(b, n, slot):
                dve.wait_ge(s_qhi, n + (b * NQK + 1))
                nc.vector.tensor_tensor(qk_lo[:, n, :], rt1[:, slot, :], qk_hi[:, n, :],
                                        ALU.subtract).then_inc(s_qlo, 1)
                dve.wait_ge(s_qlo, n + (b * NQK + 1))

            def qkv(b):
                for m in range(TT):
                    dve.wait_ge(s_vhi, b * TT + (m + 1))
                    nc.vector.scalar_tensor_tensor(v_lo[:, m, :], ps[:, m, :], 1.0 / WSCALE, v_hi[:, m, :],
                                                   ALU.mult, ALU.subtract).then_inc(s_vlo, 1)
                rot_cos(b, 0, 0, 0)
                with dve.Fori(0, NQK // 4 - 1) as u:
                    for r in range(4):
                        rot_sum(b, u * 4 + r, r % 2)
                        rot_cos(b, u * 4 + (r + 1), (r + 1) % 4, (r + 1) % 2)
                        rot_lo(b, u * 4 + r, r % 2)
                for n in range(NQK - 4, NQK):
                    rot_sum(b, n, n % 2)
                    if n + 1 < NQK:
                        rot_cos(b, n + 1, (n + 1) % 4, (n + 1) % 2)
                    rot_lo(b, n, n % 2)

            def maxima(H, slot):
                for q, i in enumerate(STRIPS):
                    bank, col = S_BANK[i]
                    dve.wait_ge(s_sc, H * 3 + S_READY[i])
                    nc.vector.tensor_reduce(negm[:, slot, i:i + 1], ps[:, bank, col:col + 128 * (i + 1)], AX.X,
                                            ALU.max, negate=True).then_inc(s_max, 1)

            def inverse(H, slot):
                dve.wait_ge(s_exp, H * TT + 2 * TT)
                nc.vector.reciprocal(rinv[:, slot, :], rsum[:, slot, :]).then_inc(s_rinv, 1)

            def head(b, h, slot, more):
                H = h + b * NH
                for n, (bank, at, w) in enumerate(PT_EVAC):
                    dve.wait_ge(s_pthi, H * 3 + (n + 1))
                    nc.vector.scalar_tensor_tensor(pt_lo[:, at:at + w], ps[:, bank, 0:w], PSCALE, pt_hi[:, at:at + w],
                                                   ALU.mult, ALU.subtract).then_inc(s_ptlo, 1)
                if more:
                    maxima(H + 2, slot)
                    inverse(H + 2, slot)
                dve.wait_ge(s_ohi, H + 1)
                nc.vector.scalar_tensor_tensor(qk_lo[:, h, :], ps[:, 6 + slot, :], 1.0 / PSCALE, qk_hi[:, h, :],
                                               ALU.mult, ALU.subtract).then_inc(s_olo, 1)

            def attention(b):
                for k in range(2):
                    maxima(b * NH + k, k)
                    inverse(b * NH + k, k)
                with dve.Fori(0, NKV - 1) as g:
                    for r in range(GRP):
                        head(b, g * GRP + r, r % 2, True)
                for h in range(NH - GRP, NH):
                    head(b, h, h % 2, h < NH - 2)

            def residual(b):
                for i in range(TT):
                    dve.wait_ge(s_op, b * TT + (i + 1))
                    if i == 0:
                        dve.wait_ge(s_rb, b * 16 + 16)
                    nc.vector.scalar_tensor_tensor(tmpD[:, i, :], ps[:, 4 + i, 0:D], 1.0 / WSCALE, rows_b[:, 0, :],
                                                   ALU.mult, ALU.mult).then_inc(s_opev, 1)
                for i in range(TT):
                    dve.wait_ge(s_opev, b * TT + (i + 1))
                    nc.vector.tensor_tensor(xs[:, b * TT + i, :], xs[:, b * TT + i, :], tmpD[:, i, :],
                                            ALU.add).then_inc(s_x2, 1)
                dve.wait_ge(s_x2, b * TT + TT)

            def routing(b):
                tiles = bass.ds(b * TT, TT)
                dve.wait_ge(s_lgmm, b + 1)
                nc.vector.tensor_scalar(lg[:, :, 0:E], ps[:, 6, 0:TT * 16].rearrange("p (t e) -> p t e", e=16)[:, :, 0:E],
                                        1.0 / WSCALE, None, ALU.mult).then_inc(s_route, 1)
                dve.wait_ge(s_route, b * ROUTE + 1)
                nc.vector.tensor_reduce(lsum[:, 0, :], lg[:, :, 0:E], AX.X, ALU.max, negate=True).then_inc(s_route, 1)
                dve.wait_ge(s_lgex, b * TT + TT)
                nc.vector.reciprocal(lsum[:, 2, :], lsum[:, 1, :]).then_inc(s_route, 1)
                dve.wait_ge(s_route, b * ROUTE + 3)
                for i in range(TT):
                    last = nc.vector.tensor_scalar(prob[:, i, 0:E], ex[:, i, 0:E], lsum[:, 2, i:i + 1], None, ALU.mult)
                last.then_inc(s_route, 1)
                dve.wait_ge(s_route, b * ROUTE + 4)
                carrier()
                for i in range(TT):
                    last = nc.vector.max(rep[:, 0, i, 0:8], prob[:, i, 0:E])
                last.then_inc(s_route, 1)
                dve.wait_ge(s_route, b * ROUTE + 5)
                nc.vector.tensor_copy(mx8[:, 0, :, 0:1], rep[:, 0, :, 0:1])
                nc.vector.tensor_copy(mx8[:, 1, :, 0:2], rep[:, 0, :, 0:2])
                nc.vector.tensor_copy(wts[:, :, tiles], rep[:, 0, :, 0:2].rearrange("p t k -> p k t")).then_inc(s_route, 1)
                dve.wait_ge(s_route, b * ROUTE + 6)
                carrier()
                for k in range(2):
                    for i in range(TT):
                        last = nc.vector.match_replace(out=rep[:, k, i, 0:22], in_to_replace=mx8[:, k, i, :],
                                                       in_values=prob[:, i, 0:22], imm_value=-2.0)
                last.then_inc(s_route, 1)
                dve.wait_ge(s_route, b * ROUTE + 7)
                nc.vector.tensor_scalar(hot[:, 1:3, :, :].rearrange("p k t e -> p (k t) e"),
                                        rep[:, :, :, 0:E].rearrange("p k t e -> p (k t) e"), -2.0, None, ALU.is_equal)
                nc.vector.tensor_scalar(hot16[:, :, :], rep[:, 1, :, 0:E], -2.0, None, ALU.is_equal).then_inc(s_route, 1)
                dve.wait_ge(s_route, b * ROUTE + 8)
                nc.vector.tensor_tensor(hot[:, 0, :, :], hot[:, 2, :, :], hot[:, 1, :, :], ALU.subtract).then_inc(s_p1, 1)
                dve.wait_ge(s_posmm, b + 1)
                dve.wait_ge(s_run, b + 1)
                nc.vector.tensor_tensor(posa[:, 2, :, :], ps[:, 7, 0:TT * 16].rearrange("p (t e) -> p t e", e=16)[:, :, 0:E],
                                        run[:, :].unsqueeze(1).to_broadcast([128, TT, E]), ALU.add).then_inc(s_p1, 1)
                dve.wait_ge(s_p1, b * 6 + 2)
                nc.vector.tensor_tensor(run[:, :], run[:, :], ps[:, 7, TT * 16:TT * 16 + E], ALU.add).then_inc(s_run, 1)
                nc.vector.tensor_tensor(posa[:, 0, :, :], posa[:, 2, :, :], hot[:, 1, :, :], ALU.mult).then_inc(s_p1, 1)
                nc.vector.tensor_tensor(posa[:, 1, :, :], posa[:, 2, :, :], hot[:, 0, :, :], ALU.mult).then_inc(s_p1, 1)
                dve.wait_ge(s_p1, b * 6 + 4)
                nc.vector.tensor_reduce(posf[:, :, :], posa[:, 0:2, :, :], AX.X, ALU.add).then_inc(s_p1, 1)
                dve.wait_ge(s_p1, b * 6 + 5)
                dve.wait_ge(s_sent, b + 1)
                nc.vector.tensor_copy(idxs[:, :, :], posf[:, :, :]).then_inc(s_idx, 1)
                nc.vector.tensor_copy(dst[:, :, tiles], posf[:, :, :]).then_inc(s_p1, 1)

            transposed_lo(0, 2)
            qkv(0)
            with dve.Fori(0, B - 1) as b:
                layernorm(b * 2 + 1, b * TT + TT)
                attention(b)
                transposed_lo(b * 2 + 1, 2)
                residual(b)
                layernorm(b * 2 + 2, b * TT)
                qkv(b + 1)
                transposed_lo(b * 2 + 2, 4)
                routing(b)
            attention(B - 1)
            residual(B - 1)
            layernorm(2 * B - 1, (B - 1) * TT)
            transposed_lo(2 * B - 1, 4)
            routing(B - 1)
            dve.wait_ge(s_run, B + 1)
            dve.wait_ge(s_shst, 16 * (B + 1))
            dve.wait_ge(s_sent, B + 1)

            step = [0]

            def then(ins):
                step[0] += 1
                ins.then_inc(s_tab, 1)
                dve.wait_ge(s_tab, step[0])

            def row(t, shape, axis=None):
                return t.unsqueeze(axis).to_broadcast(shape)

            c0 = lambda at, n: tc[0:1, at:at + n]
            call = lambda at, n: tc[:, at:at + n]
            cnt, tiles, cum, off, base, jump = (tcnt[:, k, :] for k in range(6))
            seq_e, seq_a, seq_u, seq_d, seq_m = (tseq[:, k, :] for k in range(5))
            then(nc.vector.tensor_copy(runu[:, :], run[0:1, :]))
            then(nc.vector.tensor_tensor(cnt, run[:, :], call(C_E0, E), ALU.subtract))
            m = tcmp[:, 0:E * 32].rearrange("p (e k) -> p e k", k=32)
            then(nc.vector.tensor_tensor(m, row(cnt, [128, E, 32], 2), row(call(C_K, 32), [128, E, 32], 1), ALU.is_gt))
            then(nc.vector.tensor_reduce(tiles, m, AX.X, ALU.add))
            m = tcmp[:, 0:E * E].rearrange("p (e k) -> p e k", k=E)
            then(nc.vector.tensor_tensor(m, row(tiles, [128, E, E], 1), call(C_TRI, E * E).rearrange("p (e k) -> p e k", k=E),
                                         ALU.mult))
            then(nc.vector.tensor_reduce(cum, m, AX.X, ALU.add))
            then(nc.vector.tensor_tensor(off, cum, tiles, ALU.subtract))
            then(nc.vector.scalar_tensor_tensor(base, off, -128.0, call(C_E0, E), ALU.mult, ALU.add))
            then(nc.vector.tensor_scalar(jump, tiles, 128.0, -float(REG), ALU.mult, ALU.add))
            rows = dst[:, :, :].rearrange("p k t -> p (k t)")
            n, big = 2 * B * TT, [128, 2 * B * TT, E - 1]
            m = tcmp[:, 0:n * (E - 1)].rearrange("p (n e) -> p n e", e=E - 1)
            then(nc.vector.tensor_tensor(m, row(rows, big, 2), row(call(C_E0 + 1, E - 1), big, 1), ALU.is_ge))
            then(nc.vector.tensor_tensor(m, m, row(jump[:, 0:E - 1], big, 1), ALU.mult))
            then(nc.vector.tensor_reduce(tsum[:, :], m, AX.X, ALU.add))
            then(nc.vector.scalar_tensor_tensor(yrow[:, :, :].rearrange("p k t -> p (k t)"), tsum[:, :], float(NSH * 128),
                                                rows, ALU.add, ALU.add))
            m = tcmp[0:1, :].rearrange("p (j e) -> p j e", e=E)
            then(nc.vector.tensor_tensor(m, row(cum[0:1, :], [1, NRT, E], 1), row(c0(C_J, NRT), [1, NRT, E], 2), ALU.is_le))
            then(nc.vector.tensor_reduce(seq_e, m, AX.X, ALU.add))
            then(nc.vector.tensor_tensor(m, row(seq_e, [1, NRT, E], 2), row(c0(C_J, E), [1, NRT, E], 1), ALU.is_equal))
            then(nc.vector.tensor_tensor(m, m, row(base[0:1, :], [1, NRT, E], 1), ALU.mult))
            then(nc.vector.tensor_reduce(seq_a, m, AX.X, ALU.add))
            then(nc.vector.tensor_scalar(seq_u, seq_e, float(E), None, ALU.is_lt))
            then(nc.vector.tensor_scalar(seq_d, c0(C_J, NRT), 128.0, -float(SH0), ALU.mult, ALU.add))
            then(nc.vector.tensor_tensor(seq_m, seq_d, seq_u, ALU.mult))
            then(nc.vector.scalar_tensor_tensor(tab_r[:, NSH:], seq_a, float(SH0), seq_m, ALU.add, ALU.add))
            then(nc.vector.tensor_copy(tab_e[:, NSH:], seq_e))
            then(nc.vector.tensor_copy(tab_e[:, 0:NSH], c0(C_SE, NSH)))
            then(nc.vector.tensor_copy(tab_r[:, 0:NSH], c0(C_SR, NSH)))
            assert step[0] == TABSTEPS

            for n, (hi, lo, p, w) in enumerate(P2):
                dve.wait_ge(s_w2hi, n + 1)
                nc.vector.scalar_tensor_tensor(lo, stage[0:p, n % 2, 0:w], WSCALE, hi, ALU.mult,
                                               ALU.subtract).then_inc(s_w2lo, 1)

            def tile_step(u, r):
                for what, n, m, q in stages(u, r):
                    if what == "t1":
                        dve.wait_ge(s_t1hi, n + 1)
                        nc.vector.tensor_tensor(xT_lo[:, m % 2, :, :], pst1(m), xT_hi[:, m % 2, :, :],
                                                ALU.subtract).then_inc(s_t1lo, 1)
                    if what == "up":
                        dve.wait_ge(s_sg, n + 1)
                        nc.vector.scalar_tensor_tensor(hh[:, m % 2, :], ps[:, 2 + m % 2, INTER:2 * INTER], 1.0 / WSCALE,
                                                       sg[:, m % 2, :], ALU.mult, ALU.mult).then_inc(s_hh, 1)
                    if what == "t2":
                        dve.wait_ge(s_t2hi, n + 1)
                        nc.vector.tensor_tensor(aT_lo[:, m % 2, :, :], pst2(m), aT_hi[:, m % 2, :, :],
                                                ALU.subtract).then_inc(s_t2lo, 1)
                    if what == "dn":
                        dve.wait_ge(s_dn, n + 1)
                        dve.wait_ge(s_st[m], q * 16 + 16)
                        nc.vector.tensor_scalar(ys[:, m, :], ps[:, 6 + m % 2, 0:D], 1.0 / WSCALE, None,
                                                ALU.mult).then_inc(s_ev, 1)

            run_tiles(dve, tile_step)

            for r in range(UNR):
                dve.wait_ge(s_st[r], 16 * (NT // UNR + 1))

            def indices(b, r):
                nc.vector.tensor_copy(ixg[:, r, :, :], yrow[:, :, bass.ds(b * TT, TT)]).then_inc(s_ix, 1)

            def combine(b, u, r):
                dve.wait_ge(s_ga[r], u * (16 * 2 * TT) + 16 * 2 * TT)
                dve.wait_ge(s_sh[r], u * 32 + 32)
                for i in range(TT):
                    last = nc.vector.scalar_tensor_tensor(ysh[:, r, i, :], yg[:, r, 0, i, :], wts[:, 0, bass.ds(b * TT + i, 1)],
                                                          ysh[:, r, i, :], ALU.mult, ALU.add)
                last.then_inc(s_c1, 1)
                dve.wait_ge(s_c1, b + 1)
                for i in range(TT):
                    last = nc.vector.scalar_tensor_tensor(ysh[:, r, i, :], yg[:, r, 1, i, :], wts[:, 1, bass.ds(b * TT + i, 1)],
                                                          ysh[:, r, i, :], ALU.mult, ALU.add)
                last.then_inc(s_c2, 1)
                dve.wait_ge(s_c2, b + 1)
                nc.vector.tensor_tensor(ysh[:, r, :, :], ysh[:, r, :, :], gbr[:, r:r + 1, :].to_broadcast([128, TT, D]),
                                        ALU.mult).then_inc(s_c3, 1)
                dve.wait_ge(s_c3, b + 1)
                dve.wait_ge(s_out[r], u * 16 + 16)
                nc.vector.tensor_tensor(yo[:, r, :, :], ysh[:, r, :, :], xs[:, bass.ds(b * TT, TT), :],
                                        ALU.add).then_inc(s_yo, 1)

            indices(0, 0)
            indices(1, 1)
            with dve.Fori(0, B // 2 - 1) as u:
                for r in range(2):
                    combine(u * 2 + r, u, r)
                    indices(u * 2 + (r + 2), r)
            for r in range(2):
                combine(B - 2 + r, B // 2 - 1, r)

        @block.tensor
        def _(pe):
            def split_product(dst, a_hi, a_lo, b_hi, b_lo, first, last):
                nc.tensor.matmul(dst, a_hi, b_hi, start=first, stop=False, skip_group_check=True)
                nc.tensor.matmul(dst, a_hi, b_lo, start=False, stop=False, skip_group_check=True)
                return nc.tensor.matmul(dst, a_lo, b_hi, start=False, stop=last, skip_group_check=True)

            pe.wait_ge(s_silu, 3)
            wm = wmod_st.rearrange("p (k n) -> p k n", k=KK)
            for j in range(3):
                for k in range(KK):
                    last = nc.tensor.matmul(ps[0:B, 5 + j, :], siluT[:, k, :], wm[:, k, j * 512:(j + 1) * 512],
                                            start=(k == 0), stop=(k == KK - 1))
            last.then_inc(s_modmm, 1)
            pe.wait_ge(s_const, 12)

            def transposes(n, bank):
                pe.wait_ge(s_hm, n + 1)
                hm = (hm_a, hm_b)[bank == 4]
                for k in range(KK):
                    for i in range(TT):
                        last = nc.tensor.transpose(ps[:, bank + k, i * 128:(i + 1) * 128],
                                                   hm[:, i, k * 128:(k + 1) * 128], ident[:, :])
                    last.then_inc(s_tr, 1)

            def qkv(b, n):
                pe.wait_ge(s_trlo, n * KK + KK)
                for m in range(TT):
                    for k in range(KK):
                        t = slice(m * 128, (m + 1) * 128)
                        last = split_product(ps[:, m, :], hT_hi[:, k, t], hT_lo[:, k, t], wqkv_hi[:, k, 2560:3072],
                                             wqkv_lo[:, k, 2560:3072], k == 0, k == KK - 1)
                    last.then_inc(s_vmm, 1)
                with pe.Fori(0, NQK // 4) as u:
                    for r in range(4):
                        pe.wait_ge(s_vlo, b * TT + (r + 1))
                        pe.wait_ge(s_rt1, u * 4 + (b * NQK + r + 1))
                        w = bass.ds(u * 512 + r * 128, 128)
                        for k in range(KK):
                            last = split_product(ps[:, r, :], wqkv_hi[:, k, w], wqkv_lo[:, k, w],
                                                 hT_hi[:, k, :], hT_lo[:, k, :], k == 0, k == KK - 1)
                        last.then_inc(s_qmm, 1)

            def scores(b, h, g):
                for i in STRIPS:
                    bank, col = S_BANK[i]
                    w = 128 * (i + 1)
                    dst = ps[:, bank, col:col + w]
                    q = slice(i * 128, (i + 1) * 128)
                    if i != 2:
                        pe.wait_ge(s_exp, h * TT + (b * (NH * TT) + E_DONE[i]))
                    split_product(dst, qk_hi[:, h, q], qk_lo[:, h, q], qk_hi[:, g + NH, 0:w], qk_lo[:, g + NH, 0:w],
                                  True, False)
                    last = nc.tensor.matmul(ps[:, bank, col + i * 128:col + w], identb[:, :], maskb[:, :],
                                            start=False, stop=True, skip_group_check=True)
                    if i != 0:
                        last.then_inc(s_sc, 1)

            def head(b, h, g, slot, nxt):
                H = h + b * NH
                pe.wait_ge(s_norm, H + 1)
                for j in (0, 1, 3, 2):
                    bank, col = PT_BANK[j]
                    for i in range(j, TT):
                        at = P_AT[i] + 128 * j
                        last = nc.tensor.transpose(ps[:, bank, col + (i - j) * 128:col + (i - j + 1) * 128],
                                                   pr[:, slot, at:at + 128], ident[:, :])
                    if j != 1:
                        last.then_inc(s_pt, 1)
                if nxt is not None:
                    scores(b, *nxt)
                pe.wait_ge(s_olo, H + 1)
                for j in range(TT):
                    pe.wait_ge(s_ptlo, H * 3 + (1, 2, 3, 3)[j])
                    at, w = PT_AT[j], 512 - 128 * j
                    vs = bass.ds(g * HD, HD)
                    dst = ps[:, 6 + slot, 128 * j:512]
                    last = split_product(dst, v_hi[:, j, vs], v_lo[:, j, vs], pt_hi[:, at:at + w], pt_lo[:, at:at + w],
                                         j == 0, j == TT - 1)
                last.then_inc(s_pv, 1)

            def attention(b):
                pe.wait_ge(s_qlo, b * NQK + NQK)
                scores(b, 0, 0)
                scores(b, 1, 0)
                with pe.Fori(0, NKV - 1) as g:
                    for r in range(GRP):
                        head(b, g * GRP + r, g, r % 2, (g * GRP + (r + 2), g if r < GRP - 2 else g + 1))
                for h in range(NH - GRP, NH):
                    head(b, h, NKV - 1, h % 2, (h + 2, NKV - 1) if h < NH - 2 else None)

            def out_projection(b):
                with pe.Fori(0, TT) as i:
                    pe.wait_ge(s_olo, b * NH + (NH + SLOTS))
                    t = bass.ds(i * 128, 128)
                    for h in range(NH):
                        last = split_product(ps[:, i + 4, 0:D], qk_hi[:, h, t], qk_lo[:, h, t], wo_hi[:, h, :],
                                             wo_lo[:, h, :], h == 0, h == NH - 1)
                    last.then_inc(s_op, 1)

            def route(b, n):
                pe.wait_ge(s_trlo, n * KK + KK)
                for i in range(TT):
                    t = slice(i * 128, (i + 1) * 128)
                    for k in range(KK):
                        last = split_product(ps[:, 6, i * 16:i * 16 + E], hT_hi[:, k, t], hT_lo[:, k, t],
                                             gate_hi[:, k, :], gate_lo[:, k, :], k == 0, k == KK - 1)
                last.then_inc(s_lgmm, 1)
                pe.wait_ge(s_route, b * ROUTE + ROUTE)
                for i in range(TT):
                    for j in range(i + 1):
                        nc.tensor.matmul(ps[:, 7, i * 16:i * 16 + E], (upper if j == i else ones)[:, :], hot16[:, j, :],
                                         start=(j == 0), stop=(j == i), skip_group_check=True)
                for j in range(TT):
                    last = nc.tensor.matmul(ps[:, 7, TT * 16:TT * 16 + E], ones[:, :], hot16[:, j, :],
                                            start=(j == 0), stop=(j == TT - 1), skip_group_check=True)
                last.then_inc(s_posmm, 1)

            transposes(0, 2)
            pe.wait_ge(s_wlo, NPIECE)
            qkv(0, 0)
            with pe.Fori(0, B - 1) as b:
                attention(b)
                transposes(b * 2 + 1, 2)
                out_projection(b)
                qkv(b + 1, b * 2 + 1)
                transposes(b * 2 + 2, 4)
                route(b, b * 2 + 2)
            attention(B - 1)
            out_projection(B - 1)
            transposes(2 * B - 1, 4)
            route(B - 1, 2 * B - 1)

            pe.wait_ge(s_w2lo, NP2)
            pe.wait_ge(s_tab, TABSTEPS)

            def tile_step(u, r):
                for what, n, m, q in stages(u, r):
                    if what == "t1":
                        pe.wait_ge(s_ld[m], q * 16 + 16)
                        for k in range(KK):
                            last = nc.tensor.transpose(ps[:, m % 2, k * 128:(k + 1) * 128],
                                                       xt[:, m, k * 128:(k + 1) * 128], ident[:, :])
                        last.then_inc(s_t1, 1)
                    if what == "up":
                        e = pe.value_load(tab_e[0:1, bass.ds(n, 1)], min_val=0, max_val=NE - 1)
                        pe.wait_ge(s_t1lo, n + 1)
                        w = bass.ds(e * (2 * INTER), 2 * INTER)
                        for k in range(KK):
                            last = split_product(ps[:, 2 + m % 2, 0:2 * INTER], xT_hi[:, m % 2, k, :], xT_lo[:, m % 2, k, :],
                                                 w13_hi[:, k, w], w13_lo[:, k, w], k == 0, k == KK - 1)
                        last.then_inc(s_up, 1)
                    if what == "t2":
                        pe.wait_ge(s_hh, n + 1)
                        for k in range(2):
                            last = nc.tensor.transpose(ps[0:HI, 4 + m % 2, k * 128:(k + 1) * 128],
                                                       hh[:, m % 2, k * HI:(k + 1) * HI], ident[:, :])
                        last.then_inc(s_t2, 1)
                    if what == "dn":
                        e = pe.value_load(tab_e[0:1, bass.ds(n, 1)], min_val=0, max_val=NE - 1)
                        pe.wait_ge(s_t2lo, n + 1)
                        pe.wait_ge(s_ev, n + 1)
                        w = bass.ds(e * D, D)
                        for k in range(2):
                            last = split_product(ps[:, 6 + m % 2, 0:D], aT_hi[:, m % 2, k, :], aT_lo[:, m % 2, k, :],
                                                 w2_hi[:, k, w], w2_lo[:, k, w], k == 0, k == 1)
                        last.then_inc(s_dn, 1)

            run_tiles(pe, tile_step)


NT_ROUTED = 80
MODSTEPS = 15
TABSTEPS = 25


def _perm(w, heads):
    a = w.reshape(heads, 64, 2, w.shape[1])
    return a.transpose(0, 2, 1, 3).reshape(w.shape)


def kernel(**inputs):
    import numpy as np
    import concourse.bacc as bacc
    from concourse.bass_utils import run_bass_kernel_spmd as run

    g = {k: np.asarray(v) for k, v in inputs.items()}
    B, S, D = g["L0_attn_x"].shape
    E, INTER, _ = g["L0_ffn_w1"].shape
    NE, HI = E + 1, INTER // 2
    wqkv = np.concatenate([_perm(g["L0_attn_Wq"], 16), _perm(g["L0_attn_Wk"], 4), g["L0_attn_Wv"]], axis=0)
    w1 = np.concatenate([g["L0_ffn_w1"], g["L0_ffn_sw1"][None]], axis=0)
    w3 = np.concatenate([g["L0_ffn_w3"], g["L0_ffn_sw3"][None]], axis=0)
    w2 = np.concatenate([g["L0_ffn_w2"], g["L0_ffn_sw2"][None]], axis=0)
    w13_t = np.stack([w1, w3], axis=1).reshape(NE * 2 * INTER, D).T.reshape(D // 128, 128, NE * 2 * INTER)
    w2_t = w2.transpose(2, 0, 1).reshape(2, HI, NE * D)
    HD, WSCALE = 128, np.float32(16.0)
    freqs = np.float32(1.0) / np.float32(10000.0) ** (np.arange(0, HD, 2, dtype=np.float32) / np.float32(HD))
    angles = (np.arange(S, dtype=np.float32)[None, :] * freqs[:, None]).astype(np.float64)
    cos, sin = (np.cos(angles) / WSCALE).astype(np.float32), (np.sin(angles) / WSCALE).astype(np.float32)
    rope = np.stack([np.concatenate([cos, cos]), np.concatenate([-sin, sin])])
    region, nsh = B * S + 128, B * S // 128
    ar = np.arange
    tabc = np.concatenate([
        ar(NE) * region, ar(32) * 128, (ar(E)[:, None] >= ar(E)[None, :]).reshape(-1), ar(NT_ROUTED),
        np.full(nsh, E), E * region + 128 * ar(nsh)]).astype(np.float32)
    arrays = {
        "x": g["L0_attn_x"], "c_t": g["L0_c"].T, "wmod": g["L0_wmod"], "wqkv_t": wqkv.T,
        "wo_t": g["L0_attn_Wo"].T, "gate_t": g["L0_ffn_gate_w"].T, "w13_t": w13_t, "w2_t": w2_t,
        "rope": rope, "tabc": tabc,
    }
    arrays = {k: np.ascontiguousarray(v) for k, v in arrays.items()}
    nc = bacc.Bacc("TRN2", target_bir_lowering=False, num_devices=1)
    args = [nc.dram_tensor(k, v.shape, mybir.dt.from_np(v.dtype), kind="ExternalInput").ap() for k, v in arrays.items()]
    out = nc.dram_tensor("out", (B, S, D), mybir.dt.float32, kind="ExternalOutput").ap()
    adaln_moe_kernel(nc, *args, out)
    r = run(nc, [arrays], core_ids=[0])
    return r.results[0]["out"]
```

```python
import math
from contextlib import ExitStack

import concourse.bass as bass
from concourse import mybir


def adaln_moe_kernel(nc, x, c_t, wmod, wqkv_t, wo_t, gate_t, w13_t, w2_t, rope, tabc, out):
    fp32, f16, bf16, u32 = mybir.dt.float32, mybir.dt.float16, mybir.dt.bfloat16, mybir.dt.uint32
    ALU, ACT, AX = mybir.AluOpType, mybir.ActivationFunctionType, mybir.AxisListType

    B, S, D = x.shape
    TT = S // 128
    KK = D // 128
    HD = 128
    NKV = 4
    NH = 16
    GRP = NH // NKV
    NQK = NKV + NH
    NPROJ = (NQK + NKV) * HD
    VAT = NQK * HD
    E = gate_t.shape[1]
    NE = E + 1
    INTER = 176
    HI = INTER // 2
    T = B * S
    REG = T + 128
    SH0 = E * REG
    NSH = T // 128
    NRT = NT_ROUTED
    NT = NSH + NRT
    UNR = 8
    WSCALE = 16.0
    PSCALE = 1024.0
    SCALE = 1.0 / math.sqrt(HD)
    EPS = 1e-5
    NEG = -1e30
    P_AT = [0, 128, 384, 768]
    PT_AT = [0, 512, 1024, 896]
    PW = 1280

    ctx = ExitStack()
    with ctx:
        def sb(name, shape, dt, stack=ctx):
            return stack.enter_context(nc.sbuf_tensor(name, shape, dt))

        def sem(name):
            return ctx.enter_context(nc.semaphore(name))

        xs = sb("xs", [128, B * TT, D], fp32)
        dst = sb("dst", [128, 2, B * TT], fp32)
        wts = sb("wts", [128, 2, B * TT], fp32)
        run = sb("run", [128, E], fp32)
        tc = sb("tc", [128, tabc.shape[0]], fp32)
        ident = sb("ident", [128, 128], fp32)
        carry = sb("carry", [128, 3], fp32)

        p1 = ExitStack()
        wqkv_hi = sb("wqkv_hi", [128, KK, NPROJ], f16, p1)
        wqkv_lo = sb("wqkv_lo", [128, KK, NPROJ], f16, p1)
        wo_hi = sb("wo_hi", [128, NH, D], f16, p1)
        wo_lo = sb("wo_lo", [128, NH, D], f16, p1)
        gate_f = sb("gate_f", [128, KK, E], fp32, p1)
        gate_hi = sb("gate_hi", [128, KK, E], f16, p1)
        gate_lo = sb("gate_lo", [128, KK, E], f16, p1)
        qk_hi = sb("qk_hi", [128, NQK, S], f16, p1)
        qk_lo = sb("qk_lo", [128, NQK, S], f16, p1)
        v_hi = sb("v_hi", [128, TT, NKV * HD], f16, p1)
        v_lo = sb("v_lo", [128, TT, NKV * HD], f16, p1)
        hT_hi = sb("hT_hi", [128, KK, S], f16, p1)
        hT_lo = sb("hT_lo", [128, KK, S], f16, p1)
        xn = sb("xn", [128, TT, D], fp32, p1)
        hm_a = sb("hm_a", [128, TT, D], fp32, p1)
        hm_b = sb("hm_b", [128, TT, D], fp32, p1)
        pr = sb("pr", [128, GRP, PW], fp32, p1)
        pt_hi = sb("pt_hi", [128, 2, PW], f16, p1)
        pt_lo = sb("pt_lo", [128, 2, PW], f16, p1)
        ropes = sb("ropes", [128, 2, S], fp32, p1)
        qsw = sb("qsw", [128, 2, S], fp32, p1)
        rt1 = sb("rt1", [128, 2, S], fp32, p1)
        rt2 = sb("rt2", [128, 2, S], fp32, p1)
        hc = rt2[:, :, :].rearrange("p a b -> p (a b)").rearrange("p (t d) -> p t d", d=D)
        rows_a = sb("rows_a", [128, 2, D], fp32, p1)
        rows_b = sb("rows_b", [128, 3, D], fp32, p1)
        ones = sb("ones", [128, 128], f16, p1)
        upper = sb("upper", [128, 128], f16, p1)
        maskb = sb("maskb", [128, 128], bf16, p1)
        identb = sb("identb", [128, 128], bf16, p1)
        bst = sb("bst", [128, TT, 6], fp32, p1)
        mv = sb("mv", [128, TT, 2], fp32, p1)
        rstd = sb("rstd", [128, TT], fp32, p1)
        vare = sb("vare", [128, TT], fp32, p1)
        cst = sb("cst", [128, 2, TT], fp32, p1)
        negm = sb("negm", [128, GRP, TT], fp32, p1)
        rsum = sb("rsum", [128, GRP, TT], fp32, p1)
        rinv = sb("rinv", [128, GRP, TT], fp32, p1)
        lg = sb("lg", [128, TT, 16], fp32, p1)
        ex = sb("ex", [128, TT, 16], fp32, p1)
        prob = sb("prob", [128, TT, 24], fp32, p1)
        rep = sb("rep", [128, 2, TT, 24], fp32, p1)
        mx8 = sb("mx8", [128, 2, TT, 8], fp32, p1)
        hot = sb("hot", [128, 3, TT, E], fp32, p1)
        hot16 = sb("hot16", [128, TT, E], f16, p1)
        posa = sb("posa", [128, 3, TT, E], fp32, p1)
        posf = sb("posf", [128, 2, TT], fp32, p1)
        idxs = sb("idxs", [128, 2, TT], u32, p1)
        lsum = sb("lsum", [128, 3, TT], fp32, p1)
        cT = sb("cT", [128, KK, B], fp32, p1)
        cE = sb("cE", [128, KK, B], fp32, p1)
        siluT = sb("siluT", [128, KK, B], fp32, p1)
        p1.close()

        p2 = ExitStack()
        w13_hi = sb("w13_hi", [128, KK, NE * 2 * INTER], f16, p2)
        w13_lo = sb("w13_lo", [128, KK, NE * 2 * INTER], f16, p2)
        w2_hi = sb("w2_hi", [HI, 2, NE * D], f16, p2)
        w2_lo = sb("w2_lo", [HI, 2, NE * D], f16, p2)
        stage = sb("stage", [128, 2, NE * INTER], fp32, p2)
        zrow = sb("zrow", [128, D], fp32, p2)
        tcmp = sb("tcmp", [128, NRT * E], fp32, p2)
        tcnt = sb("tcnt", [128, 6, E], fp32, p2)
        tseq = sb("tseq", [1, 5, NRT], fp32, p2)
        tab_e = sb("tab_e", [1, NT], u32, p2)
        tab_r = sb("tab_r", [1, NT], u32, p2)
        runu = sb("runu", [1, E], u32, p2)
        xt = sb("xt", [128, UNR, D], fp32, p2)
        xT_hi = sb("xT_hi", [128, 2, KK, 128], f16, p2)
        xT_lo = sb("xT_lo", [128, 2, KK, 128], f16, p2)
        sg = sb("sg", [128, 2, INTER], fp32, p2)
        hh = sb("hh", [128, 2, INTER], fp32, p2)
        aT_hi = sb("aT_hi", [HI, 2, 2, 128], f16, p2)
        aT_lo = sb("aT_lo", [HI, 2, 2, 128], f16, p2)
        ys = sb("ys", [128, UNR, D], fp32, p2)
        tsum = sb("tsum", [128, 2 * B * TT], fp32, p2)
        yrow = sb("yrow", [128, 2, B * TT], u32, p2)
        p2.close()

        p3 = ExitStack()
        yg = sb("yg", [128, 2, 2, TT, D], fp32, p3)
        ysh = sb("ysh", [128, 2, TT, D], fp32, p3)
        ixg = sb("ixg", [128, 2, 2, TT], u32, p3)
        gbr = sb("gbr", [128, 2, D], fp32, p3)
        yo = sb("yo", [128, 2, TT, D], fp32, p3)
        p3.close()

        wst = [pr[:, :, :].rearrange("p a b -> p (a b)")[:, 6 * D:6 * D + NPROJ], xs[:, TT:TT + NPROJ // D, :].rearrange("p a b -> p (a b)")]
        wo_st = qk_hi[:, 0:16, :].rearrange("p a b -> p (a b)").bitcast(fp32)
        wmod_st = qk_lo[:, 0:12, :].rearrange("p a b -> p (a b)").bitcast(fp32)
        mrow = pr[0:B, :, :].rearrange("p a b -> p (a b)")[:, 0:6 * D]
        mneg = v_hi[0:B, :, :].rearrange("p a b -> p (a b)").bitcast(fp32)[:, 0:D]
        mabs = v_lo[0:B, :, :].rearrange("p a b -> p (a b)").bitcast(fp32)[:, 0:D]
        mneg2 = v_hi[0:B, :, :].rearrange("p a b -> p (a b)").bitcast(fp32)[:, D:2 * D]
        mabs2 = v_lo[0:B, :, :].rearrange("p a b -> p (a b)").bitcast(fp32)[:, D:2 * D]

        ps = ctx.enter_context(nc.psum_tensor("ps", [128, 8, 512], fp32))
        mscr = nc.dram_tensor("mod_rows", (B, 6 * D), fp32, kind="Internal").ap()
        hd = nc.dram_tensor("expert_in", (NE * REG, D), fp32, kind="Internal").ap()
        yd = nc.dram_tensor("expert_out", (NT * 128, D), fp32, kind="Internal").ap()

        s_cmod = sem("s_cmod")
        s_x0, s_xr = sem("s_x0"), sem("s_xr")
        s_wq, s_wo, s_small = sem("s_wq"), sem("s_wo"), sem("s_small")
        s_const = sem("s_const")
        s_whi, s_wlo = sem("s_whi"), sem("s_wlo")
        s_cexp, s_silu, s_modmm, s_mod = sem("s_cexp"), sem("s_silu"), sem("s_modmm"), sem("s_mod")
        s_mscr, s_ra, s_rb = sem("s_mscr"), sem("s_ra"), sem("s_rb")
        s_bn, s_mv, s_var, s_rstd, s_xn = sem("s_bn"), sem("s_mv"), sem("s_var"), sem("s_rstd"), sem("s_xn")
        s_hc, s_hm = sem("s_hc"), sem("s_hm")
        s_tr, s_trhi, s_trlo = sem("s_tr"), sem("s_trhi"), sem("s_trlo")
        s_vmm, s_vhi, s_vlo = sem("s_vmm"), sem("s_vhi"), sem("s_vlo")
        s_qmm, s_qsw = sem("s_qmm"), sem("s_qsw")
        s_rt1 = sem("s_rt1")
        s_rt2, s_rot = sem("s_rt2"), sem("s_rot")
        s_qhi, s_qlo = sem("s_qhi"), sem("s_qlo")
        s_sc, s_max, s_rinv, s_norm = sem("s_sc"), sem("s_max"), sem("s_rinv"), sem("s_norm")
        s_exp = sem("s_exp")
        s_pt, s_pthi = sem("s_pt"), sem("s_pthi")
        s_ptlo = sem("s_ptlo")
        s_pv, s_ohi = sem("s_pv"), sem("s_ohi")
        s_olo = sem("s_olo")
        s_op, s_opev, s_x2 = sem("s_op"), sem("s_opev"), sem("s_x2")
        s_lgmm, s_route, s_lgex = sem("s_lgmm"), sem("s_route"), sem("s_lgex")
        s_posmm, s_idx, s_run = sem("s_posmm"), sem("s_idx"), sem("s_run")
        s_p1 = sem("s_p1")
        s_scat, s_shst = sem("s_scat"), sem("s_shst")
        s_sent = sem("s_sent")
        s_w2st = [sem("s_w2st0"), sem("s_w2st1")]
        s_w2hi, s_w2lo, s_zero, s_pad = sem("s_w2hi"), sem("s_w2lo"), sem("s_zero"), sem("s_pad")
        s_tab = sem("s_tab")
        s_ld = [sem(f"s_ld{r}") for r in range(UNR)]
        s_t1, s_t1hi, s_t1lo = sem("s_t1"), sem("s_t1hi"), sem("s_t1lo")
        s_up, s_sg, s_hh = sem("s_up"), sem("s_sg"), sem("s_hh")
        s_t2, s_t2hi, s_t2lo = sem("s_t2"), sem("s_t2hi"), sem("s_t2lo")
        s_dn = sem("s_dn")
        s_ev = sem("s_ev")
        s_st = [sem(f"s_st{r}") for r in range(UNR)]
        s_ix = sem("s_ix")
        s_gat = sem("s_gat")
        s_ga = [sem("s_ga0"), sem("s_ga1")]
        s_sh = [sem("s_sh0"), sem("s_sh1")]
        s_c1, s_c2, s_c3, s_yo = sem("s_c1"), sem("s_c2"), sem("s_c3"), sem("s_yo")
        s_out = [sem("s_out0"), sem("s_out1")]

        SLOTS = 2
        QBANKS = 4
        PTB = 3
        HEAD0 = 6
        SPANS = ((0, NKV * HD, WSCALE), (NKV * HD, VAT, WSCALE * SCALE), (VAT, NPROJ, WSCALE))
        NPIECE = 3 * KK + 2
        ROUTE = 8
        PIECE = NE * INTER
        P2 = [(w13_hi[:, k, h * PIECE:(h + 1) * PIECE], w13_lo[:, k, h * PIECE:(h + 1) * PIECE], 128, PIECE)
              for k in range(KK) for h in range(2)]
        P2 += [(w2_hi[:, m, h * 2048:(h + 1) * 2048], w2_lo[:, m, h * 2048:(h + 1) * 2048], HI, 2048)
               for m in range(2) for h in range(2)]
        NP2 = len(P2)
        STRIPS = [3, 0, 2, 1]
        S_BANK = {3: (0, 0), 0: (1, 0), 2: (1, 128), 1: (2, 0)}
        E_DONE = {3: 1, 0: 3, 1: 4}
        R_AT = 384
        S_READY = {3: 1, 0: 2, 2: 2, 1: 3}
        M_READY = {3: 1, 0: 3, 2: 3, 1: 4}
        PT_BANK = [(3, 0), (4, 0), (5, 0), (4, 384)]
        PT_EVAC = [(3, 0, 512), (4, 512, 512), (5, 1024, 256)]
        C_E0, C_K, C_TRI, C_J, C_SE, C_SR = 0, 16, 48, 48 + E * E, 48 + E * E + NRT, 48 + E * E + NRT + NSH
        xd = x.rearrange("b (t p) d -> p (b t) d", p=128)
        od = out.rearrange("b (t p) d -> p (b t) d", p=128)
        hsh = hd[SH0:SH0 + T, :].rearrange("(t p) d -> p t d", p=128)
        ysd = yd[0:T, :].rearrange("(t p) d -> p t d", p=128)
        block = ctx.enter_context(nc.Block())

        def stages(u, r):
            for what, d in (("t1", 2), ("up", 1), ("t2", 0), ("dn", -1)):
                n = u * UNR + (1 + r + d)
                if not isinstance(u, int) or 0 <= n < NT:
                    yield what, n, (1 + r + d) % UNR, u + (1 + r + d) // UNR

        def run_tiles(eng, tile_step):
            for r in range(1, UNR):
                tile_step(-1, r)
            with eng.Fori(0, NT // UNR - 1) as u:
                for r in range(UNR):
                    tile_step(u, r)
            for r in range(UNR):
                tile_step(NT // UNR - 1, r)

        def pst1(m):
            return ps[:, m % 2, 0:KK * 128].rearrange("p (k t) -> p k t", k=KK)

        def pst2(m):
            return ps[0:HI, 4 + m % 2, 0:2 * 128].rearrange("p (k t) -> p k t", k=2)

        def carrier():
            nc.vector.tensor_copy(carry[:, 0:1], ident[:, 0:1])

        def pool_carrier(k=1):
            return nc.gpsimd.tensor_tensor(carry[:, k:k + 1], ident[:, 0:1], ident[:, 1:2], ALU.add)

        @block.sync
        def _(sp):
            sp.sem_inc(s_shst, 16)
            for r in range(UNR):
                sp.sem_inc(s_st[r], 16)
            for r in range(2):
                sp.sem_inc(s_out[r], 16)
            sp.dma_start(cT[:, :, :], c_t.rearrange("(k p) b -> p k b", p=128)).then_inc(s_cmod, 16)
            sp.dma_start(wmod_st.rearrange("p (k n) -> p k n", k=KK),
                         wmod.rearrange("(k p) n -> p k n", p=128)).then_inc(s_cmod, 16)
            sp.dma_start(xs[:, 0:TT, :], xd[:, 0:TT, :]).then_inc(s_x0, 16)
            for k in range(KK):
                sp.dma_start(wst[k], wqkv_t[k * 128:(k + 1) * 128, :]).then_inc(s_wq, 16)
            sp.dma_start(ropes[:, :, :], rope.rearrange("c p s -> p c s")).then_inc(s_small, 16)
            sp.dma_start(gate_f[:, :, :], gate_t.rearrange("(k p) e -> p k e", p=128)).then_inc(s_small, 16)
            sp.dma_start(tc[:, :], tabc.rearrange("(a n) -> a n", a=1).to_broadcast([128, tabc.shape[0]])).then_inc(s_small, 16)
            sp.dma_start(wo_st.rearrange("p (h d) -> p h d", h=NH),
                         wo_t.rearrange("(h p) d -> p h d", p=128)).then_inc(s_wo, 16)
            sp.wait_ge(s_mod, MODSTEPS)
            sp.dma_start(mscr[:, :], mrow).then_inc(s_mscr, 16)
            sp.wait_ge(s_mscr, 16)

            def mod_rows(dst, b, a, n, done):
                sp.dma_start(dst, mscr[bass.ds(b, 1), a * D:(a + n) * D].to_broadcast([128, n * D])).then_inc(done, 16)

            ra, rb = (t[:, :, :].rearrange("p a b -> p (a b)") for t in (rows_a, rows_b))
            mod_rows(ra, 0, 0, 2, s_ra)
            mod_rows(rb, 0, 2, 3, s_rb)
            sp.wait_ge(s_wlo, NPIECE)
            sp.dma_start(xs[:, TT:, :], xd[:, TT:, :]).then_inc(s_xr, 16)
            sp.wait_ge(s_hm, 1)
            mod_rows(ra, 1, 0, 2, s_ra)
            with sp.Fori(0, B - 2) as b:
                sp.wait_ge(s_hm, b * 2 + 2)
                mod_rows(ra, b + 2, 0, 2, s_ra)
                sp.wait_ge(s_hm, b * 2 + 3)
                mod_rows(rb, b + 1, 2, 3, s_rb)
                sp.dma_start(hsh[:, bass.ds(b * TT, TT), :], hm_b[:, :, :]).then_inc(s_shst, 16)
            sp.wait_ge(s_hm, 2 * B - 1)
            mod_rows(rb, B - 1, 2, 3, s_rb)
            sp.dma_start(hsh[:, (B - 2) * TT:(B - 1) * TT, :], hm_b[:, :, :]).then_inc(s_shst, 16)
            sp.wait_ge(s_hm, 2 * B)
            sp.dma_start(hsh[:, (B - 1) * TT:, :], hm_b[:, :, :]).then_inc(s_shst, 16)

            sp.wait_ge(s_idx, B)
            sp.wait_ge(s_shst, 16 * (B + 1))
            sp.wait_ge(s_sent, B + 1)
            for n, (hi, lo, p, w) in enumerate(P2):
                if n >= 2:
                    sp.wait_ge(s_w2lo, n - 1)
                src = w13_t[n // 2, :, (n % 2) * w:(n % 2 + 1) * w] if n < 2 * KK else \
                    w2_t[(n - 2 * KK) // 2, :, (n % 2) * w:(n % 2 + 1) * w]
                sp.dma_start(stage[0:p, n % 2, 0:w], src).then_inc(s_w2st[n % 2], 16)
            sp.wait_ge(s_zero, 1)
            sp.wait_ge(s_tab, TABSTEPS)
            with sp.Fori(0, E) as e:
                at = sp.value_load(runu[0:1, bass.ds(e, 1)], min_val=0, max_val=SH0 - 128)
                sp.dma_start(hd[bass.ds(at, 128), :], zrow[:, :]).then_inc(s_pad, 16)

            def load(j, r):
                at = sp.value_load(tab_r[0:1, bass.ds(j, 1)], min_val=0, max_val=SH0 + T - 128)
                sp.dma_start(xt[:, r, :], hd[bass.ds(at, 128), :]).then_inc(s_ld[r], 16)

            def store(j, u, r):
                sp.wait_ge(s_ev, j + (1 + SLOTS))
                sp.dma_start(yd[bass.ds(j * 128, 128), :], ys[:, r, :]).then_inc(s_st[r], 16)

            sp.wait_ge(s_pad, 16 * E)
            for r in range(UNR):
                load(r, r)
            with sp.Fori(0, NT // UNR - 1) as u:
                for r in range(UNR):
                    sp.wait_ge(s_t1, u * UNR + (r + 1))
                    load(u * UNR + (r + UNR), r)
                    store(u * UNR + r, u, r)
            for r in range(UNR):
                store(NT - UNR + r, None, r)
            for r in range(UNR):
                sp.wait_ge(s_st[r], 16 * (NT // UNR + 1))

            def fetch(b, r):
                sp.dma_start(ysh[:, r, :, :], ysd[:, bass.ds(b * TT, TT), :]).then_inc(s_sh[r], 16)
                sp.dma_start(gbr[:, r, :], mscr[bass.ds(b, 1), 5 * D:6 * D].to_broadcast([128, D])).then_inc(s_sh[r], 16)

            fetch(0, 0)
            fetch(1, 1)
            with sp.Fori(0, B // 2 - 1) as u:
                for r in range(2):
                    sp.wait_ge(s_yo, u * 2 + (r + 1))
                    sp.dma_start(od[:, bass.ds(u * 2 * TT + r * TT, TT), :], yo[:, r, :, :]).then_inc(s_out[r], 16)
                    fetch(u * 2 + (r + 2), r)
            for r in range(2):
                sp.wait_ge(s_yo, B - 1 + r)
                sp.dma_start(od[:, (B - 2 + r) * TT:(B - 1 + r) * TT, :], yo[:, r, :, :]).then_inc(s_out[r], 16)
            for r in range(2):
                sp.wait_ge(s_out[r], 16 * (B // 2 + 1))

        @block.gpsimd
        def _(pool):
            pool.sem_inc(s_rt2, SLOTS)
            pool.sem_inc(s_sent, 1)
            pool.sem_inc(s_gat, 1)
            nc.gpsimd.memset(ident[:, :], 0.0).then_inc(s_const, 1)
            nc.gpsimd.memset(identb[:, :], 0.0).then_inc(s_const, 1)
            nc.gpsimd.memset(maskb[:, :], 0.0).then_inc(s_const, 1)
            nc.gpsimd.memset(cst[:, 0, :], EPS).then_inc(s_const, 1)
            nc.gpsimd.memset(cst[:, 1, :], -0.5).then_inc(s_const, 1)
            nc.gpsimd.memset(prob[:, :, :], -1.0).then_inc(s_const, 1)
            nc.gpsimd.memset(mx8[:, :, :, :], -1.0).then_inc(s_const, 1)
            nc.gpsimd.memset(ones[:, :], 1.0).then_inc(s_const, 1)
            pool.wait_ge(s_const, 8)
            for m in (ident, identb):
                nc.gpsimd.affine_select(out=m[:, :], in_=m[:, :], compare_op=ALU.not_equal, fill=1.0, base=0,
                                        pattern=[[-1, 128]], channel_multiplier=1).then_inc(s_const, 1)
            nc.gpsimd.affine_select(out=maskb[:, :], in_=maskb[:, :], compare_op=ALU.is_ge, fill=NEG, base=0,
                                    pattern=[[-1, 128]], channel_multiplier=1).then_inc(s_const, 1)
            nc.gpsimd.affine_select(out=upper[:, :], in_=ones[:, :], compare_op=ALU.is_gt, fill=0.0, base=0,
                                    pattern=[[1, 128]], channel_multiplier=-1).then_inc(s_const, 1)

            def inverse_std(n):
                pool.wait_ge(s_mv, n + 1)
                nc.gpsimd.tensor_tensor(vare[:, :], mv[:, :, 1], cst[:, 0, :], ALU.add).then_inc(s_var, 1)
                pool.wait_ge(s_var, n + 1)
                nc.gpsimd.tensor_tensor(rstd[:, :], vare[:, :], cst[:, 1, :], ALU.pow).then_inc(s_rstd, 1)

            def modulate(n, hm, rows, s_at, c_at, s_rows, b):
                pool.wait_ge(s_xn, n + 1)
                pool.wait_ge(s_rows, b * 16 + 16)
                nc.gpsimd.tensor_tensor(hc[:, :, :], xn[:, :, :], rows[:, c_at:c_at + 1, :].to_broadcast([128, TT, D]),
                                        ALU.mult).then_inc(s_hc, 1)
                pool.wait_ge(s_hc, n + 1)
                if hm is hm_b:
                    pool.wait_ge(s_shst, b * 16 + 16)
                    pool.wait_ge(s_sent, b + 1)
                nc.gpsimd.tensor_tensor(hm[:, :, :], hc[:, :, :], rows[:, s_at:s_at + 1, :].to_broadcast([128, TT, D]),
                                        ALU.add).then_inc(s_hm, 1)

            def rope_tile(b, n, r, first=None):
                if first is not None:
                    pool.wait_ge(s_hm, first)
                pool.wait_ge(s_qsw, n + (b * NQK + 1))
                pool.wait_ge(s_rot, n + (b * NQK + 1))
                nc.gpsimd.tensor_tensor(rt2[:, r, :], qsw[:, r, :], ropes[:, 1, :], ALU.mult).then_inc(s_rt2, 1)

            def rope_tiles(b, n, std=None):
                with pool.Fori(0, NQK // 2 - 2) as u:
                    for r in range(2):
                        rope_tile(b, u * 2 + r, r, n if r == 0 else None)
                for t in range(NQK - 4, NQK):
                    rope_tile(b, t, t % 2)
                    if std is not None and t == NQK - 3:
                        inverse_std(std)

            def normalise(b, h, slot):
                for q, i in enumerate(STRIPS):
                    w = 128 * (i + 1)
                    p = pr[:, slot, P_AT[i]:P_AT[i] + w]
                    if q == 0:
                        pool.wait_ge(s_rinv, h + (b * NH + 1))
                    last = nc.gpsimd.tensor_tensor(p, p, rinv[:, slot, i:i + 1].to_broadcast([128, w]), ALU.mult)
                last.then_inc(s_norm, 1)

            def scatter(i):
                for k in range(2):
                    nc.gpsimd.indirect_dma_start(
                        out=hd[:, :], out_offset=bass.IndirectOffsetOnAxis(ap=idxs[:, k, i:i + 1], axis=0),
                        in_=hm_b[:, i, :], in_offset=None).then_inc(s_scat, 16)

            def begin_scatter(b, n):
                pool.wait_ge(s_idx, b + 1)
                pool.wait_ge(s_hm, n + 1)
                pool_carrier()

            def end_scatter(b):
                pool.wait_ge(s_scat, b * (16 * 2 * TT) + 16 * 2 * TT)
                pool_carrier(2).then_inc(s_sent, 1)

            def attention(b, before=None):
                with pool.Fori(0, NKV - 1) as g:
                    for r in range(GRP):
                        normalise(b, g * GRP + r, r)
                for r in range(GRP):
                    normalise(b, NH - GRP + r, r)
                    if before is not None:
                        if r == 0:
                            begin_scatter(before, before * 2 + 2)
                        scatter(r)
                if before is not None:
                    end_scatter(before)

            pool.wait_ge(s_const, 12)
            pool.wait_ge(s_small, 48)
            inverse_std(0)
            modulate(0, hm_a, rows_a, 0, 1, s_ra, 0)
            rope_tiles(0, 1)
            attention(0)
            with pool.Fori(0, B - 1) as b:
                inverse_std(b * 2 + 1)
                modulate(b * 2 + 1, hm_a, rows_a, 0, 1, s_ra, b + 1)
                rope_tiles(b + 1, b * 2 + 2, b * 2 + 2)
                pool.wait_ge(s_rot, b * NQK + (2 * NQK + SLOTS))
                modulate(b * 2 + 2, hm_b, rows_b, 1, 2, s_rb, b)
                attention(b + 1, b)
            inverse_std(2 * B - 1)
            modulate(2 * B - 1, hm_b, rows_b, 1, 2, s_rb, B - 1)
            begin_scatter(B - 1, 2 * B - 1)
            for i in range(TT):
                scatter(i)
            end_scatter(B - 1)

            pool.wait_ge(s_shst, 16 * (B + 1))
            nc.gpsimd.memset(zrow[:, :], 0.0).then_inc(s_zero, 1)

            for r in range(UNR):
                pool.wait_ge(s_st[r], 16 * (NT // UNR + 1))
            with pool.Fori(0, B // 2) as u:
                for r in range(2):
                    pool.wait_ge(s_ix, u * 2 + (r + 1))
                    pool.wait_ge(s_gat, u * 2 + (r + 1))
                    pool_carrier().then_inc(s_gat, 1)
                    for k in range(2):
                        for i in range(TT):
                            nc.gpsimd.indirect_dma_start(
                                out=yg[:, r, k, i, :], out_offset=None, in_=yd[:, :],
                                in_offset=bass.IndirectOffsetOnAxis(ap=ixg[:, r, k, i:i + 1], axis=0)).then_inc(s_ga[r], 16)

        @block.scalar
        def _(act):
            act.sem_inc(s_exp, TT)
            act.wait_ge(s_cmod, 32)
            nc.scalar.activation(cE[:, :, :], cT[:, :, :], ACT.Exp, scale=-1.0).then_inc(s_cexp, 1)
            act.wait_ge(s_wq, 32)
            for k in range(KK):
                for a, b, f in SPANS:
                    nc.scalar.activation(wqkv_hi[:, k, a:b], wst[k][:, a:b], ACT.Copy,
                                         scale=f).then_inc(s_whi, 1)
            act.wait_ge(s_wo, 16)
            nc.scalar.activation(wo_hi[:, :, :].rearrange("p a b -> p (a b)"), wo_st, ACT.Copy,
                                 scale=WSCALE).then_inc(s_whi, 1)
            act.wait_ge(s_small, 48)
            nc.scalar.activation(gate_hi[:, :, :], gate_f[:, :, :], ACT.Copy, scale=WSCALE).then_inc(s_whi, 1)

            def transposed_hi(n, bank):
                for k in range(KK):
                    act.wait_ge(s_tr, n * KK + (k + 1))
                    nc.scalar.copy(hT_hi[:, k, :], ps[:, bank + k, :]).then_inc(s_trhi, 1)

            def swap(b, n, bank, slot):
                act.wait_ge(s_qmm, n + (b * NQK + 1))
                act.wait_ge(s_rt2, n + (b * NQK + 1))
                nc.scalar.copy(qsw[0:64, slot, :], ps[64:128, bank, :])
                nc.scalar.copy(qsw[64:128, slot, :], ps[0:64, bank, :]).then_inc(s_qsw, 1)

            def rot_hi(b, n, slot):
                act.wait_ge(s_rot, n + (b * NQK + 1 + SLOTS))
                nc.scalar.copy(qk_hi[:, n, :], rt1[:, slot, :]).then_inc(s_qhi, 1)

            def projections(b):
                swap(b, 0, 4, 0)
                swap(b, 1, 5, 1)
                with act.Fori(0, NQK // 4 - 1) as u:
                    for r in range(4):
                        swap(b, u * 4 + (r + 2), 4 + (r + 2) % 4, r % 2)
                        rot_hi(b, u * 4 + r, r % 2)
                for n in range(NQK - 4, NQK):
                    if n + 2 < NQK:
                        swap(b, n + 2, 4 + (n + 2) % 4, n % 2)
                    rot_hi(b, n, n % 2)
                for m in range(TT):
                    act.wait_ge(s_vmm, b * TT + (m + 1))
                    nc.scalar.activation(v_hi[:, m, :], ps[:, 4 + m, :], ACT.Copy,
                                         scale=1.0 / WSCALE).then_inc(s_vhi, 1)

            def exps(H, slot, strips=STRIPS):
                for i in strips:
                    bank, col = S_BANK[i]
                    w = 128 * (i + 1)
                    act.wait_ge(s_max, H * TT + M_READY[i])
                    nc.scalar.activation(pr[:, slot, P_AT[i]:P_AT[i] + w], ps[:, bank, col:col + w], ACT.Exp,
                                         bias=negm[:, slot, i:i + 1],
                                         accum_out=rsum[:, slot, i:i + 1]).then_inc(s_exp, 1)

            def transposed_p(H, slot):
                for n, (bank, at, w) in enumerate(PT_EVAC):
                    act.wait_ge(s_pt, H * PTB + (n + 1))
                    nc.scalar.activation(pt_hi[:, slot, at:at + w], ps[:, bank, 0:w], ACT.Copy,
                                         scale=PSCALE).then_inc(s_pthi, 1)

            def head(b, h, r, last=False, logits=None):
                H = h + b * NH
                if not last or h < NH - 1:
                    transposed_p(H + 1, (r + 1) % 2)
                if logits is not None:
                    router_exps(logits)
                more = not last or h < NH - 3
                if more:
                    exps(H + 3, (r + 3) % GRP, STRIPS[:3])
                act.wait_ge(s_pv, H + 1)
                nc.scalar.activation(qk_hi[:, NKV + h, :], ps[:, 6 + r % 2, :], ACT.Copy,
                                     scale=1.0 / PSCALE).then_inc(s_ohi, 1)
                if more:
                    exps(H + 3, (r + 3) % GRP, STRIPS[3:])

            def router_exps(b):
                act.wait_ge(s_route, b * ROUTE + 2)
                for i in range(TT):
                    nc.scalar.activation(ex[:, i, 0:E], lg[:, i, 0:E], ACT.Exp, bias=lsum[:, 0, i:i + 1],
                                         accum_out=lsum[:, 1, i:i + 1]).then_inc(s_lgex, 1)

            def attention(b, before=None):
                exps(b * NH, 0)
                exps(b * NH + 1, 1)
                if before is not None:
                    transposed_hi(before * 2 + 2, 6)
                exps(b * NH + 2, 2)
                transposed_p(b * NH, 0)
                first = 0
                if before is not None:
                    first = 1
                    for r in range(GRP):
                        head(b, r, r, False, before if r == 1 else None)
                with act.Fori(first, NKV - 1) as g:
                    for r in range(GRP):
                        head(b, g * GRP + r, r)
                for r in range(GRP):
                    head(b, NH - GRP + r, r, True)

            transposed_hi(0, 6)
            projections(0)
            attention(0)
            with act.Fori(0, B - 1) as b:
                transposed_hi(b * 2 + 1, 6)
                projections(b + 1)
                attention(b + 1, b)
            transposed_hi(2 * B - 1, 6)
            router_exps(B - 1)

            for n, (hi, lo, p, w) in enumerate(P2):
                act.wait_ge(s_w2st[n % 2], 16 * (n // 2 + 1))
                nc.scalar.activation(hi, stage[0:p, n % 2, 0:w], ACT.Copy, scale=WSCALE).then_inc(s_w2hi, 1)

            def tile_step(u, r):
                for what, n, m, q in stages(u, r):
                    if what == "t1":
                        act.wait_ge(s_t1, n + 1)
                        nc.scalar.copy(xT_hi[:, m % 2, :, :], pst1(m)).then_inc(s_t1hi, 1)
                    if what == "up":
                        act.wait_ge(s_up, n + 1)
                        nc.scalar.activation(sg[:, m % 2, :], ps[:, 2 + m % 2, 0:INTER], ACT.Silu,
                                             scale=1.0 / WSCALE).then_inc(s_sg, 1)
                    if what == "t2":
                        act.wait_ge(s_t2, n + 1)
                        nc.scalar.copy(aT_hi[:, m % 2, :, :], pst2(m)).then_inc(s_t2hi, 1)

            run_tiles(act, tile_step)

        @block.vector
        def _(dve):
            dve.sem_inc(s_rot, SLOTS)
            dve.sem_inc(s_olo, SLOTS)
            dve.sem_inc(s_ev, SLOTS)
            dve.sem_inc(s_rt1, QBANKS)
            dve.sem_inc(s_ptlo, PTB)
            dve.wait_ge(s_const, 12)

            dve.wait_ge(s_cexp, 1)
            nc.vector.tensor_scalar(siluT[:, :, :], cE[:, :, :], 1.0, None, ALU.add).then_inc(s_silu, 1)
            dve.wait_ge(s_silu, 1)
            nc.vector.reciprocal(cE[:, :, :], siluT[:, :, :]).then_inc(s_silu, 1)
            dve.wait_ge(s_silu, 2)
            nc.vector.tensor_tensor(siluT[:, :, :], cE[:, :, :], cT[:, :, :], ALU.mult).then_inc(s_silu, 1)

            def statistics(n, t):
                carrier()
                for i in range(TT):
                    last = nc.vector.bn_stats(bst[:, i, :], xs[:, t + i, :])
                last.then_inc(s_bn, 1)
                dve.wait_ge(s_bn, n + 1)
                carrier()
                for i in range(TT):
                    last = nc.vector.bn_aggr(mv[:, i, :], bst[:, i, :])
                last.then_inc(s_mv, 1)

            def normalise(n, t):
                dve.wait_ge(s_mv, n + 1)
                dve.wait_ge(s_rstd, n + 1)
                for i in range(TT):
                    last = nc.vector.tensor_scalar(xn[:, i, :], xs[:, t + i, :], mv[:, i, 0:1], rstd[:, i:i + 1],
                                                   ALU.subtract, ALU.mult)
                last.then_inc(s_xn, 1)

            dve.wait_ge(s_x0, 16)
            statistics(0, 0)
            normalise(0, 0)

            dve.wait_ge(s_modmm, 1)
            nc.vector.tensor_copy(mrow, ps[0:B, 5:8, :].rearrange("p a b -> p (a b)")).then_inc(s_mod, 1)
            dve.wait_ge(s_mod, 1)
            for a in (1, 4):
                m = mrow[:, a * D:(a + 1) * D]
                nc.vector.tensor_scalar(m, m, 1.0, None, ALU.add).then_inc(s_mod, 1)
            for j, (a, neg, ab) in enumerate(((2, mneg, mabs), (5, mneg2, mabs2))):
                m = mrow[:, a * D:(a + 1) * D]
                nc.vector.tensor_scalar(neg, m, -1.0, None, ALU.mult).then_inc(s_mod, 1)
                dve.wait_ge(s_mod, 4 + 6 * j)
                nc.vector.tensor_tensor(ab, m, neg, ALU.max).then_inc(s_mod, 1)
                dve.wait_ge(s_mod, 5 + 6 * j)
                nc.vector.tensor_scalar(neg, m, 0.0, 2.0, ALU.is_ge, ALU.mult).then_inc(s_mod, 1)
                nc.vector.tensor_scalar(ab, ab, 0.25, None, ALU.max).then_inc(s_mod, 1)
                dve.wait_ge(s_mod, 7 + 6 * j)
                nc.vector.tensor_scalar(neg, neg, 1.0, None, ALU.subtract).then_inc(s_mod, 1)
                dve.wait_ge(s_mod, 8 + 6 * j)
                nc.vector.tensor_tensor(m, neg, ab, ALU.mult).then_inc(s_mod, 1)

            n = 0
            for k in range(KK):
                for a, b, f in SPANS:
                    n += 1
                    dve.wait_ge(s_whi, n)
                    nc.vector.scalar_tensor_tensor(wqkv_lo[:, k, a:b], wst[k][:, a:b], f,
                                                   wqkv_hi[:, k, a:b], ALU.mult, ALU.subtract).then_inc(s_wlo, 1)
            dve.wait_ge(s_whi, n + 1)
            nc.vector.scalar_tensor_tensor(wo_lo[:, :, :].rearrange("p a b -> p (a b)"), wo_st, WSCALE,
                                           wo_hi[:, :, :].rearrange("p a b -> p (a b)"),
                                           ALU.mult, ALU.subtract).then_inc(s_wlo, 1)
            dve.wait_ge(s_whi, n + 2)
            nc.vector.scalar_tensor_tensor(gate_lo[:, :, :], gate_f[:, :, :], WSCALE, gate_hi[:, :, :],
                                           ALU.mult, ALU.subtract).then_inc(s_wlo, 1)
            dve.wait_ge(s_wlo, NPIECE)
            dve.wait_ge(s_small, 48)
            nc.vector.tensor_copy(run[:, :], tc[:, C_E0:C_E0 + E]).then_inc(s_run, 1)
            dve.wait_ge(s_xr, 16)

            def transposed_lo(n, bank):
                for k in range(KK):
                    dve.wait_ge(s_trhi, n * KK + (k + 1))
                    nc.vector.tensor_tensor(hT_lo[:, k, :], ps[:, bank + k, :], hT_hi[:, k, :],
                                            ALU.subtract).then_inc(s_trlo, 1)

            def rot_cos(b, n, bank, slot):
                dve.wait_ge(s_qsw, n + (b * NQK + 1))
                nc.vector.tensor_tensor(rt1[:, slot, :], ps[:, bank, :], ropes[:, 0, :],
                                        ALU.mult).then_inc(s_rt1, 1)

            def rot_sum(b, n, slot):
                dve.wait_ge(s_rt1, n + (b * NQK + 1 + QBANKS))
                dve.wait_ge(s_rt2, n + (b * NQK + 1 + SLOTS))
                nc.vector.tensor_tensor(rt1[:, slot, :], rt1[:, slot, :], rt2[:, slot, :],
                                        ALU.add).then_inc(s_rot, 1)

            def rot_lo(b, n, slot):
                dve.wait_ge(s_qhi, n + (b * NQK + 1))
                nc.vector.tensor_tensor(qk_lo[:, n, :], rt1[:, slot, :], qk_hi[:, n, :],
                                        ALU.subtract).then_inc(s_qlo, 1)
                dve.wait_ge(s_qlo, n + (b * NQK + 1))

            def projections(b, residual_of=None):
                rot_cos(b, 0, 4, 0)
                rot_sum(b, 0, 0)
                with dve.Fori(0, NQK // 4 - 1) as u:
                    for r in range(4):
                        rot_cos(b, u * 4 + (r + 1), 4 + (r + 1) % 4, (r + 1) % 2)
                        rot_sum(b, u * 4 + (r + 1), (r + 1) % 2)
                        rot_lo(b, u * 4 + r, r % 2)
                for n in range(NQK - 4, NQK):
                    if n + 1 < NQK:
                        rot_cos(b, n + 1, 4 + (n + 1) % 4, (n + 1) % 2)
                        rot_sum(b, n + 1, (n + 1) % 2)
                    rot_lo(b, n, n % 2)
                    if residual_of is not None and n == NQK - 4:
                        residual(residual_of, residual_of * 2 + 1)
                        statistics(residual_of * 2 + 2, residual_of * TT)
                    if residual_of is not None and n == NQK - 2:
                        normalise(residual_of * 2 + 2, residual_of * TT)
                for m in range(TT):
                    dve.wait_ge(s_vhi, b * TT + (m + 1))
                    nc.vector.scalar_tensor_tensor(v_lo[:, m, :], ps[:, 4 + m, :], 1.0 / WSCALE, v_hi[:, m, :],
                                                   ALU.mult, ALU.subtract).then_inc(s_vlo, 1)

            def maxima(H, slot, strips=STRIPS, rows_of=None):
                for i in strips:
                    bank, col = S_BANK[i]
                    dve.wait_ge(s_sc, H * 3 + S_READY[i])
                    if rows_of is not None and i == 1:
                        expert_rows(rows_of)
                    nc.vector.tensor_reduce(negm[:, slot, i:i + 1], ps[:, bank, col:col + 128 * (i + 1)], AX.X,
                                            ALU.max, negate=True).then_inc(s_max, 1)

            def inverse(H, slot):
                dve.wait_ge(s_exp, H * TT + 2 * TT)
                nc.vector.reciprocal(rinv[:, slot, :], rsum[:, slot, :]).then_inc(s_rinv, 1)

            def transposed_p(H, slot, parts=range(PTB)):
                for n in parts:
                    bank, at, w = PT_EVAC[n]
                    dve.wait_ge(s_pthi, H * PTB + (n + 1))
                    nc.vector.scalar_tensor_tensor(pt_lo[:, slot, at:at + w], ps[:, bank, 0:w], PSCALE,
                                                   pt_hi[:, slot, at:at + w], ALU.mult, ALU.subtract).then_inc(s_ptlo, 1)

            def head(b, h, r, last=False, rows_of=None):
                H = h + b * NH
                after, more = not last or h < NH - 1, not last or h < NH - 3
                if more:
                    maxima(H + 3, (r + 3) % GRP, STRIPS[:3])
                if after:
                    transposed_p(H + 1, (r + 1) % 2, (0, 1))
                if more:
                    maxima(H + 3, (r + 3) % GRP, STRIPS[3:], rows_of)
                if after:
                    transposed_p(H + 1, (r + 1) % 2, (2,))
                if more:
                    inverse(H + 3, (r + 3) % GRP)
                dve.wait_ge(s_ohi, H + 1)
                nc.vector.scalar_tensor_tensor(qk_lo[:, NKV + h, :], ps[:, 6 + r % 2, :], 1.0 / PSCALE,
                                               qk_hi[:, NKV + h, :], ALU.mult, ALU.subtract).then_inc(s_olo, 1)

            def attention(b, before=None):
                for k in range(2):
                    maxima(b * NH + k, k)
                    inverse(b * NH + k, k)
                if before is not None:
                    transposed_lo(before * 2 + 2, 6)
                maxima(b * NH + 2, 2)
                inverse(b * NH + 2, 2)
                transposed_p(b * NH, 0)
                first = 0
                if before is not None:
                    first = 1
                    for r, part in enumerate((router_logits, router_choice, router_marks, router_rows)):
                        head(b, r, r, False, before if r == 3 else None)
                        part(before)
                with dve.Fori(first, NKV - 1) as g:
                    for r in range(GRP):
                        head(b, g * GRP + r, r)
                for r in range(GRP):
                    head(b, NH - GRP + r, r, True)

            def residual(b, n):
                dve.wait_ge(s_op, b * NH + NH)
                dve.wait_ge(s_rb, b * 16 + 16)
                dve.wait_ge(s_hc, n + 1)
                nc.vector.scalar_tensor_tensor(xn[:, :, :], ps[:, 0:TT, 0:D], 1.0 / WSCALE,
                                               rows_b[:, 0:1, :].to_broadcast([128, TT, D]),
                                               ALU.mult, ALU.mult).then_inc(s_opev, 1)
                dve.wait_ge(s_opev, b + 1)
                nc.vector.tensor_tensor(xs[:, bass.ds(b * TT, TT), :], xs[:, bass.ds(b * TT, TT), :], xn[:, :, :],
                                        ALU.add).then_inc(s_x2, 1)
                dve.wait_ge(s_x2, b + 1)

            def router_logits(b):
                dve.wait_ge(s_lgmm, b + 1)
                nc.vector.tensor_scalar(lg[:, :, 0:E], ps[:, 7, 0:TT * 16].rearrange("p (t e) -> p t e", e=16)[:, :, 0:E],
                                        1.0 / WSCALE, None, ALU.mult).then_inc(s_route, 1)
                dve.wait_ge(s_route, b * ROUTE + 1)
                nc.vector.tensor_reduce(lsum[:, 0, :], lg[:, :, 0:E], AX.X, ALU.max, negate=True).then_inc(s_route, 1)

            def router_choice(b):
                dve.wait_ge(s_lgex, b * TT + TT)
                nc.vector.reciprocal(lsum[:, 2, :], lsum[:, 1, :]).then_inc(s_route, 1)
                dve.wait_ge(s_route, b * ROUTE + 3)
                for i in range(TT):
                    last = nc.vector.tensor_scalar(prob[:, i, 0:E], ex[:, i, 0:E], lsum[:, 2, i:i + 1], None, ALU.mult)
                last.then_inc(s_route, 1)
                dve.wait_ge(s_route, b * ROUTE + 4)
                carrier()
                for i in range(TT):
                    last = nc.vector.max(rep[:, 0, i, 0:8], prob[:, i, 0:E])
                last.then_inc(s_route, 1)
                dve.wait_ge(s_route, b * ROUTE + 5)
                nc.vector.tensor_copy(mx8[:, 0, :, 0:1], rep[:, 0, :, 0:1])
                nc.vector.tensor_copy(mx8[:, 1, :, 0:2], rep[:, 0, :, 0:2])
                nc.vector.tensor_copy(wts[:, :, bass.ds(b * TT, TT)], rep[:, 0, :, 0:2].rearrange("p t k -> p k t")).then_inc(s_route, 1)

            def router_marks(b):
                dve.wait_ge(s_route, b * ROUTE + 6)
                carrier()
                for k in range(2):
                    for i in range(TT):
                        last = nc.vector.match_replace(out=rep[:, k, i, 0:22], in_to_replace=mx8[:, k, i, :],
                                                       in_values=prob[:, i, 0:22], imm_value=-2.0)
                last.then_inc(s_route, 1)
                dve.wait_ge(s_route, b * ROUTE + 7)
                nc.vector.tensor_scalar(hot[:, 1:3, :, :].rearrange("p k t e -> p (k t) e"),
                                        rep[:, :, :, 0:E].rearrange("p k t e -> p (k t) e"), -2.0, None, ALU.is_equal)
                nc.vector.tensor_scalar(hot16[:, :, :], rep[:, 1, :, 0:E], -2.0, None, ALU.is_equal).then_inc(s_route, 1)
                dve.wait_ge(s_route, b * ROUTE + 8)
                nc.vector.tensor_tensor(hot[:, 0, :, :], hot[:, 2, :, :], hot[:, 1, :, :], ALU.subtract).then_inc(s_p1, 1)

            def expert_rows(b):
                dve.wait_ge(s_posmm, b + 1)
                dve.wait_ge(s_run, b + 1)
                nc.vector.tensor_tensor(posa[:, 2, :, :], ps[:, 2, R_AT:R_AT + TT * 16].rearrange("p (t e) -> p t e", e=16)[:, :, 0:E],
                                        run[:, :].unsqueeze(1).to_broadcast([128, TT, E]), ALU.add).then_inc(s_p1, 1)
                dve.wait_ge(s_p1, b * 6 + 2)
                nc.vector.tensor_tensor(run[:, :], run[:, :], ps[:, 2, R_AT + TT * 16:R_AT + TT * 16 + E], ALU.add).then_inc(s_run, 1)

            def router_rows(b):
                nc.vector.tensor_tensor(posa[:, 0, :, :], posa[:, 2, :, :], hot[:, 1, :, :], ALU.mult).then_inc(s_p1, 1)
                nc.vector.tensor_tensor(posa[:, 1, :, :], posa[:, 2, :, :], hot[:, 0, :, :], ALU.mult).then_inc(s_p1, 1)
                dve.wait_ge(s_p1, b * 6 + 4)
                nc.vector.tensor_reduce(posf[:, :, :], posa[:, 0:2, :, :], AX.X, ALU.add).then_inc(s_p1, 1)
                dve.wait_ge(s_p1, b * 6 + 5)
                dve.wait_ge(s_sent, b + 1)
                nc.vector.tensor_copy(idxs[:, :, :], posf[:, :, :]).then_inc(s_idx, 1)
                nc.vector.tensor_copy(dst[:, :, bass.ds(b * TT, TT)], posf[:, :, :]).then_inc(s_p1, 1)

            transposed_lo(0, 6)
            projections(0)
            attention(0)
            with dve.Fori(0, B - 1) as b:
                statistics(b * 2 + 1, b * TT + TT)
                normalise(b * 2 + 1, b * TT + TT)
                transposed_lo(b * 2 + 1, 6)
                projections(b + 1, b)
                attention(b + 1, b)
            residual(B - 1, 2 * B - 2)
            statistics(2 * B - 1, (B - 1) * TT)
            normalise(2 * B - 1, (B - 1) * TT)
            transposed_lo(2 * B - 1, 6)
            router_logits(B - 1)
            router_choice(B - 1)
            router_marks(B - 1)
            expert_rows(B - 1)
            router_rows(B - 1)
            dve.wait_ge(s_run, B + 1)
            dve.wait_ge(s_shst, 16 * (B + 1))
            dve.wait_ge(s_sent, B + 1)

            step = [0]

            def then(ins):
                step[0] += 1
                ins.then_inc(s_tab, 1)
                dve.wait_ge(s_tab, step[0])

            def row(t, shape, axis=None):
                return t.unsqueeze(axis).to_broadcast(shape)

            c0 = lambda at, n: tc[0:1, at:at + n]
            call = lambda at, n: tc[:, at:at + n]
            cnt, tiles, cum, off, base, jump = (tcnt[:, k, :] for k in range(6))
            seq_e, seq_a, seq_u, seq_d, seq_m = (tseq[:, k, :] for k in range(5))
            then(nc.vector.tensor_copy(runu[:, :], run[0:1, :]))
            then(nc.vector.tensor_tensor(cnt, run[:, :], call(C_E0, E), ALU.subtract))
            m = tcmp[:, 0:E * 32].rearrange("p (e k) -> p e k", k=32)
            then(nc.vector.tensor_tensor(m, row(cnt, [128, E, 32], 2), row(call(C_K, 32), [128, E, 32], 1), ALU.is_gt))
            then(nc.vector.tensor_reduce(tiles, m, AX.X, ALU.add))
            m = tcmp[:, 0:E * E].rearrange("p (e k) -> p e k", k=E)
            then(nc.vector.tensor_tensor(m, row(tiles, [128, E, E], 1), call(C_TRI, E * E).rearrange("p (e k) -> p e k", k=E),
                                         ALU.mult))
            then(nc.vector.tensor_reduce(cum, m, AX.X, ALU.add))
            then(nc.vector.tensor_tensor(off, cum, tiles, ALU.subtract))
            then(nc.vector.scalar_tensor_tensor(base, off, -128.0, call(C_E0, E), ALU.mult, ALU.add))
            then(nc.vector.tensor_scalar(jump, tiles, 128.0, -float(REG), ALU.mult, ALU.add))
            rows = dst[:, :, :].rearrange("p k t -> p (k t)")
            n, big = 2 * B * TT, [128, 2 * B * TT, E - 1]
            m = tcmp[:, 0:n * (E - 1)].rearrange("p (n e) -> p n e", e=E - 1)
            then(nc.vector.tensor_tensor(m, row(rows, big, 2), row(call(C_E0 + 1, E - 1), big, 1), ALU.is_ge))
            then(nc.vector.tensor_tensor(m, m, row(jump[:, 0:E - 1], big, 1), ALU.mult))
            then(nc.vector.tensor_reduce(tsum[:, :], m, AX.X, ALU.add))
            then(nc.vector.scalar_tensor_tensor(yrow[:, :, :].rearrange("p k t -> p (k t)"), tsum[:, :], float(NSH * 128),
                                                rows, ALU.add, ALU.add))
            m = tcmp[0:1, :].rearrange("p (j e) -> p j e", e=E)
            then(nc.vector.tensor_tensor(m, row(cum[0:1, :], [1, NRT, E], 1), row(c0(C_J, NRT), [1, NRT, E], 2), ALU.is_le))
            then(nc.vector.tensor_reduce(seq_e, m, AX.X, ALU.add))
            then(nc.vector.tensor_tensor(m, row(seq_e, [1, NRT, E], 2), row(c0(C_J, E), [1, NRT, E], 1), ALU.is_equal))
            then(nc.vector.tensor_tensor(m, m, row(base[0:1, :], [1, NRT, E], 1), ALU.mult))
            then(nc.vector.tensor_reduce(seq_a, m, AX.X, ALU.add))
            then(nc.vector.tensor_scalar(seq_u, seq_e, float(E), None, ALU.is_lt))
            then(nc.vector.tensor_scalar(seq_d, c0(C_J, NRT), 128.0, -float(SH0), ALU.mult, ALU.add))
            then(nc.vector.tensor_tensor(seq_m, seq_d, seq_u, ALU.mult))
            then(nc.vector.scalar_tensor_tensor(tab_r[:, NSH:], seq_a, float(SH0), seq_m, ALU.add, ALU.add))
            then(nc.vector.tensor_copy(tab_e[:, NSH:], seq_e))
            then(nc.vector.tensor_copy(tab_e[:, 0:NSH], c0(C_SE, NSH)))
            then(nc.vector.tensor_copy(tab_r[:, 0:NSH], c0(C_SR, NSH)))
            assert step[0] == TABSTEPS

            for n, (hi, lo, p, w) in enumerate(P2):
                dve.wait_ge(s_w2hi, n + 1)
                nc.vector.scalar_tensor_tensor(lo, stage[0:p, n % 2, 0:w], WSCALE, hi, ALU.mult,
                                               ALU.subtract).then_inc(s_w2lo, 1)

            def tile_step(u, r):
                for what, n, m, q in stages(u, r):
                    if what == "t1":
                        dve.wait_ge(s_t1hi, n + 1)
                        nc.vector.tensor_tensor(xT_lo[:, m % 2, :, :], pst1(m), xT_hi[:, m % 2, :, :],
                                                ALU.subtract).then_inc(s_t1lo, 1)
                    if what == "up":
                        dve.wait_ge(s_sg, n + 1)
                        nc.vector.scalar_tensor_tensor(hh[:, m % 2, :], ps[:, 2 + m % 2, INTER:2 * INTER], 1.0 / WSCALE,
                                                       sg[:, m % 2, :], ALU.mult, ALU.mult).then_inc(s_hh, 1)
                    if what == "t2":
                        dve.wait_ge(s_t2hi, n + 1)
                        nc.vector.tensor_tensor(aT_lo[:, m % 2, :, :], pst2(m), aT_hi[:, m % 2, :, :],
                                                ALU.subtract).then_inc(s_t2lo, 1)
                    if what == "dn":
                        dve.wait_ge(s_dn, n + 1)
                        dve.wait_ge(s_st[m], q * 16 + 16)
                        nc.vector.tensor_scalar(ys[:, m, :], ps[:, 6 + m % 2, 0:D], 1.0 / WSCALE, None,
                                                ALU.mult).then_inc(s_ev, 1)

            run_tiles(dve, tile_step)

            for r in range(UNR):
                dve.wait_ge(s_st[r], 16 * (NT // UNR + 1))

            def indices(b, r):
                nc.vector.tensor_copy(ixg[:, r, :, :], yrow[:, :, bass.ds(b * TT, TT)]).then_inc(s_ix, 1)

            def combine(b, u, r):
                dve.wait_ge(s_ga[r], u * (16 * 2 * TT) + 16 * 2 * TT)
                dve.wait_ge(s_sh[r], u * 32 + 32)
                for i in range(TT):
                    last = nc.vector.scalar_tensor_tensor(ysh[:, r, i, :], yg[:, r, 0, i, :], wts[:, 0, bass.ds(b * TT + i, 1)],
                                                          ysh[:, r, i, :], ALU.mult, ALU.add)
                last.then_inc(s_c1, 1)
                dve.wait_ge(s_c1, b + 1)
                for i in range(TT):
                    last = nc.vector.scalar_tensor_tensor(ysh[:, r, i, :], yg[:, r, 1, i, :], wts[:, 1, bass.ds(b * TT + i, 1)],
                                                          ysh[:, r, i, :], ALU.mult, ALU.add)
                last.then_inc(s_c2, 1)
                dve.wait_ge(s_c2, b + 1)
                nc.vector.tensor_tensor(ysh[:, r, :, :], ysh[:, r, :, :], gbr[:, r:r + 1, :].to_broadcast([128, TT, D]),
                                        ALU.mult).then_inc(s_c3, 1)
                dve.wait_ge(s_c3, b + 1)
                dve.wait_ge(s_out[r], u * 16 + 16)
                nc.vector.tensor_tensor(yo[:, r, :, :], ysh[:, r, :, :], xs[:, bass.ds(b * TT, TT), :],
                                        ALU.add).then_inc(s_yo, 1)

            indices(0, 0)
            indices(1, 1)
            with dve.Fori(0, B // 2 - 1) as u:
                for r in range(2):
                    combine(u * 2 + r, u, r)
                    indices(u * 2 + (r + 2), r)
            for r in range(2):
                combine(B - 2 + r, B // 2 - 1, r)

        @block.tensor
        def _(pe):
            def split_product(dst, a_hi, a_lo, b_hi, b_lo, first, last):
                nc.tensor.matmul(dst, a_hi, b_hi, start=first, stop=False, skip_group_check=True)
                nc.tensor.matmul(dst, a_hi, b_lo, start=False, stop=False, skip_group_check=True)
                return nc.tensor.matmul(dst, a_lo, b_hi, start=False, stop=last, skip_group_check=True)

            pe.wait_ge(s_silu, 3)
            wm = wmod_st.rearrange("p (k n) -> p k n", k=KK)
            for j in range(3):
                for k in range(KK):
                    last = nc.tensor.matmul(ps[0:B, 5 + j, :], siluT[:, k, :], wm[:, k, j * 512:(j + 1) * 512],
                                            start=(k == 0), stop=(k == KK - 1))
            last.then_inc(s_modmm, 1)
            pe.wait_ge(s_const, 12)

            def transposes(n, hm):
                pe.wait_ge(s_hm, n + 1)
                for k in range(KK):
                    for i in range(TT):
                        last = nc.tensor.transpose(ps[:, 6 + k, i * 128:(i + 1) * 128],
                                                   hm[:, i, k * 128:(k + 1) * 128], ident[:, :])
                    last.then_inc(s_tr, 1)

            def project(b, u):
                for r in range(4):
                    pe.wait_ge(s_rt1, u * 4 + (b * NQK + r + 1))
                    w = bass.ds(u * 512 + r * 128, 128)
                    for k in range(KK):
                        last = split_product(ps[:, 4 + r, :], wqkv_hi[:, k, w], wqkv_lo[:, k, w],
                                             hT_hi[:, k, :], hT_lo[:, k, :], k == 0, k == KK - 1)
                    last.then_inc(s_qmm, 1)

            def project_v(b):
                for m in range(TT):
                    pe.wait_ge(s_rt1, b * NQK + (NQK - TT + m + 1 + QBANKS))
                    t = slice(m * 128, (m + 1) * 128)
                    for k in range(KK):
                        last = split_product(ps[:, 4 + m, :], hT_hi[:, k, t], hT_lo[:, k, t], wqkv_hi[:, k, VAT:],
                                             wqkv_lo[:, k, VAT:], k == 0, k == KK - 1)
                    last.then_inc(s_vmm, 1)

            def project_out(b, h, first=False):
                pe.wait_ge(s_olo, h + (b * NH + 1 + SLOTS))
                for i in range(TT):
                    t = slice(i * 128, (i + 1) * 128)
                    last = split_product(ps[:, i, 0:D], qk_hi[:, h + NKV, t], qk_lo[:, h + NKV, t], wo_hi[:, h, :],
                                         wo_lo[:, h, :], first, True)
                last.then_inc(s_op, 1)

            def scores(b, h, g, marks=None):
                pe.wait_ge(s_qlo, h + (b * NQK + NKV + 1))
                for i in STRIPS:
                    bank, col = S_BANK[i]
                    w = 128 * (i + 1)
                    q = slice(i * 128, (i + 1) * 128)
                    if i != 2:
                        pe.wait_ge(s_exp, h * TT + (b * (NH * TT) + E_DONE[i]))
                    if marks is not None and i == 1:
                        count(marks)
                    split_product(ps[:, bank, col:col + w], qk_hi[:, h + NKV, q], qk_lo[:, h + NKV, q],
                                  qk_hi[:, g, 0:w], qk_lo[:, g, 0:w], True, False)
                    last = nc.tensor.matmul(ps[:, bank, col + i * 128:col + w], identb[:, :], maskb[:, :],
                                            start=False, stop=True, skip_group_check=True)
                    if i != 0:
                        last.then_inc(s_sc, 1)

            def transpose_p(b, h, r):
                H = h + b * NH
                pe.wait_ge(s_norm, H + 1)
                for j in (0, 1, 3, 2):
                    bank, col = PT_BANK[j]
                    if j != 3:
                        pe.wait_ge(s_ptlo, H * PTB + (j + 1))
                    for i in range(j, TT):
                        at = P_AT[i] + 128 * j
                        last = nc.tensor.transpose(ps[:, bank, col + (i - j) * 128:col + (i - j + 1) * 128],
                                                   pr[:, r, at:at + 128], ident[:, :])
                    if j != 1:
                        last.then_inc(s_pt, 1)

            def head(b, h, r, g, last=False, marks=None):
                H = h + b * NH
                if not last or h < NH - 1:
                    transpose_p(b, h + 1, (r + 1) % GRP)
                if not last or h < NH - 3:
                    scores(b, h + 3, g if r == 0 else g + 1, marks)
                pe.wait_ge(s_olo, H + 1)
                for j in range(TT):
                    pe.wait_ge(s_ptlo, H * PTB + (PTB + (1, 2, 3, 3)[j]))
                    at, w = PT_AT[j], 512 - 128 * j
                    vs = bass.ds(g * HD, HD)
                    a = slice(at, at + w)
                    end = split_product(ps[:, 6 + r % 2, 128 * j:512], v_hi[:, j, vs], v_lo[:, j, vs],
                                        pt_hi[:, r % 2, a], pt_lo[:, r % 2, a], j == 0, j == TT - 1)
                end.then_inc(s_pv, 1)

            def attention(b, before=None):
                for h in range(2):
                    scores(b, h, 0)
                pe.wait_ge(s_vlo, b * TT + TT)
                if before is not None:
                    transposes(before * 2 + 2, hm_b)
                scores(b, 2, 0)
                transpose_p(b, 0, 0)
                first = 0
                if before is not None:
                    first = 1
                    logits(before, before * 2 + 2)
                    for r in range(GRP):
                        if r == 1:
                            pe.wait_ge(s_route, before * ROUTE + 1)
                        head(b, r, r, 0, False, before if r == 3 else None)
                with pe.Fori(first, NKV - 1) as g:
                    for r in range(GRP):
                        head(b, g * GRP + r, r, g)
                for r in range(GRP):
                    head(b, NH - GRP + r, r, NKV - 1, True)

            def logits(b, n):
                pe.wait_ge(s_trlo, n * KK + KK)
                for i in range(TT):
                    t = slice(i * 128, (i + 1) * 128)
                    for k in range(KK):
                        last = split_product(ps[:, 7, i * 16:i * 16 + E], hT_hi[:, k, t], hT_lo[:, k, t],
                                             gate_hi[:, k, :], gate_lo[:, k, :], k == 0, k == KK - 1)
                last.then_inc(s_lgmm, 1)

            def count(b):
                pe.wait_ge(s_route, b * ROUTE + ROUTE)
                for i in range(TT):
                    at = R_AT + i * 16
                    for j in range(i + 1):
                        nc.tensor.matmul(ps[:, 2, at:at + E], (upper if j == i else ones)[:, :], hot16[:, j, :],
                                         start=(j == 0), stop=(j == i), skip_group_check=True)
                at = R_AT + TT * 16
                for j in range(TT):
                    last = nc.tensor.matmul(ps[:, 2, at:at + E], ones[:, :], hot16[:, j, :],
                                            start=(j == 0), stop=(j == TT - 1), skip_group_check=True)
                last.then_inc(s_posmm, 1)

            def out_heads(b):
                pe.wait_ge(s_exp, b * (NH * TT) + (NH * TT + TT))
                for h in range(HEAD0):
                    project_out(b, h, h == 0)

            transposes(0, hm_a)
            pe.wait_ge(s_trlo, KK)
            pe.wait_ge(s_wlo, NPIECE)
            with pe.Fori(0, NQK // 4) as u:
                project(0, u)
            project_v(0)
            attention(0)
            with pe.Fori(0, B - 1) as b:
                out_heads(b)
                pe.wait_ge(s_olo, b * NH + (NH + SLOTS))
                transposes(b * 2 + 1, hm_a)
                with pe.Fori(0, NQK // 4) as u:
                    for r in range(2):
                        project_out(b, u * 2 + (HEAD0 + r))
                    pe.wait_ge(s_trlo, b * (2 * KK) + 2 * KK)
                    project(b + 1, u)
                project_v(b + 1)
                pe.wait_ge(s_opev, b + 1)
                attention(b + 1, b)
            out_heads(B - 1)
            for h in range(HEAD0, NH):
                project_out(B - 1, h)
            transposes(2 * B - 1, hm_b)
            logits(B - 1, 2 * B - 1)
            count(B - 1)

            pe.wait_ge(s_w2lo, NP2)
            pe.wait_ge(s_tab, TABSTEPS)

            def tile_step(u, r):
                for what, n, m, q in stages(u, r):
                    if what == "t1":
                        pe.wait_ge(s_ld[m], q * 16 + 16)
                        for k in range(KK):
                            last = nc.tensor.transpose(ps[:, m % 2, k * 128:(k + 1) * 128],
                                                       xt[:, m, k * 128:(k + 1) * 128], ident[:, :])
                        last.then_inc(s_t1, 1)
                    if what == "up":
                        e = pe.value_load(tab_e[0:1, bass.ds(n, 1)], min_val=0, max_val=NE - 1)
                        pe.wait_ge(s_t1lo, n + 1)
                        w = bass.ds(e * (2 * INTER), 2 * INTER)
                        for k in range(KK):
                            last = split_product(ps[:, 2 + m % 2, 0:2 * INTER], xT_hi[:, m % 2, k, :], xT_lo[:, m % 2, k, :],
                                                 w13_hi[:, k, w], w13_lo[:, k, w], k == 0, k == KK - 1)
                        last.then_inc(s_up, 1)
                    if what == "t2":
                        pe.wait_ge(s_hh, n + 1)
                        for k in range(2):
                            last = nc.tensor.transpose(ps[0:HI, 4 + m % 2, k * 128:(k + 1) * 128],
                                                       hh[:, m % 2, k * HI:(k + 1) * HI], ident[:, :])
                        last.then_inc(s_t2, 1)
                    if what == "dn":
                        e = pe.value_load(tab_e[0:1, bass.ds(n, 1)], min_val=0, max_val=NE - 1)
                        pe.wait_ge(s_t2lo, n + 1)
                        pe.wait_ge(s_ev, n + 1)
                        w = bass.ds(e * D, D)
                        for k in range(2):
                            last = split_product(ps[:, 6 + m % 2, 0:D], aT_hi[:, m % 2, k, :], aT_lo[:, m % 2, k, :],
                                                 w2_hi[:, k, w], w2_lo[:, k, w], k == 0, k == 1)
                        last.then_inc(s_dn, 1)

            run_tiles(pe, tile_step)


NT_ROUTED = 80
MODSTEPS = 15
TABSTEPS = 25


def _perm(w, heads):
    a = w.reshape(heads, 64, 2, w.shape[1])
    return a.transpose(0, 2, 1, 3).reshape(w.shape)


def kernel(**inputs):
    import numpy as np
    import concourse.bacc as bacc
    from concourse.bass_utils import run_bass_kernel_spmd as run

    g = {k: np.asarray(v) for k, v in inputs.items()}
    B, S, D = g["L0_attn_x"].shape
    E, INTER, _ = g["L0_ffn_w1"].shape
    NE, HI = E + 1, INTER // 2
    wqkv = np.concatenate([_perm(g["L0_attn_Wk"], 4), _perm(g["L0_attn_Wq"], 16), g["L0_attn_Wv"]], axis=0)
    w1 = np.concatenate([g["L0_ffn_w1"], g["L0_ffn_sw1"][None]], axis=0)
    w3 = np.concatenate([g["L0_ffn_w3"], g["L0_ffn_sw3"][None]], axis=0)
    w2 = np.concatenate([g["L0_ffn_w2"], g["L0_ffn_sw2"][None]], axis=0)
    w13_t = np.stack([w1, w3], axis=1).reshape(NE * 2 * INTER, D).T.reshape(D // 128, 128, NE * 2 * INTER)
    w2_t = w2.transpose(2, 0, 1).reshape(2, HI, NE * D)
    HD, WSCALE = 128, np.float32(16.0)
    freqs = np.float32(1.0) / np.float32(10000.0) ** (np.arange(0, HD, 2, dtype=np.float32) / np.float32(HD))
    angles = (np.arange(S, dtype=np.float32)[None, :] * freqs[:, None]).astype(np.float64)
    cos, sin = (np.cos(angles) / WSCALE).astype(np.float32), (np.sin(angles) / WSCALE).astype(np.float32)
    rope = np.stack([np.concatenate([cos, cos]), np.concatenate([-sin, sin])])
    region, nsh = B * S + 128, B * S // 128
    ar = np.arange
    tabc = np.concatenate([
        ar(NE) * region, ar(32) * 128, (ar(E)[:, None] >= ar(E)[None, :]).reshape(-1), ar(NT_ROUTED),
        np.full(nsh, E), E * region + 128 * ar(nsh)]).astype(np.float32)
    arrays = {
        "x": g["L0_attn_x"], "c_t": g["L0_c"].T, "wmod": g["L0_wmod"], "wqkv_t": wqkv.T,
        "wo_t": g["L0_attn_Wo"].T, "gate_t": g["L0_ffn_gate_w"].T, "w13_t": w13_t, "w2_t": w2_t,
        "rope": rope, "tabc": tabc,
    }
    arrays = {k: np.ascontiguousarray(v) for k, v in arrays.items()}
    nc = bacc.Bacc("TRN2", target_bir_lowering=False, num_devices=1)
    args = [nc.dram_tensor(k, v.shape, mybir.dt.from_np(v.dtype), kind="ExternalInput").ap() for k, v in arrays.items()]
    out = nc.dram_tensor("out", (B, S, D), mybir.dt.float32, kind="ExternalOutput").ap()
    adaln_moe_kernel(nc, *args, out)
    r = run(nc, [arrays], core_ids=[0])
    return r.results[0]["out"]
```

```python
import math
from contextlib import ExitStack

import concourse.bass as bass
from concourse import mybir


def adaln_moe_kernel(nc, x, c_t, wmod, wqkv_t, wo_t, gate_t, w13_t, w2_t, rope, tabc, tokc, out):
    fp32, f16, bf16, u32 = mybir.dt.float32, mybir.dt.float16, mybir.dt.bfloat16, mybir.dt.uint32
    ALU, ACT, AX = mybir.AluOpType, mybir.ActivationFunctionType, mybir.AxisListType

    B, S, D = x.shape
    TT = S // 128
    KK = D // 128
    HD = 128
    NKV = 4
    NH = 16
    GRP = NH // NKV
    NQK = NKV + NH
    NPROJ = (NQK + NKV) * HD
    VAT = NQK * HD
    E = gate_t.shape[1]
    NE = E + 1
    INTER = 176
    HI = INTER // 2
    T = B * S
    W = D + 4
    REG = T + 128
    SH0 = E * REG
    NSH = T // 128
    PAD0 = SH0 + T
    FAR = 1 << 20
    NRT = NT_ROUTED
    NT = NSH + NRT
    RSLOTS = 4
    STAGES = 4
    UNR = 8
    WSCALE = 16.0
    PSCALE = 1024.0
    SCALE = 1.0 / math.sqrt(HD)
    EPS = 1e-5
    NEG = -1e30
    PW = 1280
    P_AT = [0, 128, 384, 768]
    PT_AT = [0, 512, 1024, 896]

    ctx = ExitStack()
    with ctx:
        def sb(name, shape, dt, stack=ctx):
            return stack.enter_context(nc.sbuf_tensor(name, shape, dt))

        def sem(name):
            return ctx.enter_context(nc.semaphore(name))

        xs = sb("xs", [128, B * TT, D], fp32)
        tok = sb("tok", [128, B * TT], fp32)
        run = sb("run", [128, E], fp32)
        tc = sb("tc", [128, tabc.shape[0]], fp32)
        ident = sb("ident", [128, 128], fp32)
        carry = sb("carry", [128, 3], fp32)

        p1 = ExitStack()
        wqkv_hi = sb("wqkv_hi", [128, KK, NPROJ], f16, p1)
        wqkv_lo = sb("wqkv_lo", [128, KK, NPROJ], f16, p1)
        ropes = sb("ropes", [128, 2, S], fp32, p1)
        qsw = sb("qsw", [128, 2, S], fp32, p1)
        rt1 = sb("rt1", [128, RSLOTS, S], fp32, p1)
        rows_a = sb("rows_a", [128, 2, D], fp32, p1)
        hm_a = sb("hm_a", [128, TT, D], fp32, p1)
        v_hi = sb("v_hi", [128, TT, NKV * HD], f16, p1)
        v_lo = sb("v_lo", [128, TT, NKV * HD], f16, p1)
        pr = sb("pr", [128, GRP, PW], fp32, p1)
        pt_hi = sb("pt_hi", [128, 2, PW], f16, p1)
        pt_lo = sb("pt_lo", [128, 2, PW], f16, p1)
        qk_hi = sb("qk_hi", [128, NQK, S], f16, p1)
        qk_lo = sb("qk_lo", [128, NQK, S], f16, p1)
        wo_hi = sb("wo_hi", [128, NH, D], f16, p1)
        wo_lo = sb("wo_lo", [128, NH, D], f16, p1)
        hT_hi = sb("hT_hi", [128, KK, S], f16, p1)
        hT_lo = sb("hT_lo", [128, KK, S], f16, p1)
        gate_f = sb("gate_f", [128, KK, E], fp32, p1)
        gate_hi = sb("gate_hi", [128, KK, E], f16, p1)
        gate_lo = sb("gate_lo", [128, KK, E], f16, p1)
        xn = sb("xn", [128, TT, D], fp32, p1)
        rt2 = sb("rt2", [128, 2, S], fp32, p1)
        hc = rt2[:, :, :].rearrange("p a b -> p (a b)").rearrange("p (t d) -> p t d", d=D)
        rows_b = sb("rows_b", [128, 3, D], fp32, p1)
        ones = sb("ones", [128, 128], f16, p1)
        upper = sb("upper", [128, 128], f16, p1)
        maskb = sb("maskb", [128, 128], bf16, p1)
        identb = sb("identb", [128, 128], bf16, p1)
        bst = sb("bst", [128, TT, 6], fp32, p1)
        mv = sb("mv", [128, TT, 2], fp32, p1)
        rstd = sb("rstd", [128, TT], fp32, p1)
        vare = sb("vare", [128, TT], fp32, p1)
        cst = sb("cst", [128, 2, TT], fp32, p1)
        negm = sb("negm", [128, GRP, TT], fp32, p1)
        rsum = sb("rsum", [128, GRP, TT], fp32, p1)
        rinv = sb("rinv", [128, GRP, TT], fp32, p1)
        lg = sb("lg", [128, TT, 16], fp32, p1)
        ex = sb("ex", [128, TT, 16], fp32, p1)
        prob = sb("prob", [128, TT, 24], fp32, p1)
        rep = sb("rep", [128, 2, TT, 24], fp32, p1)
        mx8 = sb("mx8", [128, 2, TT, 8], fp32, p1)
        hot = sb("hot", [128, 3, TT, E], fp32, p1)
        hot16 = sb("hot16", [128, TT, E], f16, p1)
        posa = sb("posa", [128, 3, TT, E], fp32, p1)
        posf = sb("posf", [128, 2, TT], fp32, p1)
        wtp = sb("wtp", [128, 2, TT], fp32, p1)
        lsum = sb("lsum", [128, 3, TT], fp32, p1)
        cT = sb("cT", [128, KK, B], fp32, p1)
        cE = sb("cE", [128, KK, B], fp32, p1)
        siluT = sb("siluT", [128, KK, B], fp32, p1)
        hm_b = sb("hm_b", [128, TT, W], fp32, p1)
        idxs = sb("idxs", [128, 2, TT], u32, p1)
        p1.close()

        p2 = ExitStack()
        stage = sb("stage", [128, STAGES, NE * INTER], fp32, p2)
        w13_hi = sb("w13_hi", [128, KK, NE * 2 * INTER], f16, p2)
        w2_hi = sb("w2_hi", [HI, 2, NE * D], f16, p2)
        w13_lo = sb("w13_lo", [128, KK, NE * 2 * INTER], f16, p2)
        w2_lo = sb("w2_lo", [HI, 2, NE * D], f16, p2)
        xt = sb("xt", [128, UNR, W], fp32, p2)
        ys = sb("ys", [128, UNR, D], fp32, p2)
        gates = sb("gates", [128, B, D], fp32, p2)
        tcnt = sb("tcnt", [128, 5, E], fp32, p2)
        tcol = sb("tcol", [NRT, 6], fp32, p2)
        thot = sb("thot", [NRT, 2, E], fp32, p2)
        trow = sb("trow", [NRT, 128], fp32, p2)
        rowno = sb("rowno", [128, NRT], fp32, p2)
        tab_e = sb("tab_e", [1, NT], u32, p2)
        tab_r = sb("tab_r", [1, NT], u32, p2)
        runu = sb("runu", [1, NE], u32, p2)
        zrow = sb("zrow", [128, W], fp32, p2)
        xT_hi = sb("xT_hi", [128, 2, KK, 128], f16, p2)
        xT_lo = sb("xT_lo", [128, 2, KK, 128], f16, p2)
        sg = sb("sg", [128, 2, INTER], fp32, p2)
        second = sb("second", [128, UNR], fp32, p2)
        goal = sb("goal", [128, UNR], u32, p2)
        gain = sb("gain", [128, UNR], fp32, p2)
        hh = sb("hh", [128, 2, INTER], fp32, p2)
        aT_hi = sb("aT_hi", [HI, 2, 2, 128], f16, p2)
        aT_lo = sb("aT_lo", [HI, 2, 2, 128], f16, p2)
        p2.close()

        p3 = ExitStack()
        yk = sb("yk", [128, 4, 2, TT, D], fp32, p3)
        yo = sb("yo", [128, 2, TT, D], fp32, p3)
        p3.close()

        wst = [pr[:, :, :].rearrange("p a b -> p (a b)")[:, 6 * D:6 * D + NPROJ],
               xs[:, TT:TT + NPROJ // D, :].rearrange("p a b -> p (a b)")]
        wo_st = qk_hi[:, 0:16, :].rearrange("p a b -> p (a b)").bitcast(fp32)
        wmod_st = qk_lo[:, 0:12, :].rearrange("p a b -> p (a b)").bitcast(fp32)
        mrow = pr[0:B, :, :].rearrange("p a b -> p (a b)")[:, 0:6 * D]
        mneg = v_hi[0:B, :, :].rearrange("p a b -> p (a b)").bitcast(fp32)[:, 0:D]
        mabs = v_lo[0:B, :, :].rearrange("p a b -> p (a b)").bitcast(fp32)[:, 0:D]
        mneg2 = v_hi[0:B, :, :].rearrange("p a b -> p (a b)").bitcast(fp32)[:, D:2 * D]
        mabs2 = v_lo[0:B, :, :].rearrange("p a b -> p (a b)").bitcast(fp32)[:, D:2 * D]

        ps = ctx.enter_context(nc.psum_tensor("ps", [128, 8, 512], fp32))
        mscr = nc.dram_tensor("mod_rows", (B, 6 * D), fp32, kind="Internal").ap()
        hd = nc.dram_tensor("expert_in", (NE * REG, W), fp32, kind="Internal").ap()
        yd = nc.dram_tensor("results", (2 * T, D), fp32, kind="Internal").ap()

        c_loaded = sem("c_loaded")
        x0_loaded, x_loaded = sem("x0_loaded"), sem("x_loaded")
        wqkv_loaded, wo_loaded = sem("wqkv_loaded"), sem("wo_loaded")
        small_loaded = sem("small_loaded")
        consts_set = sem("consts_set")
        weights_hi_set, weights_lo_set = sem("weights_hi_set"), sem("weights_lo_set")
        c_exp, silu_step = sem("c_exp"), sem("silu_step")
        mod_product, mod_step = sem("mod_product"), sem("mod_step")
        mod_stored, rows_a_loaded = sem("mod_stored"), sem("rows_a_loaded")
        rows_b_loaded = sem("rows_b_loaded")
        stats_taken, mean_var = sem("stats_taken"), sem("mean_var")
        var_eps, rstd_set = sem("var_eps"), sem("rstd_set")
        xn_set = sem("xn_set")
        ln1_scaled, ln1_done = sem("ln1_scaled"), sem("ln1_done")
        ln2_scaled, ln2_done = sem("ln2_scaled"), sem("ln2_done")
        rows_transposed, rows_t_hi = sem("rows_transposed"), sem("rows_t_hi")
        rows_t_lo = sem("rows_t_lo")
        v_product, v_hi_set = sem("v_product"), sem("v_hi_set")
        v_lo_set = sem("v_lo_set")
        qk_product, qk_swapped = sem("qk_product"), sem("qk_swapped")
        cos_product = sem("cos_product")
        sin_product, qk_rotated = sem("sin_product"), sem("qk_rotated")
        qk_hi_set = sem("qk_hi_set")
        qk_lo_set = sem("qk_lo_set")
        scores_ready, max_ready = sem("scores_ready"), sem("max_ready")
        sum_inverted, probs_ready = sem("sum_inverted"), sem("probs_ready")
        exp_done = sem("exp_done")
        probs_transposed, probs_t_hi = sem("probs_transposed"), sem("probs_t_hi")
        probs_t_lo = sem("probs_t_lo")
        pv_product, head_hi_set = sem("pv_product"), sem("head_hi_set")
        head_lo_set = sem("head_lo_set")
        head_projected, out_gated = sem("head_projected"), sem("out_gated")
        x_updated = sem("x_updated")
        logits_ready, route_step = sem("logits_ready"), sem("route_step")
        logits_exp = sem("logits_exp")
        counts_ready, dest_rows_ready = sem("counts_ready"), sem("dest_rows_ready")
        running_counts = sem("running_counts")
        dest_step = sem("dest_step")
        row_scattered, shared_rows_stored = sem("row_scattered"), sem("shared_rows_stored")
        batch_sent = sem("batch_sent")
        piece_loaded = [sem(f"piece_loaded{k}") for k in range(STAGES)]
        piece_hi_set, piece_lo_set = sem("piece_hi_set"), sem("piece_lo_set")
        zero_rows_set, pads_stored = sem("zero_rows_set"), sem("pads_stored")
        table_step = sem("table_step")
        table_transposed = sem("table_transposed")
        tile_loaded = [sem(f"tile_loaded{r}") for r in range(UNR)]
        tile_transposed, tile_t_hi = sem("tile_transposed"), sem("tile_t_hi")
        tile_t_lo = sem("tile_t_lo")
        up_product, silu_gate = sem("up_product"), sem("silu_gate")
        act_ready = sem("act_ready")
        act_transposed, act_t_hi = sem("act_transposed"), sem("act_t_hi")
        act_t_lo = sem("act_t_lo")
        down_product = sem("down_product")
        result_evacuated = sem("result_evacuated")
        gates_loaded = sem("gates_loaded")
        shared_added = sem("shared_added")
        choice_told = sem("choice_told")
        goal_set = sem("goal_set")
        result_sent = [sem(f"result_sent{r}") for r in range(UNR)]
        send_begun = sem("send_begun")
        results_loaded = [sem(f"results_loaded{r}") for r in range(4)]
        choices_added, sum_gated = sem("choices_added"), sem("sum_gated")
        output_ready = sem("output_ready")
        output_stored = [sem("output_stored0"), sem("output_stored1")]

        SLOTS = 2
        QBANKS = 4
        PTB = 3
        HEAD0 = 6
        SPANS = ((0, NKV * HD, WSCALE), (NKV * HD, VAT, WSCALE * SCALE), (VAT, NPROJ, WSCALE))
        NPIECE = 3 * KK + 2
        ROUTE = 8
        PIECE = NE * INTER
        P2 = [(w13_hi[:, k, h * PIECE:(h + 1) * PIECE], w13_lo[:, k, h * PIECE:(h + 1) * PIECE], 128, PIECE)
              for k in range(KK) for h in range(2)]
        P2 += [(w2_hi[:, m, h * 2048:(h + 1) * 2048], w2_lo[:, m, h * 2048:(h + 1) * 2048], HI, 2048)
               for m in range(2) for h in range(2)]
        NP2 = len(P2)
        STRIPS = [3, 0, 2, 1]
        S_BANK = {3: (0, 0), 0: (1, 0), 2: (1, 128), 1: (2, 0)}
        E_DONE = {3: 1, 0: 3, 1: 4}
        R_AT = 384
        S_READY = {3: 1, 0: 2, 2: 2, 1: 3}
        M_READY = {3: 1, 0: 3, 2: 3, 1: 4}
        PT_BANK = [(3, 0), (4, 0), (5, 0), (4, 384)]
        PT_EVAC = [(3, 0, 512), (4, 512, 512), (5, 1024, 256)]
        C_E0, C_K, C_TRI, C_J, C_SE, C_SR = 0, 16, 48, 48 + E * E, 48 + E * E + NRT, 48 + E * E + NRT + NSH
        xd = x.rearrange("b (t p) d -> p (b t) d", p=128)
        od = out.rearrange("b (t p) d -> p (b t) d", p=128)
        hsh = hd[SH0:SH0 + T, 0:D].rearrange("(t p) d -> p t d", p=128)
        by_choice = yd.rearrange("(k t p) d -> p k t d", k=2, p=128)
        block = ctx.enter_context(nc.Block())

        def stages(u, r, routed=None):
            for what, d in (("t1", 2), ("up", 1), ("t2", 0), ("dn", -1)):
                n = u * UNR + (1 + r + d)
                if not isinstance(u, int):
                    yield what, n, (1 + r + d) % UNR, u + (1 + r + d) // UNR, routed
                elif 0 <= n < NT:
                    yield what, n, n % UNR, n // UNR, n >= NSH

        def run_tiles(eng, tile_step):
            for r in range(1, UNR):
                tile_step(-1, r)
            with eng.Fori(0, NSH // UNR - 1) as u:
                for r in range(UNR):
                    tile_step(u, r, False)
            for u in (NSH // UNR - 1, NSH // UNR):
                for r in range(UNR):
                    tile_step(u, r)
            with eng.Fori(NSH // UNR + 1, NT // UNR - 1) as u:
                for r in range(UNR):
                    tile_step(u, r, True)
            for r in range(UNR):
                tile_step(NT // UNR - 1, r)

        def pst1(m):
            return ps[:, m % 2, 0:KK * 128].rearrange("p (k t) -> p k t", k=KK)

        def pst2(m):
            return ps[0:HI, 4 + m % 2, 0:2 * 128].rearrange("p (k t) -> p k t", k=2)

        def carrier():
            nc.vector.tensor_copy(carry[:, 0:1], ident[:, 0:1])

        def pool_carrier(k=1):
            return nc.gpsimd.tensor_tensor(carry[:, k:k + 1], ident[:, 0:1], ident[:, 1:2], ALU.add)

        @block.sync
        def _(sp):
            sp.sem_inc(shared_rows_stored, 16)
            sp.dma_start(cT[:, :, :], c_t.rearrange("(k p) b -> p k b", p=128)).then_inc(c_loaded, 16)
            sp.dma_start(wmod_st.rearrange("p (k n) -> p k n", k=KK),
                         wmod.rearrange("(k p) n -> p k n", p=128)).then_inc(c_loaded, 16)
            sp.dma_start(xs[:, 0:TT, :], xd[:, 0:TT, :]).then_inc(x0_loaded, 16)
            for k in range(KK):
                sp.dma_start(wst[k], wqkv_t[k * 128:(k + 1) * 128, :]).then_inc(wqkv_loaded, 16)
            sp.dma_start(ropes[:, :, :], rope.rearrange("c p s -> p c s")).then_inc(small_loaded, 16)
            sp.dma_start(gate_f[:, :, :], gate_t.rearrange("(k p) e -> p k e", p=128)).then_inc(small_loaded, 16)
            sp.dma_start(tc[:, :], tabc.rearrange("(a n) -> a n", a=1).to_broadcast([128, tabc.shape[0]])).then_inc(small_loaded, 16)
            sp.dma_start(tok[:, :], tokc[:, :]).then_inc(small_loaded, 16)
            sp.dma_start(wo_st.rearrange("p (h d) -> p h d", h=NH),
                         wo_t.rearrange("(h p) d -> p h d", p=128)).then_inc(wo_loaded, 16)
            sp.wait_ge(mod_step, MODSTEPS)
            sp.dma_start(mscr[:, :], mrow).then_inc(mod_stored, 16)
            sp.wait_ge(mod_stored, 16)

            def mod_rows(dst, b, a, n, done):
                sp.dma_start(dst, mscr[bass.ds(b, 1), a * D:(a + n) * D].to_broadcast([128, n * D])).then_inc(done, 16)

            ra, rb = (t[:, :, :].rearrange("p a b -> p (a b)") for t in (rows_a, rows_b))
            mod_rows(ra, 0, 0, 2, rows_a_loaded)
            mod_rows(rb, 0, 2, 3, rows_b_loaded)
            sp.wait_ge(weights_lo_set, NPIECE)
            sp.dma_start(xs[:, TT:, :], xd[:, TT:, :]).then_inc(x_loaded, 16)
            sp.wait_ge(ln1_done, 1)
            mod_rows(ra, 1, 0, 2, rows_a_loaded)
            with sp.Fori(0, B - 2) as b:
                sp.wait_ge(ln1_done, b + 2)
                mod_rows(ra, b + 2, 0, 2, rows_a_loaded)
                sp.wait_ge(ln2_done, b + 1)
                mod_rows(rb, b + 1, 2, 3, rows_b_loaded)
                sp.dma_start(hsh[:, bass.ds(b * TT, TT), :], hm_b[:, :, 0:D]).then_inc(shared_rows_stored, 16)
            sp.wait_ge(ln2_done, B - 1)
            mod_rows(rb, B - 1, 2, 3, rows_b_loaded)
            sp.dma_start(hsh[:, (B - 2) * TT:(B - 1) * TT, :], hm_b[:, :, 0:D]).then_inc(shared_rows_stored, 16)

            def stage_piece(n):
                hi, lo, p, w = P2[n]
                src = w13_t[n // 2, :, (n % 2) * w:(n % 2 + 1) * w] if n < 2 * KK else \
                    w2_t[(n - 2 * KK) // 2, :, (n % 2) * w:(n % 2 + 1) * w]
                sp.dma_start(stage[0:p, n % STAGES, 0:w], src).then_inc(piece_loaded[n % STAGES], 16)

            sp.wait_ge(qk_lo_set, B * NQK + RSLOTS)
            sp.wait_ge(v_lo_set, B * TT)
            for n in range(STAGES - 1):
                stage_piece(n)
            sp.wait_ge(pv_product, B * NH)
            stage_piece(STAGES - 1)
            for n in range(STAGES, STAGES + 3):
                sp.wait_ge(piece_lo_set, n - STAGES + 1)
                stage_piece(n)
            sp.wait_ge(ln2_done, B)
            sp.dma_start(hsh[:, (B - 1) * TT:, :], hm_b[:, :, 0:D]).then_inc(shared_rows_stored, 16)
            for n in range(STAGES + 3, NP2):
                sp.wait_ge(piece_lo_set, n - STAGES + 1)
                stage_piece(n)
            sp.wait_ge(shared_rows_stored, 16 * (B + 1))
            sp.wait_ge(table_step, TABSTEPS)

            def load(j, r, w):
                at = sp.value_load(tab_r[0:1, bass.ds(j, 1)], min_val=0, max_val=PAD0)
                sp.dma_start(xt[:, r, 0:w], hd[bass.ds(at, 128), 0:w]).then_inc(tile_loaded[r], 16)

            for r in range(UNR):
                load(r, r, D)
            sp.dma_start(gates[:, :, :], mscr[:, 5 * D:6 * D].unsqueeze(0).to_broadcast([128, B, D])).then_inc(gates_loaded, 16)
            with sp.Fori(0, NSH // UNR - 1) as u:
                for r in range(UNR):
                    sp.wait_ge(tile_transposed, u * UNR + (r + 1))
                    load(u * UNR + (r + UNR), r, D)
            sp.wait_ge(pads_stored, 16 * NE)
            sp.wait_ge(batch_sent, B + 1)
            for r in range(UNR):
                sp.wait_ge(tile_transposed, NSH - UNR + r + 1)
                load(NSH + r, r, W)
            with sp.Fori(NSH // UNR, NT // UNR - 1) as u:
                for r in range(UNR):
                    sp.wait_ge(tile_transposed, u * UNR + (r + 1))
                    sp.wait_ge(goal_set, u * UNR + (r + 1))
                    load(u * UNR + (r + UNR), r, W)
            for r in range(UNR):
                sp.wait_ge(result_sent[r], 16 * (NRT // UNR))
            for b in range(B):
                if b >= 4:
                    sp.wait_ge(output_ready, b - 3)
                for k in range(2):
                    sp.dma_start(yk[:, b % 4, k, :, :], by_choice[:, k, b * TT:(b + 1) * TT, :]).then_inc(results_loaded[b % 4], 16)

        @block.gpsimd
        def _(pool):
            pool.sem_inc(sin_product, SLOTS)
            pool.sem_inc(batch_sent, 1)
            pool.sem_inc(send_begun, 1)
            nc.gpsimd.memset(ident[:, :], 0.0).then_inc(consts_set, 1)
            nc.gpsimd.memset(identb[:, :], 0.0).then_inc(consts_set, 1)
            nc.gpsimd.memset(maskb[:, :], 0.0).then_inc(consts_set, 1)
            nc.gpsimd.memset(cst[:, 0, :], EPS).then_inc(consts_set, 1)
            nc.gpsimd.memset(cst[:, 1, :], -0.5).then_inc(consts_set, 1)
            nc.gpsimd.memset(prob[:, :, :], -1.0).then_inc(consts_set, 1)
            nc.gpsimd.memset(mx8[:, :, :, :], -1.0).then_inc(consts_set, 1)
            nc.gpsimd.memset(ones[:, :], 1.0).then_inc(consts_set, 1)
            pool.wait_ge(consts_set, 8)
            for m in (ident, identb):
                nc.gpsimd.affine_select(out=m[:, :], in_=m[:, :], compare_op=ALU.not_equal, fill=1.0, base=0,
                                        pattern=[[-1, 128]], channel_multiplier=1).then_inc(consts_set, 1)
            nc.gpsimd.affine_select(out=maskb[:, :], in_=maskb[:, :], compare_op=ALU.is_ge, fill=NEG, base=0,
                                    pattern=[[-1, 128]], channel_multiplier=1).then_inc(consts_set, 1)
            nc.gpsimd.affine_select(out=upper[:, :], in_=ones[:, :], compare_op=ALU.is_gt, fill=0.0, base=0,
                                    pattern=[[1, 128]], channel_multiplier=-1).then_inc(consts_set, 1)

            def inverse_std(n):
                pool.wait_ge(mean_var, n + 1)
                nc.gpsimd.tensor_tensor(vare[:, :], mv[:, :, 1], cst[:, 0, :], ALU.add).then_inc(var_eps, 1)
                pool.wait_ge(var_eps, n + 1)
                nc.gpsimd.tensor_tensor(rstd[:, :], vare[:, :], cst[:, 1, :], ALU.pow).then_inc(rstd_set, 1)

            def modulate(b):
                pool.wait_ge(xn_set, b + 1)
                pool.wait_ge(rows_b_loaded, b * 16 + 16)
                nc.gpsimd.tensor_tensor(hc[:, :, :], xn[:, :, :], rows_b[:, 2:3, :].to_broadcast([128, TT, D]),
                                        ALU.mult).then_inc(ln2_scaled, 1)

            def modulate_rest(b):
                pool.wait_ge(ln2_scaled, b + 1)
                pool.wait_ge(shared_rows_stored, b * 16 + 16)
                pool.wait_ge(batch_sent, b + 1)
                nc.gpsimd.tensor_tensor(hm_b[:, :, 0:D], hc[:, :, :], rows_b[:, 1:2, :].to_broadcast([128, TT, D]),
                                        ALU.add).then_inc(ln2_done, 1)

            def rope_tile(b, n, r):
                pool.wait_ge(qk_swapped, n + (b * NQK + 1))
                pool.wait_ge(qk_rotated, n + (b * NQK + 1))
                nc.gpsimd.tensor_tensor(rt2[:, r, :], qsw[:, r, :], ropes[:, 1, :], ALU.mult).then_inc(sin_product, 1)

            def rope_tiles(b, std=None):
                with pool.Fori(0, NQK // 2 - 2) as u:
                    for r in range(2):
                        rope_tile(b, u * 2 + r, r)
                for t in range(NQK - 4, NQK):
                    rope_tile(b, t, t % 2)
                if std is not None:
                    inverse_std(std)

            def normalise(b, h, slot):
                for q, i in enumerate(STRIPS):
                    w = 128 * (i + 1)
                    p = pr[:, slot, P_AT[i]:P_AT[i] + w]
                    if q == 0:
                        pool.wait_ge(sum_inverted, h + (b * NH + 1))
                    last = nc.gpsimd.tensor_tensor(p, p, rinv[:, slot, i:i + 1].to_broadcast([128, w]), ALU.mult)
                last.then_inc(probs_ready, 1)

            def scatter(i):
                for k in range(2):
                    nc.gpsimd.indirect_dma_start(
                        out=hd[:, :], out_offset=bass.IndirectOffsetOnAxis(ap=idxs[:, k, i:i + 1], axis=0),
                        in_=hm_b[:, i, :], in_offset=None).then_inc(row_scattered, 16)

            def begin_scatter(b):
                pool.wait_ge(dest_rows_ready, b + 1)
                pool.wait_ge(ln2_done, b + 1)
                pool_carrier()

            def end_scatter(b):
                pool.wait_ge(row_scattered, b * (16 * 2 * TT) + 16 * 2 * TT)
                pool_carrier(2).then_inc(batch_sent, 1)

            def attention(b, before=None):
                first = 0
                if before is not None:
                    first = 1
                    for r in range(GRP):
                        normalise(b, r, r)
                        if r == 0:
                            modulate_rest(before)
                with pool.Fori(first, NKV - 1) as g:
                    for r in range(GRP):
                        normalise(b, g * GRP + r, r)
                for r in range(GRP):
                    normalise(b, NH - GRP + r, r)
                    if before is not None:
                        if r == 0:
                            begin_scatter(before)
                        scatter(r)

            pool.wait_ge(consts_set, 12)
            pool.wait_ge(small_loaded, 64)
            inverse_std(0)
            rope_tiles(0)
            attention(0)
            with pool.Fori(0, B - 1) as b:
                inverse_std(b * 2 + 1)
                rope_tiles(b + 1, b * 2 + 2)
                pool.wait_ge(qk_rotated, b * NQK + (2 * NQK + SLOTS))
                modulate(b)
                attention(b + 1, b)
                end_scatter(b)
            inverse_std(2 * B - 1)
            modulate(B - 1)
            modulate_rest(B - 1)
            begin_scatter(B - 1)
            for i in range(TT):
                scatter(i)
            end_scatter(B - 1)

            pool.wait_ge(shared_rows_stored, 16 * (B + 1))
            nc.gpsimd.memset(zrow[:, 0:D], 0.0).then_inc(zero_rows_set, 1)
            nc.gpsimd.memset(zrow[:, D:D + 1], -1.0).then_inc(zero_rows_set, 1)
            nc.gpsimd.memset(zrow[:, D + 1:D + 2], float(FAR)).then_inc(zero_rows_set, 1)
            nc.gpsimd.memset(zrow[:, D + 2:W], 0.0).then_inc(zero_rows_set, 1)
            pool.wait_ge(table_step, 2)
            pool.wait_ge(zero_rows_set, 4)
            with pool.Fori(0, NE) as e:
                at = pool.value_load(runu[0:1, bass.ds(e, 1)], min_val=0, max_val=PAD0)
                pool.dma_start(hd[bass.ds(at, 128), :], zrow[:, :]).then_inc(pads_stored, 16)
            with pool.Fori(0, NRT // UNR) as u:
                for r in range(UNR):
                    pool.wait_ge(result_evacuated, u * UNR + (NSH + r + 1 + SLOTS))
                    pool.wait_ge(send_begun, u * UNR + (r + 1))
                    pool_carrier().then_inc(send_begun, 1)
                    nc.gpsimd.indirect_dma_start(
                        out=yd[:, :], out_offset=bass.IndirectOffsetOnAxis(ap=goal[:, r:r + 1], axis=0),
                        in_=ys[:, r, :], in_offset=None, bounds_check=2 * T - 1,
                        oob_is_err=False).then_inc(result_sent[r], 16)

            for b in range(B):
                pool.wait_ge(results_loaded[b % 4], 32 * (b // 4 + 1))
                nc.gpsimd.tensor_tensor(yk[:, b % 4, 0, :, :], yk[:, b % 4, 0, :, :], yk[:, b % 4, 1, :, :],
                                        ALU.add).then_inc(choices_added, 1)

        @block.scalar
        def _(act):
            act.sem_inc(exp_done, TT)
            act.wait_ge(c_loaded, 32)
            nc.scalar.activation(cE[:, :, :], cT[:, :, :], ACT.Exp, scale=-1.0).then_inc(c_exp, 1)
            act.wait_ge(wqkv_loaded, 32)
            for k in range(KK):
                for a, b, f in SPANS:
                    nc.scalar.activation(wqkv_hi[:, k, a:b], wst[k][:, a:b], ACT.Copy,
                                         scale=f).then_inc(weights_hi_set, 1)
            act.wait_ge(wo_loaded, 16)
            nc.scalar.activation(wo_hi[:, :, :].rearrange("p a b -> p (a b)"), wo_st, ACT.Copy,
                                 scale=WSCALE).then_inc(weights_hi_set, 1)
            act.wait_ge(small_loaded, 64)
            nc.scalar.activation(gate_hi[:, :, :], gate_f[:, :, :], ACT.Copy, scale=WSCALE).then_inc(weights_hi_set, 1)

            def transposed_hi(n, bank):
                for k in range(KK):
                    act.wait_ge(rows_transposed, n * KK + (k + 1))
                    nc.scalar.copy(hT_hi[:, k, :], ps[:, bank + k, :]).then_inc(rows_t_hi, 1)

            def swap(b, n, bank, slot):
                act.wait_ge(qk_product, n + (b * NQK + 1))
                act.wait_ge(sin_product, n + (b * NQK + 1))
                nc.scalar.copy(qsw[0:64, slot, :], ps[64:128, bank, :])
                nc.scalar.copy(qsw[64:128, slot, :], ps[0:64, bank, :]).then_inc(qk_swapped, 1)

            def rot_hi(b, n, slot):
                act.wait_ge(qk_rotated, n + (b * NQK + 1 + SLOTS))
                nc.scalar.copy(qk_hi[:, n, :], rt1[:, slot, :]).then_inc(qk_hi_set, 1)

            def projections(b):
                swap(b, 0, 4, 0)
                swap(b, 1, 5, 1)
                with act.Fori(0, NQK // 4 - 1) as u:
                    for r in range(4):
                        swap(b, u * 4 + (r + 2), 4 + (r + 2) % 4, r % 2)
                        rot_hi(b, u * 4 + r, r)
                for n in range(NQK - 4, NQK):
                    if n + 2 < NQK:
                        swap(b, n + 2, 4 + (n + 2) % 4, n % 2)
                    rot_hi(b, n, n % RSLOTS)
                for m in range(TT):
                    act.wait_ge(v_product, b * TT + (m + 1))
                    nc.scalar.activation(v_hi[:, m, :], ps[:, 4 + m, :], ACT.Copy,
                                         scale=1.0 / WSCALE).then_inc(v_hi_set, 1)

            def exps(H, slot, strips=STRIPS):
                for i in strips:
                    bank, col = S_BANK[i]
                    w = 128 * (i + 1)
                    act.wait_ge(max_ready, H * TT + M_READY[i])
                    nc.scalar.activation(pr[:, slot, P_AT[i]:P_AT[i] + w], ps[:, bank, col:col + w], ACT.Exp,
                                         bias=negm[:, slot, i:i + 1],
                                         accum_out=rsum[:, slot, i:i + 1]).then_inc(exp_done, 1)

            def transposed_p(H, slot):
                for n, (bank, at, w) in enumerate(PT_EVAC):
                    act.wait_ge(probs_transposed, H * PTB + (n + 1))
                    nc.scalar.activation(pt_hi[:, slot, at:at + w], ps[:, bank, 0:w], ACT.Copy,
                                         scale=PSCALE).then_inc(probs_t_hi, 1)

            def head(b, h, r, last=False, logits=None):
                H = h + b * NH
                if not last or h < NH - 1:
                    transposed_p(H + 1, (r + 1) % 2)
                if logits is not None:
                    router_exps(logits)
                more = not last or h < NH - 3
                if more:
                    exps(H + 3, (r + 3) % GRP, STRIPS[:3])
                act.wait_ge(pv_product, H + 1)
                nc.scalar.activation(qk_hi[:, NKV + h, :], ps[:, 6 + r % 2, :], ACT.Copy,
                                     scale=1.0 / PSCALE).then_inc(head_hi_set, 1)
                if more:
                    exps(H + 3, (r + 3) % GRP, STRIPS[3:])

            def router_exps(b):
                act.wait_ge(route_step, b * ROUTE + 2)
                for i in range(TT):
                    nc.scalar.activation(ex[:, i, 0:E], lg[:, i, 0:E], ACT.Exp, bias=lsum[:, 0, i:i + 1],
                                         accum_out=lsum[:, 1, i:i + 1]).then_inc(logits_exp, 1)

            def attention(b, before=None):
                exps(b * NH, 0)
                exps(b * NH + 1, 1)
                exps(b * NH + 2, 2)
                transposed_p(b * NH, 0)
                first = 0
                if before is not None:
                    transposed_hi(before * 2 + 2, 6)
                    first = 1
                    for r in range(GRP):
                        head(b, r, r, False, before if r == 1 else None)
                with act.Fori(first, NKV - 1) as g:
                    for r in range(GRP):
                        head(b, g * GRP + r, r)
                for r in range(GRP):
                    head(b, NH - GRP + r, r, True)

            transposed_hi(0, 6)
            projections(0)
            attention(0)
            with act.Fori(0, B - 1) as b:
                transposed_hi(b * 2 + 1, 6)
                projections(b + 1)
                attention(b + 1, b)

            def weights_hi(n):
                hi, lo, p, w = P2[n]
                act.wait_ge(piece_loaded[n % STAGES], 16 * (n // STAGES + 1))
                nc.scalar.activation(hi, stage[0:p, n % STAGES, 0:w], ACT.Copy, scale=WSCALE).then_inc(piece_hi_set, 1)

            for n in range(STAGES):
                weights_hi(n)
            transposed_hi(2 * B - 1, 6)
            router_exps(B - 1)
            for n in range(STAGES, NP2):
                weights_hi(n)

            def tile_step(u, r, routed=None):
                for what, n, m, q, home in stages(u, r, routed):
                    if what == "t1":
                        act.wait_ge(tile_transposed, n + 1)
                        nc.scalar.copy(xT_hi[:, m % 2, :, :], pst1(m)).then_inc(tile_t_hi, 1)
                    if what == "up":
                        act.wait_ge(up_product, n + 1)
                        nc.scalar.activation(sg[:, m % 2, :], ps[:, 2 + m % 2, 0:INTER], ACT.Silu,
                                             scale=1.0 / WSCALE).then_inc(silu_gate, 1)
                    if what == "t2":
                        act.wait_ge(act_transposed, n + 1)
                        nc.scalar.copy(aT_hi[:, m % 2, :, :], pst2(m)).then_inc(act_t_hi, 1)

            run_tiles(act, tile_step)

            for b in range(B):
                act.wait_ge(output_ready, b + 1)
                act.dma_start(od[:, b * TT:(b + 1) * TT, :], yo[:, b % 2, :, :]).then_inc(output_stored[b % 2], 16)
            for r in range(2):
                act.wait_ge(output_stored[r], 16 * (B // 2))

        @block.vector
        def _(dve):
            dve.sem_inc(qk_rotated, SLOTS)
            dve.sem_inc(head_lo_set, SLOTS)
            dve.sem_inc(result_evacuated, SLOTS)
            dve.sem_inc(shared_added, UNR)
            dve.sem_inc(cos_product, QBANKS)
            dve.sem_inc(probs_t_lo, PTB)
            dve.sem_inc(goal_set, NSH)
            dve.sem_inc(qk_lo_set, RSLOTS)
            dve.wait_ge(consts_set, 12)

            dve.wait_ge(c_exp, 1)
            nc.vector.tensor_scalar(siluT[:, :, :], cE[:, :, :], 1.0, None, ALU.add).then_inc(silu_step, 1)
            dve.wait_ge(silu_step, 1)
            nc.vector.reciprocal(cE[:, :, :], siluT[:, :, :]).then_inc(silu_step, 1)
            dve.wait_ge(silu_step, 2)
            nc.vector.tensor_tensor(siluT[:, :, :], cE[:, :, :], cT[:, :, :], ALU.mult).then_inc(silu_step, 1)

            def statistics(n, t):
                carrier()
                for i in range(TT):
                    last = nc.vector.bn_stats(bst[:, i, :], xs[:, t + i, :])
                last.then_inc(stats_taken, 1)
                dve.wait_ge(stats_taken, n + 1)
                carrier()
                for i in range(TT):
                    last = nc.vector.bn_aggr(mv[:, i, :], bst[:, i, :])
                last.then_inc(mean_var, 1)

            def modulate_first(n, t, b):
                dve.wait_ge(mean_var, n + 1)
                dve.wait_ge(rows_a_loaded, b * 16 + 16)
                for i in range(TT):
                    last = nc.vector.scalar_tensor_tensor(xn[:, i, :], xs[:, t + i, :], mv[:, i, 0:1], rows_a[:, 1, :],
                                                          ALU.subtract, ALU.mult)
                last.then_inc(ln1_scaled, 1)
                dve.wait_ge(ln1_scaled, b + 1)
                dve.wait_ge(rstd_set, n + 1)
                for i in range(TT):
                    last = nc.vector.scalar_tensor_tensor(hm_a[:, i, :], xn[:, i, :], rstd[:, i:i + 1], rows_a[:, 0, :],
                                                          ALU.mult, ALU.add)
                last.then_inc(ln1_done, 1)

            def normalise(n, t, b):
                dve.wait_ge(mean_var, n + 1)
                dve.wait_ge(rstd_set, n + 1)
                for i in range(TT):
                    last = nc.vector.tensor_scalar(xn[:, i, :], xs[:, t + i, :], mv[:, i, 0:1], rstd[:, i:i + 1],
                                                   ALU.subtract, ALU.mult)
                last.then_inc(xn_set, 1)

            dve.wait_ge(x0_loaded, 16)
            statistics(0, 0)

            dve.wait_ge(mod_product, 1)
            nc.vector.tensor_copy(mrow, ps[0:B, 5:8, :].rearrange("p a b -> p (a b)")).then_inc(mod_step, 1)
            dve.wait_ge(mod_step, 1)
            for a in (1, 4):
                m = mrow[:, a * D:(a + 1) * D]
                nc.vector.tensor_scalar(m, m, 1.0, None, ALU.add).then_inc(mod_step, 1)
            for j, (a, neg, ab) in enumerate(((2, mneg, mabs), (5, mneg2, mabs2))):
                m = mrow[:, a * D:(a + 1) * D]
                nc.vector.tensor_scalar(neg, m, -1.0, None, ALU.mult).then_inc(mod_step, 1)
                dve.wait_ge(mod_step, 4 + 6 * j)
                nc.vector.tensor_tensor(ab, m, neg, ALU.max).then_inc(mod_step, 1)
                dve.wait_ge(mod_step, 5 + 6 * j)
                nc.vector.tensor_scalar(neg, m, 0.0, 2.0, ALU.is_ge, ALU.mult).then_inc(mod_step, 1)
                nc.vector.tensor_scalar(ab, ab, 0.25, None, ALU.max).then_inc(mod_step, 1)
                dve.wait_ge(mod_step, 7 + 6 * j)
                nc.vector.tensor_scalar(neg, neg, 1.0, None, ALU.subtract).then_inc(mod_step, 1)
                dve.wait_ge(mod_step, 8 + 6 * j)
                nc.vector.tensor_tensor(m, neg, ab, ALU.mult).then_inc(mod_step, 1)

            n = 0
            for k in range(KK):
                for a, b, f in SPANS:
                    n += 1
                    dve.wait_ge(weights_hi_set, n)
                    nc.vector.scalar_tensor_tensor(wqkv_lo[:, k, a:b], wst[k][:, a:b], f,
                                                   wqkv_hi[:, k, a:b], ALU.mult, ALU.subtract).then_inc(weights_lo_set, 1)

            def other_weights_lo():
                dve.wait_ge(weights_hi_set, n + 1)
                nc.vector.scalar_tensor_tensor(wo_lo[:, :, :].rearrange("p a b -> p (a b)"), wo_st, WSCALE,
                                               wo_hi[:, :, :].rearrange("p a b -> p (a b)"),
                                               ALU.mult, ALU.subtract).then_inc(weights_lo_set, 1)
                dve.wait_ge(weights_hi_set, n + 2)
                nc.vector.scalar_tensor_tensor(gate_lo[:, :, :], gate_f[:, :, :], WSCALE, gate_hi[:, :, :],
                                               ALU.mult, ALU.subtract).then_inc(weights_lo_set, 1)
                dve.wait_ge(weights_lo_set, NPIECE)
                dve.wait_ge(small_loaded, 64)
                nc.vector.tensor_copy(run[:, :], tc[:, C_E0:C_E0 + E]).then_inc(running_counts, 1)

            def transposed_lo(n, bank):
                for k in range(KK):
                    dve.wait_ge(rows_t_hi, n * KK + (k + 1))
                    nc.vector.tensor_tensor(hT_lo[:, k, :], ps[:, bank + k, :], hT_hi[:, k, :],
                                            ALU.subtract).then_inc(rows_t_lo, 1)

            def rot_cos(b, n, bank, slot):
                dve.wait_ge(qk_swapped, n + (b * NQK + 1))
                dve.wait_ge(qk_lo_set, n + (b * NQK + 1))
                nc.vector.tensor_tensor(rt1[:, slot, :], ps[:, bank, :], ropes[:, 0, :],
                                        ALU.mult).then_inc(cos_product, 1)

            def rot_sum(b, n, slot):
                dve.wait_ge(cos_product, n + (b * NQK + 1 + QBANKS))
                dve.wait_ge(sin_product, n + (b * NQK + 1 + SLOTS))
                nc.vector.tensor_tensor(rt1[:, slot, :], rt1[:, slot, :], rt2[:, slot % 2, :],
                                        ALU.add).then_inc(qk_rotated, 1)

            def rot_lo(b, n, slot):
                dve.wait_ge(qk_hi_set, n + (b * NQK + 1))
                nc.vector.tensor_tensor(qk_lo[:, n, :], rt1[:, slot, :], qk_hi[:, n, :],
                                        ALU.subtract).then_inc(qk_lo_set, 1)

            def projections(b, residual_of=None):
                rot_cos(b, 0, 4, 0)
                rot_cos(b, 1, 5, 1)
                rot_sum(b, 0, 0)
                rot_cos(b, 2, 6, 2)
                rot_sum(b, 1, 1)
                with dve.Fori(0, NQK // 4 - 1) as u:
                    for r in range(4):
                        rot_lo(b, u * 4 + r, r)
                        rot_cos(b, u * 4 + (r + 3), 4 + (r + 3) % 4, (r + 3) % 4)
                        rot_sum(b, u * 4 + (r + 2), (r + 2) % 4)
                for n in range(NQK - 3, NQK + 1):
                    rot_lo(b, n - 1, (n - 1) % 4)
                    if n + 2 < NQK:
                        rot_cos(b, n + 2, 4 + (n + 2) % 4, (n + 2) % 4)
                    if n + 1 < NQK:
                        rot_sum(b, n + 1, (n + 1) % 4)
                    if residual_of is not None and n == NQK - 3:
                        residual(residual_of)

            def values_lo(b, tiles):
                for m in tiles:
                    dve.wait_ge(v_hi_set, b * TT + (m + 1))
                    nc.vector.scalar_tensor_tensor(v_lo[:, m, :], ps[:, 4 + m, :], 1.0 / WSCALE, v_hi[:, m, :],
                                                   ALU.mult, ALU.subtract).then_inc(v_lo_set, 1)

            def maxima(H, slot, strips=STRIPS, rows_of=None):
                for i in strips:
                    bank, col = S_BANK[i]
                    dve.wait_ge(scores_ready, H * 3 + S_READY[i])
                    if rows_of is not None and i == 1:
                        expert_rows(rows_of)
                    nc.vector.tensor_reduce(negm[:, slot, i:i + 1], ps[:, bank, col:col + 128 * (i + 1)], AX.X,
                                            ALU.max, negate=True).then_inc(max_ready, 1)

            def inverse(H, slot):
                dve.wait_ge(exp_done, H * TT + 2 * TT)
                nc.vector.reciprocal(rinv[:, slot, :], rsum[:, slot, :]).then_inc(sum_inverted, 1)

            def transposed_p(H, slot, parts=range(PTB)):
                for n in parts:
                    bank, at, w = PT_EVAC[n]
                    dve.wait_ge(probs_t_hi, H * PTB + (n + 1))
                    nc.vector.scalar_tensor_tensor(pt_lo[:, slot, at:at + w], ps[:, bank, 0:w], PSCALE,
                                                   pt_hi[:, slot, at:at + w], ALU.mult, ALU.subtract).then_inc(probs_t_lo, 1)

            def head(b, h, r, last=False, rows_of=None):
                H = h + b * NH
                after, more = not last or h < NH - 1, not last or h < NH - 3
                if more:
                    maxima(H + 3, (r + 3) % GRP, STRIPS[:3])
                if after:
                    transposed_p(H + 1, (r + 1) % 2, (0, 1))
                if more:
                    maxima(H + 3, (r + 3) % GRP, STRIPS[3:], rows_of)
                if after:
                    transposed_p(H + 1, (r + 1) % 2, (2,))
                if more:
                    inverse(H + 3, (r + 3) % GRP)
                dve.wait_ge(head_hi_set, H + 1)
                nc.vector.scalar_tensor_tensor(qk_lo[:, NKV + h, :], ps[:, 6 + r % 2, :], 1.0 / PSCALE,
                                               qk_hi[:, NKV + h, :], ALU.mult, ALU.subtract).then_inc(head_lo_set, 1)

            def attention(b, before=None):
                if before is not None:
                    statistics(before * 2 + 2, before * TT)
                maxima(b * NH, 0)
                if before is not None:
                    normalise(before * 2 + 2, before * TT, before)
                inverse(b * NH, 0)
                values_lo(b, (0, 1))
                maxima(b * NH + 1, 1)
                values_lo(b, (2, 3))
                inverse(b * NH + 1, 1)
                maxima(b * NH + 2, 2)
                inverse(b * NH + 2, 2)
                transposed_p(b * NH, 0)
                first = 0
                if before is not None:
                    transposed_lo(before * 2 + 2, 6)
                    first = 1
                    for r, part in enumerate((router_logits, router_choice, router_marks, router_rows)):
                        head(b, r, r, False, before if r == 3 else None)
                        part(before)
                with dve.Fori(first, NKV - 1) as g:
                    for r in range(GRP):
                        head(b, g * GRP + r, r)
                for r in range(GRP):
                    head(b, NH - GRP + r, r, True)

            def residual(b):
                dve.wait_ge(head_projected, b * NH + NH)
                dve.wait_ge(rows_b_loaded, b * 16 + 16)
                nc.vector.scalar_tensor_tensor(xn[:, :, :], ps[:, 0:TT, 0:D], 1.0 / WSCALE,
                                               rows_b[:, 0:1, :].to_broadcast([128, TT, D]),
                                               ALU.mult, ALU.mult).then_inc(out_gated, 1)
                dve.wait_ge(out_gated, b + 1)
                nc.vector.tensor_tensor(xs[:, bass.ds(b * TT, TT), :], xs[:, bass.ds(b * TT, TT), :], xn[:, :, :],
                                        ALU.add).then_inc(x_updated, 1)
                dve.wait_ge(x_updated, b + 1)

            def router_logits(b):
                dve.wait_ge(logits_ready, b + 1)
                nc.vector.tensor_scalar(lg[:, :, 0:E], ps[:, 7, 0:TT * 16].rearrange("p (t e) -> p t e", e=16)[:, :, 0:E],
                                        1.0 / WSCALE, None, ALU.mult).then_inc(route_step, 1)
                dve.wait_ge(route_step, b * ROUTE + 1)
                nc.vector.tensor_reduce(lsum[:, 0, :], lg[:, :, 0:E], AX.X, ALU.max, negate=True).then_inc(route_step, 1)

            def router_choice(b):
                dve.wait_ge(logits_exp, b * TT + TT)
                nc.vector.reciprocal(lsum[:, 2, :], lsum[:, 1, :]).then_inc(route_step, 1)
                dve.wait_ge(route_step, b * ROUTE + 3)
                for i in range(TT):
                    last = nc.vector.tensor_scalar(prob[:, i, 0:E], ex[:, i, 0:E], lsum[:, 2, i:i + 1], None, ALU.mult)
                last.then_inc(route_step, 1)
                dve.wait_ge(route_step, b * ROUTE + 4)
                carrier()
                for i in range(TT):
                    last = nc.vector.max(rep[:, 0, i, 0:8], prob[:, i, 0:E])
                last.then_inc(route_step, 1)
                dve.wait_ge(route_step, b * ROUTE + 5)
                nc.vector.tensor_copy(mx8[:, 0, :, 0:1], rep[:, 0, :, 0:1])
                nc.vector.tensor_copy(mx8[:, 1, :, 0:2], rep[:, 0, :, 0:2])
                nc.vector.tensor_copy(wtp[:, :, :], rep[:, 0, :, 0:2].rearrange("p t k -> p k t")).then_inc(route_step, 1)

            def router_marks(b):
                dve.wait_ge(route_step, b * ROUTE + 6)
                carrier()
                for k in range(2):
                    for i in range(TT):
                        last = nc.vector.match_replace(out=rep[:, k, i, 0:22], in_to_replace=mx8[:, k, i, :],
                                                       in_values=prob[:, i, 0:22], imm_value=-2.0)
                last.then_inc(route_step, 1)
                dve.wait_ge(route_step, b * ROUTE + 7)
                nc.vector.tensor_scalar(hot[:, 1:3, :, :].rearrange("p k t e -> p (k t) e"),
                                        rep[:, :, :, 0:E].rearrange("p k t e -> p (k t) e"), -2.0, None, ALU.is_equal)
                nc.vector.tensor_scalar(hot16[:, :, :], rep[:, 1, :, 0:E], -2.0, None, ALU.is_equal).then_inc(route_step, 1)
                dve.wait_ge(route_step, b * ROUTE + 8)
                nc.vector.tensor_tensor(hot[:, 0, :, :], hot[:, 2, :, :], hot[:, 1, :, :], ALU.subtract).then_inc(dest_step, 1)

            def expert_rows(b):
                dve.wait_ge(counts_ready, b + 1)
                dve.wait_ge(running_counts, b + 1)
                nc.vector.tensor_tensor(posa[:, 2, :, :], ps[:, 2, R_AT:R_AT + TT * 16].rearrange("p (t e) -> p t e", e=16)[:, :, 0:E],
                                        run[:, :].unsqueeze(1).to_broadcast([128, TT, E]), ALU.add).then_inc(dest_step, 1)
                dve.wait_ge(dest_step, b * 5 + 2)
                nc.vector.tensor_tensor(run[:, :], run[:, :], ps[:, 2, R_AT + TT * 16:R_AT + TT * 16 + E], ALU.add).then_inc(running_counts, 1)

            def router_rows(b):
                nc.vector.tensor_tensor(posa[:, 0, :, :], posa[:, 2, :, :], hot[:, 1, :, :], ALU.mult).then_inc(dest_step, 1)
                nc.vector.tensor_tensor(posa[:, 1, :, :], posa[:, 2, :, :], hot[:, 0, :, :], ALU.mult).then_inc(dest_step, 1)
                dve.wait_ge(dest_step, b * 5 + 4)
                nc.vector.tensor_reduce(posf[:, :, :], posa[:, 0:2, :, :], AX.X, ALU.add).then_inc(dest_step, 1)
                dve.wait_ge(dest_step, b * 5 + 5)
                dve.wait_ge(batch_sent, b + 1)
                nc.vector.tensor_copy(hm_b[:, :, D], posf[:, 1, :])
                nc.vector.tensor_copy(hm_b[:, :, D + 1], tok[:, bass.ds(b * TT, TT)])
                nc.vector.tensor_copy(hm_b[:, :, D + 2], wtp[:, 0, :])
                nc.vector.tensor_tensor(hm_b[:, :, D + 3], wtp[:, 1, :], wtp[:, 0, :], ALU.subtract)
                nc.vector.tensor_copy(idxs[:, :, :], posf[:, :, :]).then_inc(dest_rows_ready, 1)

            modulate_first(0, 0, 0)
            transposed_lo(0, 6)
            other_weights_lo()
            projections(0)
            attention(0)
            dve.wait_ge(x_loaded, 16)
            with dve.Fori(0, B - 1) as b:
                statistics(b * 2 + 1, b * TT + TT)
                modulate_first(b * 2 + 1, b * TT + TT, b + 1)
                transposed_lo(b * 2 + 1, 6)
                projections(b + 1, b)
                attention(b + 1, b)

            def weights_lo(n):
                hi, lo, p, w = P2[n]
                dve.wait_ge(piece_hi_set, n + 1)
                nc.vector.scalar_tensor_tensor(lo, stage[0:p, n % STAGES, 0:w], WSCALE, hi, ALU.mult,
                                               ALU.subtract).then_inc(piece_lo_set, 1)

            residual(B - 1)
            statistics(2 * B - 1, (B - 1) * TT)
            normalise(2 * B - 1, (B - 1) * TT, B - 1)
            weights_lo(0)
            weights_lo(1)
            weights_lo(2)
            transposed_lo(2 * B - 1, 6)
            router_logits(B - 1)
            weights_lo(3)
            router_choice(B - 1)
            router_marks(B - 1)
            expert_rows(B - 1)
            router_rows(B - 1)
            dve.wait_ge(running_counts, B + 1)

            step = [0]

            def then(ins):
                step[0] += 1
                ins.then_inc(table_step, 1)
                dve.wait_ge(table_step, step[0])

            def row(t, shape, axis=None):
                return t.unsqueeze(axis).to_broadcast(shape)

            c0 = lambda at, n: tc[0:1, at:at + n]
            call = lambda at, n: tc[:, at:at + n]
            tcb = ys[:, 0:2, :].rearrange("p a b -> p (a b)")
            cnt, tiles, cum, off, base = (tcnt[:, k, :] for k in range(5))
            then(nc.vector.tensor_copy(runu[:, 0:E], run[0:1, :]))
            then(nc.vector.tensor_scalar(runu[:, E:NE], c0(C_E0 + E, 1), float(T), None, ALU.add))
            then(nc.vector.tensor_tensor(cnt, run[:, :], call(C_E0, E), ALU.subtract))
            m = tcb[:, 0:E * 32].rearrange("p (e k) -> p e k", k=32)
            then(nc.vector.tensor_tensor(m, row(cnt, [128, E, 32], 2), row(call(C_K, 32), [128, E, 32], 1), ALU.is_gt))
            then(nc.vector.tensor_reduce(tiles, m, AX.X, ALU.add))
            m = tcb[:, 0:E * E].rearrange("p (e k) -> p e k", k=E)
            then(nc.vector.tensor_tensor(m, row(tiles, [128, E, E], 1), call(C_TRI, E * E).rearrange("p (e k) -> p e k", k=E),
                                         ALU.mult))
            then(nc.vector.tensor_reduce(cum, m, AX.X, ALU.add))
            then(nc.vector.tensor_tensor(off, cum, tiles, ALU.subtract))
            then(nc.vector.scalar_tensor_tensor(base, off, -128.0, call(C_E0, E), ALU.mult, ALU.add))
            hot0, hot1 = thot[:, 0, :], thot[:, 1, :]
            col = [tcol[:, k:k + 1] for k in range(6)]
            then(nc.vector.tensor_scalar(hot0, cum[0:NRT, :], tok[0:NRT, 0:1], None, ALU.is_le))
            then(nc.vector.tensor_reduce(col[0], hot0, AX.X, ALU.add))
            then(nc.vector.tensor_scalar(hot0, tc[0:NRT, C_J:C_J + E], col[0], None, ALU.is_equal))
            then(nc.vector.tensor_tensor(hot1, hot0, base[0:NRT, :], ALU.mult))
            then(nc.vector.tensor_reduce(col[2], hot1, AX.X, ALU.add))
            then(nc.vector.tensor_scalar(col[3], col[0], float(E), None, ALU.is_lt))
            then(nc.vector.tensor_scalar(col[4], tok[0:NRT, 0:1], 128.0, -float(PAD0), ALU.mult, ALU.add))
            then(nc.vector.tensor_tensor(col[5], col[4], col[3], ALU.mult))
            then(nc.vector.scalar_tensor_tensor(col[1], col[2], float(PAD0), col[5], ALU.add, ALU.add))
            then(nc.vector.tensor_copy(trow[:, :], col[1].to_broadcast([NRT, 128])))
            dve.wait_ge(table_transposed, 1)
            then(nc.vector.tensor_copy(tab_e[:, NSH:], ps[0:1, 3, 0:NRT]))
            then(nc.vector.tensor_copy(tab_r[:, NSH:], ps[0:1, 3, 128:128 + NRT]))
            then(nc.vector.tensor_copy(tab_e[:, 0:NSH], c0(C_SE, NSH)))
            then(nc.vector.tensor_copy(tab_r[:, 0:NSH], c0(C_SR, NSH)))
            then(nc.vector.tensor_scalar(rowno[:, :], ps[:, 3, 256:256 + NRT], tok[:, 0:1], None, ALU.add))
            assert step[0] == TABSTEPS

            for n in range(STAGES, NP2):
                weights_lo(n)

            def tile_step(u, r, routed=None):
                for what, n, m, q, home in stages(u, r, routed):
                    if what == "t1":
                        dve.wait_ge(tile_t_hi, n + 1)
                        nc.vector.tensor_tensor(xT_lo[:, m % 2, :, :], pst1(m), xT_hi[:, m % 2, :, :],
                                                ALU.subtract).then_inc(tile_t_lo, 1)
                        if home:
                            j = n - NSH
                            nc.vector.tensor_tensor(second[:, m:m + 1], xt[:, m, D:D + 1], rowno[:, bass.ds(j, 1)],
                                                    ALU.is_equal).then_inc(choice_told, 1)
                            dve.wait_ge(choice_told, j + 1)
                            if not isinstance(n, int) or n >= NSH + UNR:
                                dve.wait_ge(result_sent[m], (q - NSH // UNR) * 16)
                            nc.vector.scalar_tensor_tensor(goal[:, m:m + 1], second[:, m:m + 1], float(T),
                                                           xt[:, m, D + 1:D + 2], ALU.mult, ALU.add)
                            nc.vector.scalar_tensor_tensor(gain[:, m:m + 1], second[:, m:m + 1], xt[:, m, D + 3:D + 4],
                                                           xt[:, m, D + 2:D + 3], ALU.mult, ALU.add).then_inc(goal_set, 1)
                    if what == "up":
                        dve.wait_ge(silu_gate, n + 1)
                        nc.vector.scalar_tensor_tensor(hh[:, m % 2, :], ps[:, 2 + m % 2, INTER:2 * INTER], 1.0 / WSCALE,
                                                       sg[:, m % 2, :], ALU.mult, ALU.mult).then_inc(act_ready, 1)
                    if what == "t2":
                        dve.wait_ge(act_t_hi, n + 1)
                        nc.vector.tensor_tensor(aT_lo[:, m % 2, :, :], pst2(m), aT_hi[:, m % 2, :, :],
                                                ALU.subtract).then_inc(act_t_lo, 1)
                    if what == "dn":
                        dve.wait_ge(down_product, n + 1)
                        if not home:
                            dve.wait_ge(shared_added, n + 1)
                            nc.vector.scalar_tensor_tensor(ys[:, m, :], ps[:, 6 + m % 2, 0:D], 1.0 / WSCALE,
                                                           gates[:, bass.ds(q * (UNR // TT) + m // TT, 1), :].squeeze(1),
                                                           ALU.mult, ALU.mult).then_inc(result_evacuated, 1)
                            dve.wait_ge(result_evacuated, n + (1 + SLOTS))
                            x_tile = xs[:, bass.ds(n, 1), :].squeeze(1)
                            nc.vector.tensor_tensor(x_tile, x_tile, ys[:, m, :], ALU.add).then_inc(shared_added, 1)
                            continue
                        if isinstance(n, int) and n < NSH + UNR:
                            dve.wait_ge(shared_added, NSH + UNR)
                        else:
                            dve.wait_ge(result_sent[m], (q - NSH // UNR) * 16)
                        nc.vector.tensor_scalar(ys[:, m, :], ps[:, 6 + m % 2, 0:D], gain[:, m:m + 1], 1.0 / WSCALE,
                                                ALU.mult, ALU.mult).then_inc(result_evacuated, 1)

            dve.wait_ge(gates_loaded, 16)
            run_tiles(dve, tile_step)

            for b in range(B):
                dve.wait_ge(choices_added, b + 1)
                total = yk[:, b % 4, 0, :, :]
                nc.vector.tensor_tensor(total, total, gates[:, b:b + 1, :].to_broadcast([128, TT, D]),
                                        ALU.mult).then_inc(sum_gated, 1)
                dve.wait_ge(sum_gated, b + 1)
                if b >= 2:
                    dve.wait_ge(output_stored[b % 2], 16 * (b // 2))
                nc.vector.tensor_tensor(yo[:, b % 2, :, :], total, xs[:, b * TT:(b + 1) * TT, :],
                                        ALU.add).then_inc(output_ready, 1)

        @block.tensor
        def _(pe):
            def split_product(dst, a_hi, a_lo, b_hi, b_lo, first, last):
                nc.tensor.matmul(dst, a_hi, b_hi, start=first, stop=False, skip_group_check=True)
                nc.tensor.matmul(dst, a_hi, b_lo, start=False, stop=False, skip_group_check=True)
                return nc.tensor.matmul(dst, a_lo, b_hi, start=False, stop=last, skip_group_check=True)

            pe.wait_ge(silu_step, 3)
            wm = wmod_st.rearrange("p (k n) -> p k n", k=KK)
            for j in range(3):
                for k in range(KK):
                    last = nc.tensor.matmul(ps[0:B, 5 + j, :], siluT[:, k, :], wm[:, k, j * 512:(j + 1) * 512],
                                            start=(k == 0), stop=(k == KK - 1))
            last.then_inc(mod_product, 1)
            pe.wait_ge(consts_set, 12)

            def transposes(hm, b):
                pe.wait_ge(*((ln1_done, b + 1) if hm is hm_a else (ln2_done, b + 1)))
                for k in range(KK):
                    for i in range(TT):
                        last = nc.tensor.transpose(ps[:, 6 + k, i * 128:(i + 1) * 128],
                                                   hm[:, i, k * 128:(k + 1) * 128], ident[:, :])
                    last.then_inc(rows_transposed, 1)

            def project(b, u):
                for r in range(4):
                    pe.wait_ge(cos_product, u * 4 + (b * NQK + r + 1))
                    w = bass.ds(u * 512 + r * 128, 128)
                    for k in range(KK):
                        last = split_product(ps[:, 4 + r, :], wqkv_hi[:, k, w], wqkv_lo[:, k, w],
                                             hT_hi[:, k, :], hT_lo[:, k, :], k == 0, k == KK - 1)
                    last.then_inc(qk_product, 1)

            def project_v(b):
                for m in range(TT):
                    pe.wait_ge(cos_product, b * NQK + (NQK - TT + m + 1 + QBANKS))
                    t = slice(m * 128, (m + 1) * 128)
                    for k in range(KK):
                        last = split_product(ps[:, 4 + m, :], hT_hi[:, k, t], hT_lo[:, k, t], wqkv_hi[:, k, VAT:],
                                             wqkv_lo[:, k, VAT:], k == 0, k == KK - 1)
                    last.then_inc(v_product, 1)

            def project_out(b, h, first=False):
                pe.wait_ge(head_lo_set, h + (b * NH + 1 + SLOTS))
                for i in range(TT):
                    t = slice(i * 128, (i + 1) * 128)
                    last = split_product(ps[:, i, 0:D], qk_hi[:, h + NKV, t], qk_lo[:, h + NKV, t], wo_hi[:, h, :],
                                         wo_lo[:, h, :], first, True)
                last.then_inc(head_projected, 1)

            def scores(b, h, g, marks=None):
                pe.wait_ge(qk_lo_set, h + (b * NQK + NKV + 1 + RSLOTS))
                for i in STRIPS:
                    bank, col = S_BANK[i]
                    w = 128 * (i + 1)
                    q = slice(i * 128, (i + 1) * 128)
                    if i != 2:
                        pe.wait_ge(exp_done, h * TT + (b * (NH * TT) + E_DONE[i]))
                    if marks is not None and i == 1:
                        count(marks)
                    split_product(ps[:, bank, col:col + w], qk_hi[:, h + NKV, q], qk_lo[:, h + NKV, q],
                                  qk_hi[:, g, 0:w], qk_lo[:, g, 0:w], True, False)
                    last = nc.tensor.matmul(ps[:, bank, col + i * 128:col + w], identb[:, :], maskb[:, :],
                                            start=False, stop=True, skip_group_check=True)
                    if i != 0:
                        last.then_inc(scores_ready, 1)

            def transpose_p(b, h, r):
                H = h + b * NH
                pe.wait_ge(probs_ready, H + 1)
                for j in (0, 1, 3, 2):
                    bank, col = PT_BANK[j]
                    if j != 3:
                        pe.wait_ge(probs_t_lo, H * PTB + (j + 1))
                    for i in range(j, TT):
                        at = P_AT[i] + 128 * j
                        last = nc.tensor.transpose(ps[:, bank, col + (i - j) * 128:col + (i - j + 1) * 128],
                                                   pr[:, r, at:at + 128], ident[:, :])
                    if j != 1:
                        last.then_inc(probs_transposed, 1)

            def head(b, h, r, g, last=False, marks=None, routed=None):
                H = h + b * NH
                if not last or h < NH - 1:
                    transpose_p(b, h + 1, (r + 1) % GRP)
                if not last or h < NH - 3:
                    scores(b, h + 3, g if r == 0 else g + 1, marks)
                if routed is not None:
                    pe.wait_ge(rows_t_lo, routed * (2 * KK) + 3 * KK)
                pe.wait_ge(head_lo_set, H + 1)
                for j in range(TT):
                    pe.wait_ge(probs_t_lo, H * PTB + (PTB + (1, 2, 3, 3)[j]))
                    at, w = PT_AT[j], 512 - 128 * j
                    vs = bass.ds(g * HD, HD)
                    a = slice(at, at + w)
                    end = split_product(ps[:, 6 + r % 2, 128 * j:512], v_hi[:, j, vs], v_lo[:, j, vs],
                                        pt_hi[:, r % 2, a], pt_lo[:, r % 2, a], j == 0, j == TT - 1)
                end.then_inc(pv_product, 1)

            def attention(b, before=None):
                for h in range(2):
                    scores(b, h, 0)
                scores(b, 2, 0)
                pe.wait_ge(v_lo_set, b * TT + TT)
                transpose_p(b, 0, 0)
                first = 0
                if before is not None:
                    first = 1
                    transposes(hm_b, before)
                    for r in range(GRP):
                        if r == 1:
                            logits(before, before * 2 + 2)
                            pe.wait_ge(route_step, before * ROUTE + 1)
                        head(b, r, r, 0, False, before if r == 3 else None, before if r == 0 else None)
                with pe.Fori(first, NKV - 1) as g:
                    for r in range(GRP):
                        head(b, g * GRP + r, r, g)
                for r in range(GRP):
                    head(b, NH - GRP + r, r, NKV - 1, True)

            def logits(b, n):
                pe.wait_ge(rows_t_lo, n * KK + KK)
                for i in range(TT):
                    t = slice(i * 128, (i + 1) * 128)
                    for k in range(KK):
                        last = split_product(ps[:, 7, i * 16:i * 16 + E], hT_hi[:, k, t], hT_lo[:, k, t],
                                             gate_hi[:, k, :], gate_lo[:, k, :], k == 0, k == KK - 1)
                last.then_inc(logits_ready, 1)

            def count(b):
                pe.wait_ge(route_step, b * ROUTE + ROUTE)
                for i in range(TT):
                    at = R_AT + i * 16
                    for j in range(i + 1):
                        nc.tensor.matmul(ps[:, 2, at:at + E], (upper if j == i else ones)[:, :], hot16[:, j, :],
                                         start=(j == 0), stop=(j == i), skip_group_check=True)
                at = R_AT + TT * 16
                for j in range(TT):
                    last = nc.tensor.matmul(ps[:, 2, at:at + E], ones[:, :], hot16[:, j, :],
                                            start=(j == 0), stop=(j == TT - 1), skip_group_check=True)
                last.then_inc(counts_ready, 1)

            def out_heads(b):
                pe.wait_ge(exp_done, b * (NH * TT) + (NH * TT + TT))
                for h in range(HEAD0):
                    project_out(b, h, h == 0)

            transposes(hm_a, 0)
            pe.wait_ge(rows_t_lo, KK)
            pe.wait_ge(weights_lo_set, 3 * KK)
            with pe.Fori(0, NQK // 4) as u:
                project(0, u)
            project_v(0)
            pe.wait_ge(weights_lo_set, NPIECE)
            attention(0)
            with pe.Fori(0, B - 1) as b:
                out_heads(b)
                pe.wait_ge(head_lo_set, b * NH + (NH + SLOTS))
                transposes(hm_a, b + 1)
                with pe.Fori(0, NQK // 4) as u:
                    for r in range(2):
                        project_out(b, u * 2 + (HEAD0 + r))
                    pe.wait_ge(rows_t_lo, b * (2 * KK) + 2 * KK)
                    project(b + 1, u)
                project_v(b + 1)
                pe.wait_ge(out_gated, b + 1)
                attention(b + 1, b)
            out_heads(B - 1)
            for h in range(HEAD0, NH):
                project_out(B - 1, h)
            transposes(hm_b, B - 1)
            logits(B - 1, 2 * B - 1)
            count(B - 1)

            pe.wait_ge(table_step, TABCOLS)
            for k in range(2):
                last = nc.tensor.transpose(ps[0:1, 3, k * 128:k * 128 + NRT], tcol[:, k:k + 1], ident[0:NRT, 0:NRT])
            last = nc.tensor.transpose(ps[:, 3, 256:256 + NRT], trow[:, :], ident[0:NRT, 0:NRT])
            last.then_inc(table_transposed, 1)

            pe.wait_ge(piece_lo_set, NP2)
            pe.wait_ge(table_step, TABSTEPS)

            experts = {}

            def load_experts(u):
                at, many = (u * UNR, min(UNR + 2, NT - u * UNR)) if isinstance(u, int) else (u * UNR, UNR + 2)
                _, values = nc.values_load_multi_w_load_instructions(
                    tab_e[0:1, bass.ds(at, many)], engines=(mybir.EngineType.PE,), min_val=0, max_val=NE - 1)
                experts.clear()
                experts.update(enumerate(values))

            def tile_step(u, r, routed=None):
                if r == 0 and (routed or isinstance(u, int) and u >= NSH // UNR - 1):
                    load_experts(u)
                for what, n, m, q, home in stages(u, r, routed):
                    if what == "t1":
                        pe.wait_ge(tile_loaded[m], q * 16 + 16)
                        for k in range(KK):
                            last = nc.tensor.transpose(ps[:, m % 2, k * 128:(k + 1) * 128],
                                                       xt[:, m, k * 128:(k + 1) * 128], ident[:, :])
                        last.then_inc(tile_transposed, 1)
                    if what == "up":
                        pe.wait_ge(tile_t_lo, n + 1)
                        w = bass.ds((experts[r + 2] if home else E) * (2 * INTER), 2 * INTER)
                        for k in range(KK):
                            last = split_product(ps[:, 2 + m % 2, 0:2 * INTER], xT_hi[:, m % 2, k, :], xT_lo[:, m % 2, k, :],
                                                 w13_hi[:, k, w], w13_lo[:, k, w], k == 0, k == KK - 1)
                        last.then_inc(up_product, 1)
                    if what == "t2":
                        pe.wait_ge(act_ready, n + 1)
                        for k in range(2):
                            last = nc.tensor.transpose(ps[0:HI, 4 + m % 2, k * 128:(k + 1) * 128],
                                                       hh[:, m % 2, k * HI:(k + 1) * HI], ident[:, :])
                        last.then_inc(act_transposed, 1)
                    if what == "dn":
                        pe.wait_ge(act_t_lo, n + 1)
                        pe.wait_ge(result_evacuated, n + 1)
                        w = bass.ds((experts[r] if home else E) * D, D)
                        for k in range(2):
                            last = split_product(ps[:, 6 + m % 2, 0:D], aT_hi[:, m % 2, k, :], aT_lo[:, m % 2, k, :],
                                                 w2_hi[:, k, w], w2_lo[:, k, w], k == 0, k == 1)
                        last.then_inc(down_product, 1)

            run_tiles(pe, tile_step)


NT_ROUTED = 80
MODSTEPS = 15
TABCOLS = 19
TABSTEPS = 24


def _perm(w, heads):
    a = w.reshape(heads, 64, 2, w.shape[1])
    return a.transpose(0, 2, 1, 3).reshape(w.shape)


def kernel(**inputs):
    import numpy as np
    import concourse.bacc as bacc
    from concourse.bass_utils import run_bass_kernel_spmd as run

    g = {k: np.asarray(v) for k, v in inputs.items()}
    B, S, D = g["L0_attn_x"].shape
    E, INTER, _ = g["L0_ffn_w1"].shape
    NE, HI = E + 1, INTER // 2
    wqkv = np.concatenate([_perm(g["L0_attn_Wk"], 4), _perm(g["L0_attn_Wq"], 16), g["L0_attn_Wv"]], axis=0)
    w1 = np.concatenate([g["L0_ffn_w1"], g["L0_ffn_sw1"][None]], axis=0)
    w3 = np.concatenate([g["L0_ffn_w3"], g["L0_ffn_sw3"][None]], axis=0)
    w2 = np.concatenate([g["L0_ffn_w2"], g["L0_ffn_sw2"][None]], axis=0)
    w13_t = np.stack([w1, w3], axis=1).reshape(NE * 2 * INTER, D).T.reshape(D // 128, 128, NE * 2 * INTER)
    w2_t = w2.transpose(2, 0, 1).reshape(2, HI, NE * D)
    HD, WSCALE = 128, np.float32(16.0)
    freqs = np.float32(1.0) / np.float32(10000.0) ** (np.arange(0, HD, 2, dtype=np.float32) / np.float32(HD))
    angles = (np.arange(S, dtype=np.float32)[None, :] * freqs[:, None]).astype(np.float64)
    cos, sin = (np.cos(angles) / WSCALE).astype(np.float32), (np.sin(angles) / WSCALE).astype(np.float32)
    rope = np.stack([np.concatenate([cos, cos]), np.concatenate([-sin, sin])])
    region, nsh = B * S + 128, B * S // 128
    ar = np.arange
    tabc = np.concatenate([
        ar(NE) * region, ar(32) * 128, (ar(E)[:, None] >= ar(E)[None, :]).reshape(-1), ar(NT_ROUTED),
        np.full(nsh, E), E * region + 128 * ar(nsh)]).astype(np.float32)
    arrays = {
        "x": g["L0_attn_x"], "c_t": g["L0_c"].T, "wmod": g["L0_wmod"], "wqkv_t": wqkv.T,
        "wo_t": g["L0_attn_Wo"].T, "gate_t": g["L0_ffn_gate_w"].T, "w13_t": w13_t, "w2_t": w2_t,
        "rope": rope, "tabc": tabc, "tokc": np.arange(B * S, dtype=np.float32).reshape(-1, 128).T,
    }
    arrays = {k: np.ascontiguousarray(v) for k, v in arrays.items()}
    nc = bacc.Bacc("TRN2", target_bir_lowering=False, num_devices=1)
    args = [nc.dram_tensor(k, v.shape, mybir.dt.from_np(v.dtype), kind="ExternalInput").ap() for k, v in arrays.items()]
    out = nc.dram_tensor("out", (B, S, D), mybir.dt.float32, kind="ExternalOutput").ap()
    adaln_moe_kernel(nc, *args, out)
    r = run(nc, [arrays], core_ids=[0])
    return r.results[0]["out"]
```
